# Optimizing a Trainium2 kernel written in Bass

```python
import numpy as np
import jax
import jax.numpy as jnp

def _softmax(x, axis=-1):
    return jax.nn.softmax(x, axis=axis)

def _gelu(x):
    return jax.nn.gelu(x, approximate=True)

def _silu(x):
    return jax.nn.silu(x)

def _sigmoid(x):
    return jax.nn.sigmoid(x)

def _layernorm(x, axis=-1, eps=1e-05):
    m = jnp.mean(x, axis=axis, keepdims=True)
    v = jnp.var(x, axis=axis, keepdims=True)
    return (x - m) / jnp.sqrt(v + eps)

def _scatter_add(tgt, idx, src, axis=0):
    return tgt.at[idx].add(src)

def _segment_sum(src, seg, n):
    return jax.ops.segment_sum(src, seg, n)
kernel_name = 'mk_gnn_resnorm_d4_gnn_r16_52db4a'

def setup_inputs(seed: int=0):
    np.random.seed(seed)
    _w = jnp.asarray

    def _rec_inputs():
        import jax
        import jax.numpy as jnp
        _gk = jax.random.key(seed)
        x = -0.000202 + 1 * jax.random.normal(jax.random.fold_in(_gk, 1), (6250, 64), jnp.float32)
        src = jax.random.randint(jax.random.fold_in(_gk, 2), (200000,), 0, 6250, jnp.int32)
        dst = jax.random.randint(jax.random.fold_in(_gk, 3), (200000,), 0, 6250, jnp.int32)
        _o = jnp.argsort(dst, stable=True)
        src = src[_o]
        dst = dst[_o]
        edge_attr_32 = 0.000189758 + 1.00013 * jax.random.normal(jax.random.fold_in(_gk, 12), (200000, 32), jnp.float32)
        edge_weight = jax.random.uniform(jax.random.fold_in(_gk, 14), (200000,), jnp.float32, 0.0, 0.999999)
        return (x, src, dst, edge_attr_32, edge_weight)
    x, src, dst, edge_attr_32, edge_weight = _rec_inputs()

    def _L0_gnn_setup():
        import jax, jax.numpy as jnp
        import numpy as np
        N, E, H, F = (6250, 62500, 4, 64)
        D_IN = 64

        def _gat_conv(x, src, dst, W, al, ar, b, act):
            z = (x @ W).reshape(N, H, F)
            el = jnp.sum(z * al, axis=-1)
            er = jnp.sum(z * ar, axis=-1)
            e = jax.nn.leaky_relu(el[src] + er[dst], 0.2)
            m = jax.ops.segment_max(e, dst, num_segments=N)
            ex = jnp.exp(e - m[dst])
            s = jax.ops.segment_sum(ex, dst, num_segments=N)
            alpha = ex / s[dst]
            msg = z[src] * alpha[..., None]
            out = jax.ops.segment_sum(msg, dst, num_segments=N) + b
            return act(out)
        key = jax.random.key(seed)
        ks = jax.random.split(key, 12)
        sc_in = 1.0 / np.sqrt(D_IN)
        sc_f = 1.0 / np.sqrt(F)
        return {'x': jax.random.normal(ks[0], (N, D_IN), jnp.float32), 'src': jax.random.randint(ks[1], (E,), 0, N, jnp.int32), 'dst': jax.random.randint(ks[2], (E,), 0, N, jnp.int32), 'W1': jax.random.normal(ks[3], (D_IN, H * F), jnp.float32) * sc_in, 'al1': jax.random.normal(ks[4], (H, F), jnp.float32) * sc_f, 'ar1': jax.random.normal(ks[5], (H, F), jnp.float32) * sc_f, 'b1': jnp.zeros((H, F), jnp.float32), 'W2': jax.random.normal(ks[6], (F, H * F), jnp.float32) * sc_f, 'al2': jax.random.normal(ks[7], (H, F), jnp.float32) * sc_f, 'ar2': jax.random.normal(ks[8], (H, F), jnp.float32) * sc_f, 'b2': jnp.zeros((H, F), jnp.float32)}
    _L0_gnn_all = _L0_gnn_setup()
    _L0_gnn_in = {k: v for k, v in _L0_gnn_all.items() if k in ('W1', 'al1', 'ar1', 'b1', 'W2', 'al2', 'ar2', 'b2')}
    del _L0_gnn_all

    def _L1_gnn_setup():
        import jax, jax.numpy as jnp
        import numpy as np
        N = 6250
        E = 100000
        D_IN = 64
        D_OUT = 64
        N_LAYERS = 3

        def gcn_conv(x, W, b, src, dst, ew):
            n = x.shape[0]
            loop = jnp.arange(n)
            src2 = jnp.concatenate([src, loop])
            dst2 = jnp.concatenate([dst, loop])
            ew2 = jnp.concatenate([ew, jnp.ones((n,), dtype=x.dtype)])
            deg = jax.ops.segment_sum(ew2, dst2, num_segments=n)
            dinv = jnp.where(deg > 0, jax.lax.rsqrt(deg), 0.0)
            norm = dinv[src2] * ew2 * dinv[dst2]
            h = x @ W
            msg = h[src2] * norm[:, None]
            out = jax.ops.segment_sum(msg, dst2, num_segments=n)
            return out + b
        key = jax.random.key(seed)
        ks = jax.random.split(key, 12)
        x = jax.random.normal(ks[0], (N, D_IN), dtype=jnp.float32)
        edge_index = jax.random.randint(ks[1], (2, E), 0, N, dtype=jnp.int64)
        edge_attr = jax.random.uniform(ks[2], (E,), dtype=jnp.float32)
        W0 = jax.random.normal(ks[3], (D_IN, D_OUT), dtype=jnp.float32) / np.sqrt(D_IN)
        b0 = jnp.zeros((D_OUT,), dtype=jnp.float32)
        W1 = jax.random.normal(ks[4], (D_OUT, D_OUT), dtype=jnp.float32) / np.sqrt(D_OUT)
        b1 = jnp.zeros((D_OUT,), dtype=jnp.float32)
        W2 = jax.random.normal(ks[5], (D_OUT, D_OUT), dtype=jnp.float32) / np.sqrt(D_OUT)
        b2 = jnp.zeros((D_OUT,), dtype=jnp.float32)
        d_cat = D_IN + N_LAYERS * D_OUT
        Wf = jax.random.normal(ks[6], (d_cat, D_OUT), dtype=jnp.float32) / np.sqrt(d_cat)
        bf = jnp.zeros((D_OUT,), dtype=jnp.float32)
        return {'x': x, 'edge_index': edge_index, 'edge_attr': edge_attr, 'W0': W0, 'b0': b0, 'W1': W1, 'b1': b1, 'W2': W2, 'b2': b2, 'Wf': Wf, 'bf': bf}
    _L1_gnn_all = _L1_gnn_setup()
    _L1_gnn_in = {k: v for k, v in _L1_gnn_all.items() if k in ('W0', 'b0', 'W1', 'b1', 'W2', 'b2', 'Wf', 'bf')}
    del _L1_gnn_all

    def _L2_gnn_setup():
        import jax, jax.numpy as jnp
        import numpy as np
        N_NODES = 3125
        N_EDGES = 50000
        D_FEAT = 64
        key = jax.random.key(seed)
        k1, k2 = jax.random.split(key)
        x = jax.random.normal(k1, (N_NODES, D_FEAT), dtype=jnp.float32)
        edge_index = jax.random.randint(k2, (2, N_EDGES), 0, N_NODES, dtype=jnp.int64)
        return {'x': x, 'edge_index': edge_index}
    _L2_gnn_all = _L2_gnn_setup()
    _L2_gnn_in = {k: v for k, v in _L2_gnn_all.items() if k in ()}
    del _L2_gnn_all

    def _L3_gnn_setup():
        import jax, jax.numpy as jnp
        import numpy as np
        EPS = 1e-05

        def _egnn_conv(x, src, dst, edge_attr_emb_src, W, b, bias, n_nodes):
            h = x @ W + b
            msg = h[src] + edge_attr_emb_src
            agg = jax.ops.segment_sum(msg, dst, num_segments=n_nodes) + h
            return jax.nn.relu(agg) + bias

        def _batchnorm(x, gamma, beta):
            mu = jnp.mean(x, axis=0)
            var = jnp.var(x, axis=0)
            return (x - mu) * jax.lax.rsqrt(var + EPS) * gamma + beta
        key = jax.random.key(seed)
        ks = jax.random.split(key, 20)
        N, E, F, ED, H = (6250, 100000, 64, 32, 64)
        inp = {'x': jax.random.normal(ks[0], (N, F), dtype=jnp.float32), 'edge_index': jax.random.randint(ks[1], (2, E), 0, N, dtype=jnp.int64), 'edge_attr': jax.random.normal(ks[2], (E, ED), dtype=jnp.float32), 'W1': jax.random.normal(ks[3], (F, H), dtype=jnp.float32) * (1.0 / np.sqrt(F)), 'b1': jax.random.normal(ks[4], (H,), dtype=jnp.float32) * 0.01, 'We1': jax.random.normal(ks[5], (ED, H), dtype=jnp.float32) * (1.0 / np.sqrt(ED)), 'be1': jax.random.normal(ks[6], (H,), dtype=jnp.float32) * 0.01, 'bias1': jnp.zeros((H,), dtype=jnp.float32), 'W2': jax.random.normal(ks[7], (H, H), dtype=jnp.float32) * (1.0 / np.sqrt(H)), 'b2': jax.random.normal(ks[8], (H,), dtype=jnp.float32) * 0.01, 'We2': jax.random.normal(ks[9], (ED, H), dtype=jnp.float32) * (1.0 / np.sqrt(ED)), 'be2': jax.random.normal(ks[10], (H,), dtype=jnp.float32) * 0.01, 'bias2': jnp.zeros((H,), dtype=jnp.float32), 'g1': jnp.ones((H,), dtype=jnp.float32), 'beta1': jnp.zeros((H,), dtype=jnp.float32), 'g2': jnp.ones((H,), dtype=jnp.float32), 'beta2': jnp.zeros((H,), dtype=jnp.float32)}
        return inp
    _L3_gnn_all = _L3_gnn_setup()
    _L3_gnn_in = {k: v for k, v in _L3_gnn_all.items() if k in ('W1', 'b1', 'We1', 'be1', 'bias1', 'W2', 'b2', 'We2', 'be2', 'bias2', 'g1', 'beta1', 'g2', 'beta2')}
    del _L3_gnn_all
    return {'x': x, 'src': src, 'dst': dst, 'edge_attr_32': edge_attr_32, 'edge_weight': edge_weight, 'L0_gnn_W1': _L0_gnn_in['W1'], 'L0_gnn_al1': _L0_gnn_in['al1'], 'L0_gnn_ar1': _L0_gnn_in['ar1'], 'L0_gnn_b1': _L0_gnn_in['b1'], 'L0_gnn_W2': _L0_gnn_in['W2'], 'L0_gnn_al2': _L0_gnn_in['al2'], 'L0_gnn_ar2': _L0_gnn_in['ar2'], 'L0_gnn_b2': _L0_gnn_in['b2'], 'L1_gnn_W0': _L1_gnn_in['W0'], 'L1_gnn_b0': _L1_gnn_in['b0'], 'L1_gnn_W1': _L1_gnn_in['W1'], 'L1_gnn_b1': _L1_gnn_in['b1'], 'L1_gnn_W2': _L1_gnn_in['W2'], 'L1_gnn_b2': _L1_gnn_in['b2'], 'L1_gnn_Wf': _L1_gnn_in['Wf'], 'L1_gnn_bf': _L1_gnn_in['bf'], 'L3_gnn_W1': _L3_gnn_in['W1'], 'L3_gnn_b1': _L3_gnn_in['b1'], 'L3_gnn_We1': _L3_gnn_in['We1'], 'L3_gnn_be1': _L3_gnn_in['be1'], 'L3_gnn_bias1': _L3_gnn_in['bias1'], 'L3_gnn_W2': _L3_gnn_in['W2'], 'L3_gnn_b2': _L3_gnn_in['b2'], 'L3_gnn_We2': _L3_gnn_in['We2'], 'L3_gnn_be2': _L3_gnn_in['be2'], 'L3_gnn_bias2': _L3_gnn_in['bias2'], 'L3_gnn_g1': _L3_gnn_in['g1'], 'L3_gnn_beta1': _L3_gnn_in['beta1'], 'L3_gnn_g2': _L3_gnn_in['g2'], 'L3_gnn_beta2': _L3_gnn_in['beta2']}

def reference(x, src, dst, edge_attr_32, edge_weight, L0_gnn_W1, L0_gnn_al1, L0_gnn_ar1, L0_gnn_b1, L0_gnn_W2, L0_gnn_al2, L0_gnn_ar2, L0_gnn_b2, L1_gnn_W0, L1_gnn_b0, L1_gnn_W1, L1_gnn_b1, L1_gnn_W2, L1_gnn_b2, L1_gnn_Wf, L1_gnn_bf, L3_gnn_W1, L3_gnn_b1, L3_gnn_We1, L3_gnn_be1, L3_gnn_bias1, L3_gnn_W2, L3_gnn_b2, L3_gnn_We2, L3_gnn_be2, L3_gnn_bias2, L3_gnn_g1, L3_gnn_beta1, L3_gnn_g2, L3_gnn_beta2):
    import jax
    import jax.numpy as jnp

    def _L0_gnn_ref(x, src, dst, W1, al1, ar1, b1, W2, al2, ar2, b2):
        import jax, jax.numpy as jnp
        import numpy as np
        N, E, H, F = (6250, 62500, 4, 64)
        D_IN = 64

        def _gat_conv(x, src, dst, W, al, ar, b, act):
            z = (x @ W).reshape(N, H, F)
            el = jnp.sum(z * al, axis=-1)
            er = jnp.sum(z * ar, axis=-1)
            e = jax.nn.leaky_relu(el[src] + er[dst], 0.2)
            m = jax.ops.segment_max(e, dst, num_segments=N)
            ex = jnp.exp(e - m[dst])
            s = jax.ops.segment_sum(ex, dst, num_segments=N)
            alpha = ex / s[dst]
            msg = z[src] * alpha[..., None]
            out = jax.ops.segment_sum(msg, dst, num_segments=N) + b
            return act(out)
        h = _gat_conv(x, src, dst, W1, al1, ar1, b1, jnp.tanh)
        h = h.mean(axis=-2)
        h = _gat_conv(h, src, dst, W2, al2, ar2, b2, lambda v: v)
        return h.mean(axis=-2)

    def _L1_gnn_ref(x, edge_index, edge_attr, W0, b0, W1, b1, W2, b2, Wf, bf):
        import jax, jax.numpy as jnp
        import numpy as np
        N = 6250
        E = 100000
        D_IN = 64
        D_OUT = 64
        N_LAYERS = 3

        def gcn_conv(x, W, b, src, dst, ew):
            n = x.shape[0]
            loop = jnp.arange(n)
            src2 = jnp.concatenate([src, loop])
            dst2 = jnp.concatenate([dst, loop])
            ew2 = jnp.concatenate([ew, jnp.ones((n,), dtype=x.dtype)])
            deg = jax.ops.segment_sum(ew2, dst2, num_segments=n)
            dinv = jnp.where(deg > 0, jax.lax.rsqrt(deg), 0.0)
            norm = dinv[src2] * ew2 * dinv[dst2]
            h = x @ W
            msg = h[src2] * norm[:, None]
            out = jax.ops.segment_sum(msg, dst2, num_segments=n)
            return out + b
        src, dst = (edge_index[0], edge_index[1])
        xs = [x]
        for W, b in ((W0, b0), (W1, b1), (W2, b2)):
            xs.append(jax.nn.relu(gcn_conv(xs[-1], W, b, src, dst, edge_attr)))
        h = jnp.concatenate(xs, axis=-1)
        return h @ Wf + bf

    def _L2_gnn_ref(x, edge_index):
        import jax, jax.numpy as jnp
        import numpy as np
        N_NODES = 3125
        N_EDGES = 50000
        D_FEAT = 64
        src, dst = (edge_index[0], edge_index[1])
        msg = x[src]
        out = jax.ops.segment_sum(msg, dst, num_segments=x.shape[0])
        return out

    def _L3_gnn_ref(x, edge_index, edge_attr, W1, b1, We1, be1, bias1, W2, b2, We2, be2, bias2, g1, beta1, g2, beta2):
        import jax, jax.numpy as jnp
        import numpy as np
        EPS = 1e-05

        def _egnn_conv(x, src, dst, edge_attr_emb_src, W, b, bias, n_nodes):
            h = x @ W + b
            msg = h[src] + edge_attr_emb_src
            agg = jax.ops.segment_sum(msg, dst, num_segments=n_nodes) + h
            return jax.nn.relu(agg) + bias

        def _batchnorm(x, gamma, beta):
            mu = jnp.mean(x, axis=0)
            var = jnp.var(x, axis=0)
            return (x - mu) * jax.lax.rsqrt(var + EPS) * gamma + beta
        N = x.shape[0]
        src, dst = (edge_index[0], edge_index[1])
        ea1 = edge_attr @ We1 + be1
        h = _egnn_conv(x, src, dst, ea1, W1, b1, bias1, N)
        h = _batchnorm(h, g1, beta1)
        ea2 = edge_attr @ We2 + be2
        h = _egnn_conv(h, src, dst, ea2, W2, b2, bias2, N)
        h = _batchnorm(h, g2, beta2)
        return h
    edge_index = jnp.stack([src, dst])
    x = _layernorm(x + _L0_gnn_ref(x, src, dst, L0_gnn_W1, L0_gnn_al1, L0_gnn_ar1, L0_gnn_b1, L0_gnn_W2, L0_gnn_al2, L0_gnn_ar2, L0_gnn_b2), axis=-1)
    x = _layernorm(x + _L1_gnn_ref(x, edge_index, edge_weight, L1_gnn_W0, L1_gnn_b0, L1_gnn_W1, L1_gnn_b1, L1_gnn_W2, L1_gnn_b2, L1_gnn_Wf, L1_gnn_bf), axis=-1)
    x = _layernorm(x + _L2_gnn_ref(x, edge_index), axis=-1)
    x = _layernorm(x + _L3_gnn_ref(x, edge_index, edge_attr_32, L3_gnn_W1, L3_gnn_b1, L3_gnn_We1, L3_gnn_be1, L3_gnn_bias1, L3_gnn_W2, L3_gnn_b2, L3_gnn_We2, L3_gnn_be2, L3_gnn_bias2, L3_gnn_g1, L3_gnn_beta1, L3_gnn_g2, L3_gnn_beta2), axis=-1)
    return x

_drawn_inputs = setup_inputs


def setup_inputs(seed=0):
    import zlib

    import numpy as np

    out = dict(_drawn_inputs(seed))
    spreads = {'L0_gnn_b1': (0.0, 0.1),
     'L0_gnn_b2': (0.0, 0.1),
     'L1_gnn_b0': (0.0, 0.1),
     'L1_gnn_b1': (0.0, 0.1),
     'L1_gnn_b2': (0.0, 0.1),
     'L1_gnn_bf': (0.0, 0.1),
     'L3_gnn_bias1': (0.0, 0.8),
     'L3_gnn_bias2': (0.0, 0.8),
     'L3_gnn_g1': (1.0, 0.2),
     'L3_gnn_beta1': (0.0, 0.1),
     'L3_gnn_g2': (1.0, 0.2),
     'L3_gnn_beta2': (0.0, 0.1)}
    factors = {'L0_gnn_ar1': 8.0,
     'L0_gnn_al2': 6.185,
     'L0_gnn_ar2': 8.0,
     'L3_gnn_b1': 3.343,
     'L3_gnn_b2': 2.966,
     'L3_gnn_be2': 2.742}
    for name, (base, spread) in spreads.items():
        noise = np.random.default_rng([zlib.crc32(name.encode()), seed]).standard_normal(out[name].shape)
        drawn = base * np.exp(spread * noise) if base else spread * noise
        out[name] = jnp.asarray(drawn.astype(out[name].dtype))
    for name, factor in factors.items():
        out[name] = (out[name] * factor).astype(out[name].dtype)
    return out
```

```python
import numpy as np
import concourse.bass as bass
from concourse import mybir
from contextlib import ExitStack

F32 = mybir.dt.float32
I32 = mybir.dt.int32
F16 = mybir.dt.float16
BF16 = mybir.dt.bfloat16
ALU = mybir.AluOpType
ACT = mybir.ActivationFunctionType
AX = mybir.AxisListType

N = 6250
E = 200000
F = 64
H = 4
ED = 32
P = 128

EC = 1568
EP = P * EC
GB = 16
NB = EC // GB

WN = 10
WG = 5
NG = 5
GN = WN * WG
BN = GN * NG
NT = BN // 2
T = N // NT
B = N // BN
NW = N // WN
NGR = N // GN
CH = 3
CAP = CH * P
KEY = 512
REC = 6
REC2 = 2 * H + 1
XC = F + 1 + H
EF = ED + 2
AGG = F + 1
QC = 1 + 2 * F
NQ = 5
QT = T // NQ
BIG = 1.0e30
RND = 12582912.0
LN_EPS = 1e-05
BN_EPS = 1e-05


def build(nc, a):
    ctx = ExitStack()
    with ctx:
        def dram(name, shape, dt=F32):
            return nc.dram_tensor(name, shape, dt, kind="Internal").ap()

        def sem(name):
            return ctx.enter_context(nc.semaphore(name))

        rec_d = dram("rec_d", [EP, REC])
        rec2_d = dram("rec2_d", [EP, REC2])
        rows_d = dram("rows_d", [EP, XC])
        table_d = dram("table_d", [N, XC])
        er_d = dram("er_d", [N, H])
        agg_d = dram("agg_d", [AGG, H, N])
        adj_w_d = dram("adj_w_d", [NGR, P, T, GN])
        adj_c_d = dram("adj_c_d", [NGR, P, T, GN])
        ptr_d = dram("ptr_d", [1, NW + 1])
        items_d = dram("items_d", [4, NW], I32)
        ptri_d = dram("ptri_d", [1, NW + 1], I32)

        SB = 53000
        arena = ctx.enter_context(nc.sbuf_tensor("arena", [P, SB], F32))
        top = [0]

        def at(off, parts, *dims):
            n = int(np.prod(dims))
            assert off + n <= SB, (off, n)
            v = arena[0:parts, off:off + n]
            if len(dims) == 1:
                return v
            names = "abcde"[:len(dims)]
            return v.rearrange(f"p ({' '.join(names)}) -> p {' '.join(names)}",
                               **{names[i]: dims[i] for i in range(1, len(dims))})

        def new(parts, *dims):
            off = top[0]
            top[0] += (int(np.prod(dims)) + 7) // 8 * 8
            return at(off, parts, *dims)

        x_sb = new(NT, T, F)
        dinv = new(NT, T)
        ident = new(P, P)
        flip = new(P, P)
        ones = new(P, P)
        iota_wn = new(P, WN)
        iota_key = new(P, T * WN // 2).bitcast(F16)
        iota_lo = new(P, P // 2).bitcast(F16)
        win_node = new(P, NW)
        win_key = new(P, NW)
        ptr_row = new(1, NW + 1).bitcast(I32)
        items = new(1, 4 * NW).bitcast(I32)
        n_items = new(1, 1).bitcast(I32)
        seg_t = new(EF, N)
        fixed = top[0]

        src_idx = new(P, EC).bitcast(I32)
        el_e = new(P, H, EC)
        gbuf = new(P, 2, GB, XC)
        gidx = new(P, 2, GB).bitcast(I32)
        xt = new(NT, T, XC)
        er_sb = new(NT, T, H)
        wgat = new(AGG, H, AGG)
        vw = new(F, 2, 2 * H)
        gbias = new(NT, H * F)
        rec_sl = new(P, NG, WG, CH * REC)
        ef_sl = new(P, NG, WG, CH * EF)
        oh_top = top[0]
        col_oh = new(P, 2, CH, T * WN // 2).bitcast(BF16)
        row_oh = new(P, 2, CH, 4, P // 2).bitcast(BF16)
        ckey = new(P, 2, WG * CH)
        cdl = new(P, 2, WG * CH)
        coh = new(P, 2, CH * WG, WN)
        over = top[0]
        stage = new(P, 3, 2, T, GN)
        assert top[0] <= SB, top[0]
        wv = at(oh_top, F, 2, H * F)
        alr = at(oh_top + 2 * H * F, F, 4, H * F)
        vprod = at(oh_top + 6 * H * F, F, 4, H * F)
        top[0] = over
        rec_all = new(P, EC, REC)
        tmp = [at(fixed + EC + i * EC, P, EC) for i in range(4)]
        hi_bf = new(P, EC // 2).bitcast(BF16)
        assert top[0] <= SB, top[0]
        heads = at(over, NT, EC)
        heads_f = at(over + EC, NT, EC)
        junk = at(over + 2 * EC, NT, EC)
        thr = at(over + 3 * EC, NT, 5)
        cnt = at(over + 3 * EC + 8, NT, 5)
        rowi = at(over + 3 * EC + 16, NT, 5).bitcast(I32)
        rowd = at(over + 3 * EC + 24, NT, 5, P).bitcast(I32)
        rowf = at(over + 3 * EC + 24 + 640, NT, 5, P)
        cnt2 = at(over + 3 * EC + 1400, NT, 5)
        ptr_f = at(over + 3 * EC + 1408, NT, 5)
        ptr_end = at(over + 3 * EC + 1416, 1, 1)
        o5 = over + 3 * EC + 1424
        ptrb = at(o5, NT, NW + 1)
        nover = at(o5 + 640, NT, NW)
        cum = at(o5 + 1280, NT, NW)
        offv = at(o5 + 1920, NT, NW)
        iota_nw = at(o5 + 2560, NT, NW)
        onesw = at(o5 + 3200, NT, NW)
        kid = at(o5 + 3840, NT, 5)
        itf = at(o5 + 3848, NT, 4, 5)
        iti = at(o5 + 3872, NT, 4, 5).bitcast(I32)
        ptr_i = at(o5 + 3896, NT, 5).bitcast(I32)
        itw = at(o5 + 3904, NT, 5)
        nif = at(o5 + 3912, 1, 2)
        o6 = o5 + 3920
        xT_sb = at(o6, F, N)
        top[0] = over
        mx_e = new(P, H, EC)
        sc_top = top[0]
        dst_i = new(P, EC).bitcast(I32)
        dst_f = new(P, EC)
        pen = new(P, EC + 1)
        scan_b = new(P, EC)
        edge_dst = new(P, 2).bitcast(I32)
        edge_f = new(P, 2)
        pens = new(P, 5)
        ends = new(P, 6, H)
        rows_t = new(H, 4, P)
        chain = new(H, 2, P)
        carry = new(H, 2, P)
        carry_e = new(P, 2, H)
        penf = new(P, 2, EC)
        assert top[0] <= SB, top[0]
        top[0] = sc_top
        RC = EC // 8
        rec2_c = new(P, 2, RC, REC2)
        assert top[0] <= sc_top + 3 * EC
        top[0] = over
        rec2_sl = new(P, NG, WG, CH * REC2)
        rows_sl = new(P, NG, WG, CH * XC)
        er_sl = new(P, NG, GN * H)
        gdl = new(P, 2, CH * WG)
        goh = new(P, 2, CH * WG, WN)
        gpr = new(P, CH * WG * H, WN)
        gq = new(P, CH * WG * H)
        gu = new(P, 2, CH * WG * H)
        gd = new(P, 2, CH * WG * H)
        gex = new(P, 2, CH * WG * H)
        grh = new(P, 2, CH * WG, H * WN)
        gst = new(AGG, NG, H, GN)
        ov_agg = new(AGG, H * WN)
        agg_sl = new(AGG, NG, H, BN)
        srec = new(NT, 2, H)
        yv = new(NT, 2, H * F)
        yt = new(NT, 2, H * F)
        hm = new(NT, 2, F)
        hT = new(F, BN)
        assert top[0] <= SB, top[0]
        ov_adj = at(over, P, 2, T * WN)
        top[0] = fixed
        per_node = new(NT, T, QC)
        xin = new(NT, T, F)
        facc = new(NT, T, F)
        hout = new(NT, T, F)
        sq = new(NT, T, F)
        adj_sl = new(P, NQ, NG, QT * GN)
        wconv = new(F, 5, F)
        wf = new(F, 4, F)
        we = new(EF, QC)
        bconv = new(NT, 12, F)
        bsum = new(EF, 2, 2 * F)
        xd = new(NT, 2, 2, F)
        aggs = new(F, BN)
        yc = new(NT, 2, 2, F)
        yT = new(F, 2, BN)
        stat = new(NT, 8, F)
        colm = new(NT, 4, T)
        segb = new(EF, BN)
        assert top[0] <= SB, top[0]

        bank = [ctx.enter_context(nc.psum_tensor(f"bank{i}", [P, 512], F32)) for i in range(8)]

        def bc(ap, axis, n):
            v = ap.unsqueeze(axis)
            shape = list(v.shape)
            shape[axis] = n
            return v.to_broadcast(shape)

        S = {}

        def s(name):
            if name not in S:
                S[name] = sem(name)
            return S[name]

        for names in (
            "consts_made pool_const edges_loaded heads_loaded weights_loaded x_loaded rec_made rec_stored "
            "ptr_rows_wanted ptr_rows_here ptr_made ptr_out ptr_back items_made items_out items_back xT_loaded "
            "v_made wgat_cleared wgat_loaded el_psum table_made table_stored er_stored idx_copied el_copied "
            "onehot_made adj_psum adj_evacuated seg_evacuated ov_loaded ov_onehot ov_psum ov_added "
            "ov_stored scan_loaded ends_made ends_t chain_in chain_made chain_t carry_back rec2_made "
            "logits_made exp_made rhs_made win_psum win_evac ga_loaded ga_logits ga_exp ga_rhs ga_psum ga_added "
            "ga_stored gw_loaded gat_psum gat_y gat_tanh gat_h gat_hT gat_hTc gat_v gat_xt "
            "gat_done gat_sum conv_w we_made pn_copied pn_psum pn_evac out_stored ln_var ln_std "
            "passed_sp passed_pool cv_input cv_self cv_agg cv_aggc cv_y cv_ev cv_yT cv_yTc cv_f cv_done bn_sum bn_mean bn_var bn_std "
        ).split():
            s(names)
        gathered = [sem(f"gathered{i}") for i in range(2)]
        rec2_stored = [sem(f"rec2_stored{i}") for i in range(2)]
        rows_stored = [sem(f"rows_stored{i}") for i in range(2)]
        adj_loaded = [sem(f"adj_loaded{i}") for i in range(NG)]
        adj_used = [sem(f"adj_used{i}") for i in range(NG)]
        adj_stored = [sem(f"adj_stored{i}") for i in range(3)]
        win_loaded = [sem(f"win_loaded{i}") for i in range(NG)]
        win_used = [sem(f"win_used{i}") for i in range(NG)]
        win_stored = [sem(f"win_stored{i}") for i in range(NG)]
        agg_loaded = [sem(f"agg_loaded{i}") for i in range(NG)]
        agg_used = [sem(f"agg_used{i}") for i in range(NG)]
        cv_loaded = [sem(f"cv_loaded{i}") for i in range(NQ)]
        cv_used = [sem(f"cv_used{i}") for i in range(NQ)]

        block = ctx.enter_context(nc.Block())

        def edge_rows(dram_ap, off):
            return dram_ap[bass.ds(off, CAP), :].rearrange("(p c) f -> p (c f)", c=CH)

        def nodes(dram_ap):
            return dram_ap.rearrange("(t p) f -> p t f", p=NT)

        def flat(ap):
            k = len(ap.shape) - 1
            if k == 1:
                return ap
            names = "abcde"[:k]
            return ap.rearrange(f"p {' '.join(names)} -> p ({' '.join(names)})")

        def wait_reg(eng, semaphore, value):
            eng.wait_ge(semaphore, value)
            eng.sem_inc(s(f"passed_{'sp' if eng is nc.sync else 'pool'}"), 1)

        def rounds(eng, count, peel=True):
            if peel:
                yield 0
            with eng.Fori(int(peel), count) as i:
                yield i

        def prep_sync(sp):
            sp.dma_start(src_idx, a["src"]).then_inc(s("edges_loaded"), 16)
            sp.dma_start(tmp[0].bitcast(I32), a["dst"].rearrange("a b -> (a b)").rearrange("(p c) -> p c", p=P)).then_inc(s("edges_loaded"), 16)
            sp.dma_start(tmp[1], a["edge_weight"]).then_inc(s("edges_loaded"), 16)
            sp.dma_start(x_sb, nodes(a["x"])).then_inc(s("x_loaded"), 16)
            sp.wait_ge(s("rec_made"), 1)
            sp.dma_start(rec_d.rearrange("(p c) f -> p (c f)", p=P), flat(rec_all)).then_inc(s("rec_stored"), 16)
            sp.wait_ge(s("rec_stored"), 16)
            sp.dma_start(heads.bitcast(I32), a["dst_heads"].partition_broadcast(NT) if False else a["dst_heads"].to_broadcast([NT, EC])).then_inc(s("heads_loaded"), 16)
            sp.dma_start(xT_sb, a["xT"]).then_inc(s("xT_loaded"), 16)
            sp.wait_ge(s("ptr_made"), 1)
            with nc.allow_non_contiguous_dma(reason="625 window starts"):
                sp.dma_start(ptr_d[0, 0:NW].rearrange("(c p) -> p c", p=NT), ptr_f).then_inc(s("ptr_out"), 16)
                sp.dma_start(ptri_d[0, 0:NW].rearrange("(c p) -> p c", p=NT), ptr_i).then_inc(s("ptr_out"), 16)
            sp.dma_start(ptr_d[:, NW:NW + 1], ptr_end).then_inc(s("ptr_out"), 16)
            sp.wait_ge(s("ptr_out"), 48)
            sp.dma_start(ptrb, ptr_d.to_broadcast([NT, NW + 1])).then_inc(s("ptr_back"), 16)
            sp.dma_start(ptr_row[:, 0:NW], ptri_d[:, 0:NW]).then_inc(s("ptr_back"), 16)
            sp.wait_ge(s("items_made"), 1)
            with nc.allow_non_contiguous_dma(reason="the overflow items"):
                for i in range(4):
                    sp.dma_start(items_d[i, :].rearrange("(c p) -> p c", p=NT), iti[:, i, :]).then_inc(s("items_out"), 16)
            sp.wait_ge(s("items_out"), 64)
            sp.dma_start(items, items_d.rearrange("i k -> (i k)").unsqueeze(0)).then_inc(s("items_back"), 16)
            sp.wait_ge(s("items_back"), 16)

        def logit_weights_sync(sp):
            for l in range(2):
                sp.dma_start(wv[:, l, :], a[f"L0_gnn_W{l + 1}"]).then_inc(s("weights_loaded"), 16)
                for i, n in enumerate(("al", "ar")):
                    sp.dma_start(alr[:, 2 * l + i, :], a[f"L0_gnn_{n}{l + 1}"].rearrange("h f -> (h f)").unsqueeze(0).to_broadcast([F, H * F])).then_inc(s("weights_loaded"), 16)

        def gat_weights_sync(sp, layer):
            if layer:
                sp.wait_ge(s("gat_done"), 1)
            else:
                sp.wait_ge(s("wgat_cleared"), 1)
            sp.dma_start(wgat[0:F, :, 0:F], a[f"L0_gnn_W{layer + 1}"].rearrange("k (h f) -> k h f", h=H)).then_inc(s("wgat_loaded"), 16)
            sp.dma_start(gbias, a[f"L0_gnn_b{layer + 1}"].rearrange("h f -> (h f)").unsqueeze(0).to_broadcast([NT, H * F])).then_inc(s("wgat_loaded"), 16)

        def table_sync(sp, layer):
            sp.wait_ge(s("table_made"), layer + 1)
            sp.dma_start(nodes(table_d), xt).then_inc(s("table_stored"), 16)
            sp.dma_start(nodes(er_d), er_sb).then_inc(s("er_stored"), 16)

        def adj_sync(sp):
            for b in rounds(sp, B):
                for g in range(NG):
                    wait_reg(sp, adj_used[g], b * 2)
                    for w in range(WG):
                        off = sp.value_load(ptr_row[0:1, bass.ds(b * (NG * WG) + g * WG + w, 1)], min_val=0, max_val=EP - CAP)
                        sp.dma_start(rec_sl[:, g, w, :], edge_rows(rec_d, off)).then_inc(adj_loaded[g], 16)
                        sp.dma_start(ef_sl[:, g, w, :], edge_rows(a["edge_features"], off)).then_inc(adj_loaded[g], 16)

        def adj_window(d, group, node):
            return d[bass.ds(group, 1), :, :, bass.ds(node, WN)].rearrange("a p t n -> p (a t) n")

        def item(eng, row, k, top_):
            return eng.value_load(items[0:1, bass.ds(k + row * NW, 1)], min_val=0, max_val=top_)

        def adj_overflow_sync(sp):
            for i, n in enumerate((2, 2, 1)):
                sp.wait_ge(adj_stored[i], 32 * B * n)
            count = sp.value_load(n_items, min_val=0, max_val=NW)
            with sp.If(count > 0):
                with sp.Fori(0, count) as k:
                    off = item(sp, 0, k, EP - CAP)
                    group = item(sp, 2, k, NGR - 1)
                    node = item(sp, 3, k, GN - WN)
                    sp.dma_start(rec_sl[:, 0, 0, :], edge_rows(rec_d, off)).then_inc(s("ov_loaded"), 16)
                    sp.dma_start(ef_sl[:, 0, 0, :], edge_rows(a["edge_features"], off)).then_inc(s("ov_loaded"), 16)
                    for i, d in enumerate((adj_w_d, adj_c_d)):
                        sp.dma_start(ov_adj[:, i, :].rearrange("p (t n) -> p t n", n=WN), adj_window(d, group, node)).then_inc(s("ov_loaded"), 16)
                    sp.wait_ge(s("ov_added"), k + 1)
                    for i, d in enumerate((adj_w_d, adj_c_d)):
                        sp.dma_start(adj_window(d, group, node), ov_adj[:, i, :].rearrange("p (t n) -> p t n", n=WN)).then_inc(s("ov_stored"), 16)
                    wait_reg(sp, s("ov_stored"), k * 32 + 32)

        def scan_sync(sp, layer):
            sp.wait_ge(s("win_evac"), layer * NGR)
            if layer == 0:
                for i, n in enumerate((2, 2, 1)):
                    sp.wait_ge(adj_stored[i], 32 * B * n)
                sp.wait_ge(s("seg_evacuated"), NGR)
            else:
                sp.wait_ge(s("gat_done"), 1)
            sp.dma_start(dst_i, a["dst"].rearrange("a b -> (a b)").rearrange("(p c) -> p c", p=P)).then_inc(s("scan_loaded"), 16)
            dflat = a["dst"].rearrange("a b -> (a b)")
            with nc.allow_non_contiguous_dma(reason="one neighbour per partition"):
                sp.dma_start(edge_dst[1:P, 0:1], dflat[EC - 1:EP - 1].rearrange("(p c) -> p c", c=EC)[:, 0:1]).then_inc(s("scan_loaded"), 16) if False else \
                    sp.dma_start(edge_dst[1:P, 0:1], dflat[EC - 1:EC - 1 + (P - 1) * EC].rearrange("(p c) -> p c", c=EC)[:, 0:1]).then_inc(s("scan_loaded"), 16)
                sp.dma_start(edge_dst[0:P - 1, 1:2], dflat[EC:EP].rearrange("(p c) -> p c", c=EC)[:, 0:1]).then_inc(s("scan_loaded"), 16)
                sp.dma_start(edge_dst[0:1, 0:1], dflat[EP - 1:EP].unsqueeze(0)).then_inc(s("scan_loaded"), 16)
                sp.dma_start(edge_dst[P - 1:P, 1:2], dflat[0:1].unsqueeze(0)).then_inc(s("scan_loaded"), 16)
            for c in range(8):
                sp.wait_ge(s("rec2_made"), layer * 8 + c + 1)
                sp.dma_start(rec2_d.rearrange("(p c) f -> p (c f)", p=P)[:, c * RC * REC2:(c + 1) * RC * REC2],
                             flat(rec2_c[:, c % 2])).then_inc(rec2_stored[c % 2], 16)

        def win_sync(sp, layer):
            for i in range(2):
                sp.wait_ge(rec2_stored[i], 16 * 4 * (layer + 1))
            sp.wait_ge(s("er_stored"), 16 * (layer + 1))
            for i in range(2):
                sp.wait_ge(rows_stored[i], 16 * (NB // 2) * (layer + 1))
            for b in rounds(sp, B, layer == 0):
                for g in range(NG):
                    wait_reg(sp, win_used[g], b * 2 + layer * 2 * B)
                    for w in range(WG):
                        off = sp.value_load(ptr_row[0:1, bass.ds(b * (NG * WG) + g * WG + w, 1)], min_val=0, max_val=EP - CAP)
                        sp.dma_start(rec2_sl[:, g, w, :], edge_rows(rec2_d, off)).then_inc(win_loaded[g], 16)
                        sp.dma_start(rows_sl[:, g, w, :], edge_rows(rows_d, off)).then_inc(win_loaded[g], 16)
                    sp.dma_start(er_sl[:, g, :], er_d[bass.ds(b * BN + g * GN, GN), :].rearrange("n h -> (n h)").unsqueeze(0).to_broadcast([P, GN * H])).then_inc(win_loaded[g], 16)
            for g in range(NG):
                sp.wait_ge(win_stored[g], 16 * B * (layer + 1))

        def agg_window(node):
            return agg_d[:, :, bass.ds(node, WN)]

        def win_overflow_sync(sp, layer):
            count = sp.value_load(n_items, min_val=0, max_val=NW)
            with sp.If(count > 0):
                with sp.Fori(0, count) as k:
                    off = item(sp, 0, k, EP - CAP)
                    win = item(sp, 1, k, NW - 1)
                    node = win * WN
                    sp.dma_start(rec2_sl[:, 0, 0, :], edge_rows(rec2_d, off)).then_inc(s("ga_loaded"), 16)
                    sp.dma_start(rows_sl[:, 0, 0, :], edge_rows(rows_d, off)).then_inc(s("ga_loaded"), 16)
                    sp.dma_start(er_sl[:, 0, 0:WN * H], er_d[bass.ds(node, WN), :].rearrange("n h -> (n h)").unsqueeze(0).to_broadcast([P, WN * H])).then_inc(s("ga_loaded"), 16)
                    sp.dma_start(ov_agg.rearrange("p (h n) -> p h n", h=H), agg_window(node)).then_inc(s("ga_loaded"), 16)
                    sp.wait_ge(s("ga_added"), ga_base(sp, layer) + k + 1)
                    sp.dma_start(agg_window(node), ov_agg.rearrange("p (h n) -> p h n", h=H)).then_inc(s("ga_stored"), 16)
                    wait_reg(sp, s("ga_stored"), (ga_base(sp, layer) + k) * 16 + 16)

        def ga_base(eng, layer):
            return eng.value_load(n_items, min_val=0, max_val=NW) if layer else 0

        def gat_sync(sp, layer):
            for i in rounds(sp, B // NG, layer == 0):
                for u in range(NG):
                    sp.wait_ge(agg_used[u], i + layer * (B // NG))
                    sp.dma_start(agg_sl[:, u], agg_d[:, :, bass.ds(i * (NG * BN) + u * BN, BN)]).then_inc(agg_loaded[u], 16)

        def conv_weights_sync(sp):
            sp.wait_ge(s("gat_done"), 2)
            q = s("conv_w")
            for i in range(3):
                sp.dma_start(wconv[:, i, :], a[f"L1_gnn_W{i}"]).then_inc(q, 16)
            for i in range(2):
                sp.dma_start(wconv[:, 3 + i, :], a[f"L3_gnn_W{i + 1}"]).then_inc(q, 16)
            sp.dma_start(wf, a["L1_gnn_Wf"].rearrange("(i k) f -> k i f", k=F)).then_inc(q, 16)
            for i, n in enumerate(("L1_gnn_b0", "L1_gnn_b1", "L1_gnn_b2", "L1_gnn_bf", "L3_gnn_b1", "L3_gnn_b2", "L3_gnn_bias1", "L3_gnn_bias2",
                                   "L3_gnn_g1", "L3_gnn_beta1", "L3_gnn_g2", "L3_gnn_beta2")):
                sp.dma_start(bconv[:, i, :], a[n].unsqueeze(0).to_broadcast([NT, F])).then_inc(q, 16)
            for i in range(2):
                sp.dma_start(we[0:ED, 1 + i * F:1 + (i + 1) * F], a[f"L3_gnn_We{i + 1}"]).then_inc(q, 16)
                sp.dma_start(bsum[ED:ED + 1, 0, i * F:(i + 1) * F], a[f"L3_gnn_b{i + 1}"].unsqueeze(0)).then_inc(q, 16)
                sp.dma_start(bsum[ED:ED + 1, 1, i * F:(i + 1) * F], a[f"L3_gnn_be{i + 1}"].unsqueeze(0)).then_inc(q, 16)

        CONV_W = 16 * (5 + 1 + 12 + 6)

        def conv_sync(sp, n, adj):
            for b in rounds(sp, B, n == 0):
                for q in range(NQ):
                    sp.wait_ge(cv_used[q], b + n * B)
                    sp.dma_start(adj_sl[:, q], adj[bass.ds(b * NG, NG), :, q * QT:(q + 1) * QT, :].rearrange("g p t n -> p g (t n)")).then_inc(cv_loaded[q], 16)

        @block.sync
        def _(sp):
            logit_weights_sync(sp)
            prep_sync(sp)
            gat_weights_sync(sp, 0)
            table_sync(sp, 0)
            adj_sync(sp)
            adj_overflow_sync(sp)
            scan_sync(sp, 0)
            win_sync(sp, 0)
            win_overflow_sync(sp, 0)
            gat_sync(sp, 0)
            gat_weights_sync(sp, 1)
            table_sync(sp, 1)
            scan_sync(sp, 1)
            win_sync(sp, 1)
            win_overflow_sync(sp, 1)
            gat_sync(sp, 1)
            conv_weights_sync(sp)
            for n, adj in enumerate((adj_w_d, adj_w_d, adj_w_d, adj_c_d, adj_c_d, adj_c_d)):
                if n == 0:
                    sp.wait_ge(s("pn_evac"), 1)
                conv_sync(sp, n, adj)
            sp.wait_ge(s("cv_done"), 7)
            sp.dma_start(nodes(a["out"]), x_sb).then_inc(s("out_stored"), 16)
            sp.wait_ge(s("out_stored"), 16)

        def consts_pool(pool):
            g = nc.gpsimd
            g.iota(iota_wn, [[1, WN]], base=0, channel_multiplier=0, allow_small_or_imprecise_dtypes=True)
            g.iota(iota_key, [[1, T * WN]], base=0, channel_multiplier=0, allow_small_or_imprecise_dtypes=True)
            g.iota(iota_lo, [[1, P]], base=0, channel_multiplier=0, allow_small_or_imprecise_dtypes=True)
            g.iota(win_node, [[WN, NW]], base=0, channel_multiplier=0, allow_small_or_imprecise_dtypes=True)
            g.iota(win_key, [[KEY, NW]], base=0, channel_multiplier=0, allow_small_or_imprecise_dtypes=True)
            g.memset(ones, 1.0)
            g.memset(ident, 0.0).then_inc(s("pool_const"), 1)
            g.memset(flip, 0.0).then_inc(s("pool_const"), 1)
            pool.wait_ge(s("pool_const"), 2)
            g.affine_select(out=ident, in_=ident, compare_op=ALU.not_equal, fill=1.0, base=0, pattern=[[-1, P]], channel_multiplier=1).then_inc(s("consts_made"), 1)
            g.affine_select(out=flip, in_=flip, compare_op=ALU.not_equal, fill=1.0, base=1 - P, pattern=[[1, P]], channel_multiplier=1).then_inc(s("consts_made"), 1)
            pool.wait_ge(s("rec_stored"), 16)
            g.iota(thr, [[WN * NT, 5]], base=0, channel_multiplier=WN, allow_small_or_imprecise_dtypes=True)
            g.iota(kid, [[NT, 5]], base=0, channel_multiplier=1, allow_small_or_imprecise_dtypes=True)
            g.iota(iota_nw, [[1, NW]], base=0, channel_multiplier=0, allow_small_or_imprecise_dtypes=True)
            g.memset(onesw, 1.0).then_inc(s("consts_made"), 1)
            pool.wait_ge(s("ptr_rows_wanted"), 1)
            for c in range(5):
                g.indirect_dma_start(rowd[:, c, :], None, a["dst"], bass.IndirectOffsetOnAxis(ap=rowi[:, c:c + 1], axis=0)).then_inc(s("ptr_rows_here"), 16)

        def gather_pool(pool, layer):
            g = nc.gpsimd
            base = layer * (NB // 2)

            def issue(slot, turn, batch):
                pool.wait_ge(rows_stored[slot], turn * 16)
                g.tensor_copy(gidx[:, slot, :], src_idx[:, bass.ds(batch * GB, GB)] if not isinstance(batch, int) else src_idx[:, batch * GB:(batch + 1) * GB]).then_inc(s("idx_copied"), 1)
                wait_reg(pool, s("idx_copied"), turn * 2 + slot + 1)
                for j in range(GB):
                    g.indirect_dma_start(gbuf[:, slot, j, :], None, table_d, bass.IndirectOffsetOnAxis(ap=gidx[:, slot, j:j + 1], axis=0)).then_inc(gathered[slot], 16)

            def finish(slot, turn, batch):
                pool.wait_ge(gathered[slot], turn * (16 * GB) + 16 * GB)
                cols = bass.ds(batch * GB, GB) if not isinstance(batch, int) else slice(batch * GB, (batch + 1) * GB)
                g.tensor_copy(el_e[:, :, cols], gbuf[:, slot, :, F + 1:XC].rearrange("p c h -> p h c")).then_inc(s("el_copied"), 1)
                dcols = bass.ds(batch * (GB * XC), GB * XC) if not isinstance(batch, int) else slice(batch * GB * XC, (batch + 1) * GB * XC)
                pool.wait_ge(s("el_copied"), turn * 2 + slot + 1)
                g.dma_start(rows_d.rearrange("(p c) f -> p (c f)", p=P)[:, dcols], flat(gbuf[:, slot])).then_inc(rows_stored[slot], 16)

            pool.wait_ge(s("table_stored"), 16 * (layer + 1))
            issue(0, base, 0)
            for i in rounds(pool, NB // 2 - 1, layer == 0):
                issue(1, i + base, i * 2 + 1)
                finish(0, i + base, i * 2)
                issue(0, i + (base + 1), i * 2 + 2)
                finish(1, i + base, i * 2 + 1)
            last = NB // 2 - 1
            issue(1, base + last, NB - 1)
            finish(0, base + last, NB - 2)
            finish(1, base + last, NB - 1)

        @block.gpsimd
        def _(pool):
            consts_pool(pool)
            pool.wait_ge(s("rec_made"), 1)
            gather_pool(pool, 0)
            pool.wait_ge(s("rec2_made"), 8)
            gather_pool(pool, 1)

        v = nc.vector

        def prep_vector(d):
            d.wait_ge(s("edges_loaded"), 48)
            hi, dst, ew = tmp[3], tmp[2], tmp[1]
            srcf, t0 = rec_all[:, :, 0], rec_all[:, :, 1]
            v.tensor_copy(srcf, src_idx)
            v.tensor_copy(dst, tmp[0].bitcast(I32))
            v.tensor_copy(hi_bf, ew)
            d.drain()
            v.tensor_scalar(hi, srcf, 1.0 / NT, 0.5 / NT - 0.5, ALU.mult, ALU.add)
            v.tensor_scalar(tmp[0], dst, 1.0 / WN, 0.5 / WN - 0.5, ALU.mult, ALU.add)
            v.tensor_copy(rec_all[:, :, 5], dst)
            v.tensor_copy(rec_all[:, :, 2], hi_bf)
            d.drain()
            v.tensor_scalar(hi, hi, RND, None, ALU.add)
            v.tensor_scalar(tmp[0], tmp[0], RND, None, ALU.add)
            v.tensor_tensor(ew, ew, rec_all[:, :, 2], ALU.subtract)
            d.drain()
            v.tensor_scalar(hi, hi, -RND, None, ALU.add)
            v.tensor_scalar(tmp[0], tmp[0], -RND, None, ALU.add)
            v.tensor_copy(hi_bf, ew)
            d.drain()
            v.scalar_tensor_tensor(t0, hi, -float(NT), srcf, ALU.mult, ALU.add)
            v.tensor_copy(rec_all[:, :, 3], hi_bf)
            d.drain()
            v.scalar_tensor_tensor(srcf, tmp[0], float(KEY - WN), dst, ALU.mult, ALU.add)
            v.tensor_tensor(rec_all[:, :, 4], ew, rec_all[:, :, 3], ALU.subtract)
            d.drain()
            v.scalar_tensor_tensor(srcf, hi, float(WN), srcf, ALU.mult, ALU.add)
            d.drain().then_inc(s("rec_made"), 1)

        def ptr_vector(d):
            d.wait_ge(s("heads_loaded"), 16)
            d.wait_ge(s("consts_made"), 3)
            v.tensor_copy(heads_f, heads.bitcast(I32))
            d.drain()
            for c in range(5):
                v.tensor_scalar(junk, heads_f, thr[:, c:c + 1], None, ALU.is_lt, ALU.add, accum_out=cnt[:, c:c + 1])
                d.drain()
            v.tensor_scalar(cnt, cnt, -1.0, 0.0, ALU.add, ALU.max)
            d.drain()
            v.tensor_copy(rowi, cnt).then_inc(s("ptr_rows_wanted"), 1)
            d.wait_ge(s("ptr_rows_here"), 80)
            v.tensor_copy(rowf, rowd)
            d.drain()
            for c in range(5):
                v.tensor_scalar(junk[:, 0:P], rowf[:, c, :], thr[:, c:c + 1], None, ALU.is_lt, ALU.add, accum_out=cnt2[:, c:c + 1])
                d.drain()
            v.scalar_tensor_tensor(ptr_f, cnt, float(P), cnt2, ALU.mult, ALU.add)
            v.memset(ptr_end, float(E))
            d.drain()
            v.tensor_copy(ptr_i, ptr_f)
            d.drain().then_inc(s("ptr_made"), 1)
            d.wait_ge(s("ptr_back"), 32)
            v.tensor_tensor(nover, ptrb[:, 1:NW + 1], ptrb[:, 0:NW], ALU.subtract)
            d.drain()
            v.tensor_scalar(nover, nover, 1.0 / CAP, -0.5 / CAP - 0.5, ALU.mult, ALU.add)
            d.drain()
            v.tensor_scalar(nover, nover, RND, None, ALU.add)
            d.drain()
            v.tensor_scalar(nover, nover, -RND, 0.0, ALU.add, ALU.max)
            d.drain()
            v.tensor_tensor_scan(cum, onesw, nover, 0.0, ALU.mult, ALU.add)
            d.drain()
            v.tensor_copy(n_items, cum[0:1, NW - 1:NW])
            v.tensor_tensor(nover, cum, nover, ALU.subtract)
            for c in range(5):
                v.tensor_scalar(junk[:, 0:NW], cum, kid[:, c:c + 1], None, ALU.is_le, ALU.add, accum_out=itw[:, c:c + 1])
                d.drain()
            v.tensor_scalar(offv, nover, -float(CAP), float(CAP), ALU.mult, ALU.add)
            d.drain()
            v.tensor_tensor(offv, offv, ptrb[:, 0:NW], ALU.add)
            d.drain()
            for c in range(5):
                v.scalar_tensor_tensor(junk[:, 0:NW], iota_nw, itw[:, c:c + 1], offv, ALU.is_equal, ALU.mult, accum_out=itf[:, 0, c:c + 1])
                d.drain()
            v.scalar_tensor_tensor(itf[:, 0, :], kid, float(CAP), itf[:, 0, :], ALU.mult, ALU.add)
            v.tensor_copy(itf[:, 1, :], itw)
            v.tensor_scalar(itf[:, 2, :], itw, 1.0 / WG, 0.5 / WG - 0.5, ALU.mult, ALU.add)
            d.drain()
            v.tensor_scalar(itf[:, 2, :], itf[:, 2, :], RND, None, ALU.add)
            d.drain()
            v.tensor_scalar(itf[:, 2, :], itf[:, 2, :], -RND, None, ALU.add)
            d.drain()
            v.scalar_tensor_tensor(itf[:, 3, :], itf[:, 2, :], -float(WG), itw, ALU.mult, ALU.add)
            d.drain()
            v.tensor_scalar(itf[:, 3, :], itf[:, 3, :], float(WN), None, ALU.mult)
            d.drain()
            v.tensor_copy(iti, itf)
            d.drain().then_inc(s("items_made"), 1)

        def logit_weights_vector(d):
            v.memset(wgat, 0.0)
            d.drain()
            v.memset(wgat[F:AGG, :, F:AGG], 1.0)
            d.drain().then_inc(s("wgat_cleared"), 1)
            d.wait_ge(s("weights_loaded"), 16 * 6)
            for l in range(2):
                for i in range(2):
                    v.tensor_tensor(vprod[:, 2 * l + i, :], wv[:, l, :], alr[:, 2 * l + i, :], ALU.mult)
            d.drain()
            for l in range(2):
                for i in range(2):
                    v.tensor_reduce(vw[:, l, i * H:(i + 1) * H], vprod[:, 2 * l + i, :].rearrange("p (h f) -> p h f", h=H), AX.X, ALU.add)
            d.drain().then_inc(s("v_made"), 1)

        def table0_vector(d):
            d.wait_ge(s("x_loaded"), 16)
            v.tensor_copy(xt[:, :, 0:F], x_sb)
            v.memset(xt[:, :, F:F + 1], 1.0)
            d.wait_ge(s("el_psum"), 1)
            e = bank[7][0:NT, 0:T * 2 * H].rearrange("p (t k) -> p t k", k=2 * H)
            v.tensor_copy(xt[:, :, F + 1:XC], e[:, :, 0:H])
            v.tensor_copy(er_sb, e[:, :, H:2 * H])
            d.drain().then_inc(s("table_made"), 1)

        def one_hots(d, slot, rec, key, c):
            v.tensor_scalar(col_oh[:, slot, c, :], iota_key, key, None, ALU.is_equal)
            v.tensor_scalar(row_oh[:, slot, c, 3, :], iota_lo, rec[:, c * REC + 1:c * REC + 2], None, ALU.is_equal)
            for i in range(3):
                v.tensor_scalar(row_oh[:, slot, c, i, :], iota_lo, rec[:, c * REC + 1:c * REC + 2], rec[:, c * REC + 2 + i:c * REC + 3 + i], ALU.is_equal, ALU.mult)

        def keys(d, par, recs, wk, wn, nw):
            r = recs.rearrange("p w (c r) -> p w c r", r=REC)
            n = nw * CH
            v.tensor_tensor(ckey[:, par, 0:n].rearrange("p (w c) -> p w c", c=CH), r[:, :, :, 0], bc(wk, 2, CH), ALU.subtract)
            v.tensor_tensor(cdl[:, par, 0:n].rearrange("p (w c) -> p w c", c=CH), r[:, :, :, 5], bc(wn, 2, CH), ALU.subtract)
            d.drain()
            v.tensor_tensor(coh[:, par, 0:n, :], bc(cdl[:, par, 0:n], 2, WN), bc(iota_wn, 1, n), ALU.is_equal)

        def adj_vector(d):
            d.wait_ge(s("items_back"), 16)
            for b in rounds(d, B):
                for g in range(NG):
                    par = g % 2
                    d.wait_ge(adj_loaded[g], b * (32 * WG) + 32 * WG)
                    d.wait_ge(s("adj_psum"), b * (NG * WG) + max(0, (g - 1) * WG))
                    w0 = b * (NG * WG) + g * WG
                    keys(d, par, rec_sl[:, g], win_key[:, bass.ds(w0, WG)], win_node[:, bass.ds(w0, WG)], WG)
                    for w in range(WG):
                        n = g * WG + w
                        d.wait_ge(s("adj_psum"), b * (NG * WG) + max(0, n - 1))
                        for c in range(CH):
                            one_hots(d, n % 2, rec_sl[:, g, w, :], ckey[:, par, w * CH + c:w * CH + c + 1], c)
                        d.drain().then_inc(s("onehot_made"), 1)
                    d.sem_inc(adj_used[g], 1)

        def adj_overflow_vector(d):
            d.wait_ge(s("seg_evacuated"), NGR)
            count = d.value_load(n_items, min_val=0, max_val=NW)
            with d.If(count > 0):
                with d.Fori(0, count) as k:
                    win = item(d, 1, k, NW - 1)
                    d.wait_ge(s("ov_loaded"), k * 64 + 64)
                    keys(d, 0, rec_sl[:, 0, 0:1], win_key[:, bass.ds(win, 1)], win_node[:, bass.ds(win, 1)], 1)
                    for c in range(CH):
                        one_hots(d, 0, rec_sl[:, 0, 0, :], ckey[:, 0, c:c + 1], c)
                    d.drain().then_inc(s("ov_onehot"), 1)
                    d.wait_ge(s("ov_psum"), k + 1)
                    for i in range(2):
                        v.tensor_tensor(ov_adj[:, i, :], ov_adj[:, i, :], bank[i][:, 0:T * WN], ALU.add)
                    sg = seg_t[:, bass.ds(win * WN, WN)]
                    v.tensor_tensor(sg, sg, bank[4][0:EF, 0:WN], ALU.add)
                    d.drain().then_inc(s("ov_added"), 1)

        def scan_vector(d, layer):
            d.wait_ge(s("scan_loaded"), 80 * (layer + 1))
            v.tensor_copy(dst_f, dst_i)
            v.tensor_copy(edge_f, edge_dst)
            d.drain()
            v.tensor_tensor(pen[:, 1:EC], dst_f[:, 1:EC], dst_f[:, 0:EC - 1], ALU.is_equal)
            v.memset(pen[:, 0:1], 1.0)
            v.memset(pen[:, EC:EC + 1], 1.0)
            v.tensor_tensor(pens[:, 0:1], edge_f[:, 0:1], dst_f[:, 0:1], ALU.is_equal)
            v.tensor_tensor(pens[:, 1:2], edge_f[:, 1:2], dst_f[:, EC - 1:EC], ALU.is_equal)
            v.tensor_tensor(pens[:, 2:3], dst_f[:, 0:1], dst_f[:, EC - 1:EC], ALU.is_equal)
            v.tensor_scalar(penf[:, 0], dst_f, dst_f[:, 0:1], None, ALU.is_equal)
            v.tensor_scalar(penf[:, 1], dst_f, dst_f[:, EC - 1:EC], None, ALU.is_equal)
            d.drain()
            v.tensor_scalar(pens[:, 0:3], pens[:, 0:3], 1.0, BIG, ALU.subtract, ALU.mult)
            v.tensor_scalar(pen, pen, 1.0, BIG, ALU.subtract, ALU.mult)
            v.tensor_scalar(flat(penf), flat(penf), 1.0, BIG, ALU.subtract, ALU.mult)
            d.drain()
            d.wait_ge(s("el_copied"), NB * (layer + 1))
            for h in range(H):
                v.tensor_tensor_scan(mx_e[:, h, :], pen[:, 0:EC], el_e[:, h, :], -BIG, ALU.add, ALU.max)
                v.tensor_tensor_scan(scan_b[:, ::-1], pen[:, 1:EC + 1][:, ::-1], el_e[:, h, ::-1], -BIG, ALU.add, ALU.max)
                d.drain()
                v.tensor_tensor(mx_e[:, h, :], mx_e[:, h, :], scan_b, ALU.max)
                d.drain()
            v.tensor_copy(ends[:, 0, :], mx_e[:, :, EC - 1])
            v.tensor_copy(ends[:, 1, :], mx_e[:, :, 0])
            v.tensor_tensor(pens[:, 3:4], pens[:, 0:1], pens[:, 2:3], ALU.add)
            d.drain()
            v.tensor_copy(ends[:, 2, :], pens[:, 3:4].to_broadcast([P, H]))
            v.tensor_copy(ends[:, 4, :], pens[:, 0:1].to_broadcast([P, H]))
            v.tensor_copy(ends[:, 5, :], pens[:, 1:2].to_broadcast([P, H]))
            v.tensor_tensor(pens[:, 4:5], pens[:, 1:2], pens[:, 2:3], ALU.add)
            d.drain()
            v.tensor_copy(ends[:, 3, :], pens[:, 4:5].to_broadcast([P, H]))
            d.drain().then_inc(s("ends_made"), 1)
            d.wait_ge(s("ends_t"), layer + 1)
            v.tensor_copy(flat(rows_t), bank[6][0:H, 0:4 * P])
            d.drain()
            for i in range(2):
                v.tensor_tensor_scan(chain[:, i, :], rows_t[:, 2 + i, :], rows_t[:, i, :], -BIG, ALU.add, ALU.max)
            v.memset(carry[:, 0, 0:1], -BIG)
            v.memset(carry[:, 1, P - 1:P], -BIG)
            d.drain()
            v.tensor_copy(carry[:, 0, 1:P], chain[:, 0, 0:P - 1])
            v.tensor_copy(carry[:, 1, 0:P - 1], chain[:, 1, 0:P - 1][:, ::-1])
            d.drain().then_inc(s("chain_made"), 1)
            d.wait_ge(s("chain_t"), layer + 1)
            for i in range(2):
                v.tensor_tensor(carry_e[:, i, :], ends[:, 4 + i, :], bank[7][:, i * H:(i + 1) * H], ALU.add)
            d.drain()
            for h in range(H):
                for i in range(2):
                    v.scalar_tensor_tensor(mx_e[:, h, :], penf[:, i], carry_e[:, i, h:h + 1], mx_e[:, h, :], ALU.add, ALU.max)
                    d.drain()
            for c in range(8):
                if c >= 2:
                    d.wait_ge(rec2_stored[c % 2], 16 * (4 * layer + c // 2))
                cols = slice(c * RC, (c + 1) * RC)
                o = rec2_c[:, c % 2]
                if c == 0:
                    v.tensor_copy(scan_b, dst_f)
                    d.drain()
                v.tensor_copy(o[:, :, 0:H], el_e[:, :, cols].rearrange("p h c -> p c h"))
                v.tensor_copy(o[:, :, H:2 * H], mx_e[:, :, cols].rearrange("p h c -> p c h"))
                v.tensor_copy(o[:, :, 2 * H], scan_b[:, cols])
                d.drain().then_inc(s("rec2_made"), 1)

        def logits(d, par, recs, er, wn, nw):
            n = nw * CH
            r = recs.rearrange("p w (c r) -> p c w r", r=REC2)
            v.tensor_tensor(gdl[:, par, 0:n].rearrange("p (c w) -> p c w", c=CH), r[:, :, :, 2 * H], bc(wn, 1, CH), ALU.subtract)
            d.drain()
            v.tensor_tensor(goh[:, par, 0:n, :], bc(gdl[:, par, 0:n], 2, WN), bc(iota_wn, 1, n), ALU.is_equal)
            d.drain()
            e = er.rearrange("p (w j h) -> p w h j", j=WN, h=H)
            for c in range(CH):
                o = gpr[:, c * nw * H:(c + 1) * nw * H, :].rearrange("p (w h) j -> p w h j", h=H)
                v.tensor_tensor(o, bc(goh[:, par, c * nw:(c + 1) * nw, :], 2, H), e, ALU.mult)
            d.drain()
            v.tensor_reduce(gq[:, 0:n * H], gpr[:, 0:n * H, :], AX.X, ALU.add)
            d.drain()
            q = gq[:, 0:n * H].rearrange("p (c w h) -> p c w h", c=CH, h=H)
            for i in range(2):
                v.tensor_tensor(gu[:, i, 0:n * H].rearrange("p (c w h) -> p c w h", c=CH, h=H), r[:, :, :, i * H:(i + 1) * H], q, ALU.add)
            d.drain()
            u = gu[:, :, 0:n * H]
            v.scalar_tensor_tensor(u, u, 0.2, u, ALU.mult, ALU.max)
            d.drain()
            v.tensor_tensor(gd[:, par, 0:n * H], gu[:, 0, 0:n * H], gu[:, 1, 0:n * H], ALU.subtract)

        def weighted(par, n):
            v.tensor_tensor(grh[:, par, 0:n, :].rearrange("p n (h j) -> p n h j", h=H), bc(goh[:, par, 0:n, :], 2, H),
                            bc(gex[:, par, 0:n * H].rearrange("p (n h) -> p n h", h=H), 3, WN), ALU.mult)

        def win_vector(d, layer):
            ng = NG * B * layer

            def weigh(par, count):
                d.wait_ge(s("exp_made"), count)
                weighted(par, CH * WG)
                d.drain().then_inc(s("rhs_made"), 1)

            for b in rounds(d, B, layer == 0):
                for g in range(NG):
                    par = g % 2
                    d.wait_ge(win_loaded[g], b * (16 * 11) + 16 * 11 * (B * layer + 1))
                    d.wait_ge(s("win_psum"), b * NG + (ng + max(0, g - 1)))
                    w0 = b * (NG * WG) + g * WG
                    logits(d, par, rec2_sl[:, g], er_sl[:, g], win_node[:, bass.ds(w0, WG)], WG)
                    d.drain().then_inc(s("logits_made"), 1)
                    d.sem_inc(win_used[g], 1)
                    weigh(par, b * NG + (ng + g + 1))

        def win_overflow_vector(d, layer):
            count = d.value_load(n_items, min_val=0, max_val=NW)
            with d.If(count > 0):
                with d.Fori(0, count) as k:
                    kk = ga_base(d, layer) + k
                    win = item(d, 1, k, NW - 1)
                    d.wait_ge(s("ga_loaded"), kk * 64 + 64)
                    logits(d, 0, rec2_sl[:, 0, 0:1], er_sl[:, 0, 0:WN * H], win_node[:, bass.ds(win, 1)], 1)
                    d.drain().then_inc(s("ga_logits"), 1)
                    d.wait_ge(s("ga_exp"), kk + 1)
                    weighted(0, CH)
                    d.drain().then_inc(s("ga_rhs"), 1)
                    d.wait_ge(s("ga_psum"), kk + 1)
                    v.tensor_tensor(ov_agg, ov_agg, bank[0][0:AGG, 0:H * WN], ALU.add)
                    d.drain().then_inc(s("ga_added"), 1)

        def gat_vector(d, layer):
            base = layer * B
            for i in rounds(d, B // NG, layer == 0):
                for u in range(NG):
                    n = i * NG + (u + base)
                    t0 = (i * NG + u) * 2
                    d.wait_ge(s("gat_psum"), n + 1)
                    for half in range(2):
                        y = bank[2 + half][0:NT, 0:H * AGG].rearrange("p (h f) -> p h f", h=H)
                        v.tensor_scalar(srec[:, half, :], y[:, :, F], 1e-30, None, ALU.max)
                    d.drain().then_inc(agg_used[u], 1)
                    v.reciprocal(flat(srec), flat(srec))
                    d.drain()
                    for half in range(2):
                        y = bank[2 + half][0:NT, 0:H * AGG].rearrange("p (h f) -> p h f", h=H)
                        v.tensor_tensor(yv[:, half, :].rearrange("p (h f) -> p h f", h=H), y[:, :, 0:F], bc(srec[:, half, :], 2, F), ALU.mult)
                    d.drain()
                    v.tensor_tensor(yv, yv, bc(gbias, 1, 2), ALU.add)
                    d.drain().then_inc(s("gat_y"), 1)
                    src = yv
                    if layer == 0:
                        d.wait_ge(s("gat_tanh"), n + 1)
                        src = yt
                    for half in range(2):
                        v.tensor_reduce(hm[:, half, :], src[:, half, :].rearrange("p (h f) -> p f h", h=H), AX.X, ALU.add)
                    d.drain()
                    if layer == 0:
                        v.tensor_scalar(flat(hm), flat(hm), 1.0 / H, None, ALU.mult)
                        d.drain().then_inc(s("gat_h"), 1)
                        v.tensor_copy(xt[:, bass.ds(t0, 2), 0:F], hm)
                        d.wait_ge(s("gat_v"), n + 1)
                        e = bank[5][0:NT, 0:4 * H].rearrange("p (t k) -> p t k", k=2 * H)
                        v.tensor_copy(xt[:, bass.ds(t0, 2), F + 1:XC], e[:, :, 0:H])
                        v.tensor_copy(er_sb[:, bass.ds(t0, 2), :], e[:, :, H:2 * H])
                        d.drain().then_inc(s("gat_xt"), 1)
                    else:
                        v.scalar_tensor_tensor(x_sb[:, bass.ds(t0, 2), :], hm, 1.0 / H, x_sb[:, bass.ds(t0, 2), :], ALU.mult, ALU.add)
                        d.drain()

        ln_count = [0]

        def layer_norm(d):
            ln_count[0] += 1
            v.tensor_reduce(colm[:, 0, :], x_sb, AX.X, ALU.add)
            d.drain()
            v.tensor_scalar(colm[:, 0, :], colm[:, 0, :], 1.0 / F, None, ALU.mult)
            d.drain()
            v.tensor_tensor(x_sb, x_sb, bc(colm[:, 0, :], 2, F), ALU.subtract)
            d.drain()
            v.tensor_tensor(sq, x_sb, x_sb, ALU.mult)
            d.drain()
            v.tensor_reduce(colm[:, 1, :], sq, AX.X, ALU.add)
            d.drain()
            v.tensor_scalar(colm[:, 1, :], colm[:, 1, :], 1.0 / F, LN_EPS, ALU.mult, ALU.add)
            d.drain().then_inc(s("ln_var"), 1)
            d.wait_ge(s("ln_std"), ln_count[0])
            v.reciprocal(colm[:, 3, :], colm[:, 2, :])
            d.drain()
            v.tensor_tensor(x_sb, x_sb, bc(colm[:, 3, :], 2, F), ALU.mult)
            d.drain()

        def per_node_vector(d):
            d.wait_ge(s("conv_w"), CONV_W)
            v.memset(we[0:ED, 0:1], 0.0)
            v.memset(we[ED:EF, :], 0.0)
            d.drain()
            v.tensor_copy(we[ED:EF, 0:1], ident[ED:EF, EF - 1:EF])
            v.tensor_tensor(we[ED:ED + 1, 1:QC], bsum[ED:ED + 1, 0, :], bsum[ED:ED + 1, 1, :], ALU.add)
            d.drain().then_inc(s("we_made"), 1)
            for b in rounds(d, B, False):
                d.wait_ge(s("pn_psum"), b + 1)
                v.tensor_copy(per_node[:, bass.ds(b * 2, 2), :], bank[0][0:NT, 0:2 * QC].rearrange("p (t q) -> p t q", q=QC)).then_inc(s("pn_evac"), 1)
            d.wait_ge(s("pn_evac"), B)
            v.tensor_scalar(colm[:, 3, :], per_node[:, :, 0], 1.0, None, ALU.add)
            d.drain()
            v.tensor_scalar(colm[:, 0, :], colm[:, 3, :], 0.0, None, ALU.is_gt)
            v.tensor_scalar(colm[:, 1, :], colm[:, 3, :], 1e-30, None, ALU.max)
            d.drain().then_inc(s("ln_var"), 1)
            ln_count[0] += 1
            d.wait_ge(s("ln_std"), ln_count[0])
            v.reciprocal(colm[:, 3, :], colm[:, 2, :])
            d.drain()
            v.tensor_tensor(dinv, colm[:, 3, :], colm[:, 0, :], ALU.mult)
            d.drain()

        def conv_vector(d, n, x_in, x_out):
            for b in rounds(d, B, n == 0):
                k = b + n * B
                t2 = bass.ds(b * 2, 2)
                d.wait_ge(s("cv_agg"), k)
                v.tensor_copy(xd[:, 0], x_in[:, t2, :])
                if n == 0:
                    d.wait_ge(s("cv_done"), 1)
                    v.tensor_copy(xd[:, 1], x_sb[:, t2, :])
                d.drain().then_inc(s("cv_self"), 1)
                d.wait_ge(s("cv_y"), k + 1)
                y = bank[2][0:NT, 0:2 * F].rearrange("p (t f) -> p t f", f=F)
                if n < 3:
                    dv = bc(dinv[:, t2], 2, F)
                    v.tensor_tensor(yc[:, 0], y, dv, ALU.mult)
                    d.drain()
                    v.tensor_tensor(yc[:, 0], yc[:, 0], bc(bconv[:, n, :], 1, 2), ALU.add)
                    d.drain()
                    v.tensor_scalar(flat(yc[:, 0]), flat(yc[:, 0]), 0.0, None, ALU.max)
                    d.drain().then_inc(s("cv_ev"), 1)
                    if n < 2:
                        v.tensor_tensor(x_out[:, t2, :], yc[:, 0], dv, ALU.mult)
                    d.wait_ge(s("cv_f"), k + 1)
                    f = bank[5][0:NT, 0:2 * F].rearrange("p (t f) -> p t f", f=F)
                    if n == 0:
                        v.tensor_copy(facc[:, t2, :], f)
                    else:
                        v.tensor_tensor(facc[:, t2, :], facc[:, t2, :], f, ALU.add)
                    d.drain()
                elif n == 3:
                    v.tensor_copy(x_out[:, t2, :], y)
                    d.drain().then_inc(s("cv_ev"), 1)
                else:
                    l = n - 4
                    v.tensor_tensor(yc[:, 0], y, per_node[:, t2, 1 + l * F:1 + (l + 1) * F], ALU.add)
                    d.drain().then_inc(s("cv_ev"), 1)
                    v.tensor_tensor(yc[:, 0], yc[:, 0], bc(bconv[:, 4 + l, :], 1, 2), ALU.add)
                    d.drain()
                    v.tensor_scalar(flat(yc[:, 0]), flat(yc[:, 0]), 0.0, None, ALU.max)
                    d.drain()
                    v.tensor_tensor(x_out[:, t2, :], yc[:, 0], bc(bconv[:, 6 + l, :], 1, 2), ALU.add)
                    d.drain()

        def batch_norm(d, z, l):
            v.tensor_reduce(stat[:, 0, :], z.rearrange("p t f -> p f t"), AX.X, ALU.add)
            d.drain().then_inc(s("bn_sum"), 1)
            d.wait_ge(s("bn_mean"), 2 * l + 1)
            v.tensor_scalar(stat[:, 1, :], bank[6][0:NT, 0:F], 1.0 / N, None, ALU.mult)
            d.drain()
            v.tensor_tensor(z, z, bc(stat[:, 1, :], 1, T), ALU.subtract)
            d.drain()
            v.tensor_tensor(sq, z, z, ALU.mult)
            d.drain()
            v.tensor_reduce(stat[:, 0, :], sq.rearrange("p t f -> p f t"), AX.X, ALU.add)
            d.drain().then_inc(s("bn_sum"), 1)
            d.wait_ge(s("bn_mean"), 2 * l + 2)
            v.tensor_scalar(stat[:, 2, :], bank[6][0:NT, 0:F], 1.0 / N, BN_EPS, ALU.mult, ALU.add)
            d.drain().then_inc(s("bn_var"), 1)
            d.wait_ge(s("bn_std"), l + 1)
            v.reciprocal(stat[:, 4, :], stat[:, 3, :])
            d.drain()
            v.tensor_tensor(stat[:, 4, :], stat[:, 4, :], bconv[:, 8 + 2 * l, :], ALU.mult)
            d.drain()
            v.tensor_tensor(z, z, bc(stat[:, 4, :], 1, T), ALU.mult)
            d.drain()
            v.tensor_tensor(z, z, bc(bconv[:, 9 + 2 * l, :], 1, T), ALU.add)
            d.drain()

        @block.vector
        def _(d):
            prep_vector(d)
            ptr_vector(d)
            logit_weights_vector(d)
            table0_vector(d)
            adj_vector(d)
            adj_overflow_vector(d)
            scan_vector(d, 0)
            win_vector(d, 0)
            win_overflow_vector(d, 0)
            gat_vector(d, 0)
            d.drain().then_inc(s("table_made"), 1)
            d.sem_inc(s("gat_done"), 1)
            scan_vector(d, 1)
            win_vector(d, 1)
            win_overflow_vector(d, 1)
            gat_vector(d, 1)
            d.drain().then_inc(s("gat_done"), 1)
            layer_norm(d)
            per_node_vector(d)
            v.tensor_tensor(xin, x_sb, bc(dinv, 2, F), ALU.mult)
            d.drain().then_inc(s("cv_done"), 1)
            conv_vector(d, 0, xin, hout)
            d.drain().then_inc(s("cv_done"), 1)
            conv_vector(d, 1, hout, xin)
            d.drain().then_inc(s("cv_done"), 1)
            conv_vector(d, 2, xin, None)
            v.tensor_tensor(x_sb, x_sb, facc, ALU.add)
            d.drain()
            v.tensor_tensor(x_sb, x_sb, bc(bconv[:, 3, :], 1, T), ALU.add)
            d.drain()
            layer_norm(d)
            d.drain().then_inc(s("cv_done"), 1)
            conv_vector(d, 3, x_sb, hout)
            v.tensor_copy(x_sb, hout)
            d.drain()
            layer_norm(d)
            d.drain().then_inc(s("cv_done"), 1)
            conv_vector(d, 4, x_sb, hout)
            batch_norm(d, hout, 0)
            d.drain().then_inc(s("cv_done"), 1)
            conv_vector(d, 5, hout, xin)
            batch_norm(d, xin, 1)
            v.tensor_tensor(x_sb, x_sb, xin, ALU.add)
            d.drain()
            layer_norm(d)
            d.drain().then_inc(s("cv_done"), 1)

        mm = nc.tensor.matmul

        def prep_tensor(pe):
            pe.wait_ge(s("xT_loaded"), 16)
            pe.wait_ge(s("v_made"), 1)
            for t in range(T):
                last = mm(bank[7][0:NT, t * 2 * H:(t + 1) * 2 * H], lhsT=xT_sb[:, t * NT:(t + 1) * NT], rhs=vw[:, 0, :], start=True, stop=True)
            last.then_inc(s("el_psum"), 1)

        def adj_window_mms(slot, g, w, wb, cb, seg, oh, seg_done=None):
            for c in range(CH):
                last = mm(seg, lhsT=ef_sl[:, g, w, c * EF:(c + 1) * EF], rhs=oh[:, c, :], start=(c == 0), stop=(c == CH - 1))
            if seg_done is not None:
                last.then_inc(seg_done, 1)
            for c in range(CH):
                for i in range(3):
                    mm(wb, lhsT=row_oh[:, slot, c, i, :], rhs=col_oh[:, slot, c, :], start=(c == 0 and i == 0), stop=(c == CH - 1 and i == 2))
            for c in range(CH):
                last = mm(cb, lhsT=row_oh[:, slot, c, 3, :], rhs=col_oh[:, slot, c, :], start=(c == 0), stop=(c == CH - 1))
            return last

        def adj_tensor(pe):
            for b in rounds(pe, B):
                for g in range(NG):
                    pe.wait_ge(adj_loaded[g], b * (32 * WG) + 32 * WG)
                    pe.wait_ge(s("seg_evacuated"), b * NG + max(0, g - 1))
                    for w in range(WG):
                        n = g * WG + w
                        pe.wait_ge(s("adj_evacuated"), b * (NG * WG) + max(0, n - 1))
                        pe.wait_ge(s("onehot_made"), b * (NG * WG) + (n + 1))
                        pair = 2 * (n % 2)
                        last = adj_window_mms(n % 2, g, w, bank[pair][:, 0:T * WN], bank[pair + 1][:, 0:T * WN],
                                              bank[4 + g % 2][0:EF, w * WN:(w + 1) * WN], coh[:, g % 2, w * CH:(w + 1) * CH, :],
                                              adj_used[g] if w == WG - 1 else None)
                        last.then_inc(s("adj_psum"), 1)

        def adj_overflow_tensor(pe):
            pe.wait_ge(s("adj_evacuated"), NW)
            pe.wait_ge(s("seg_evacuated"), NGR)
            count = pe.value_load(n_items, min_val=0, max_val=NW)
            with pe.If(count > 0):
                with pe.Fori(0, count) as k:
                    pe.wait_ge(s("ov_loaded"), k * 64 + 64)
                    pe.wait_ge(s("ov_onehot"), k + 1)
                    adj_window_mms(0, 0, 0, bank[0][:, 0:T * WN], bank[1][:, 0:T * WN], bank[4][0:EF, 0:WN], coh[:, 0, 0:CH, :]).then_inc(s("ov_psum"), 1)

        def scan_tensor(pe, layer):
            pe.wait_ge(s("ends_made"), layer + 1)
            for i in range(4):
                last = mm(bank[6][0:H, i * P:(i + 1) * P], lhsT=ends[:, i, :], rhs=flip if i % 2 else ident, start=True, stop=True)
            last.then_inc(s("ends_t"), 1)
            pe.wait_ge(s("chain_made"), layer + 1)
            for i in range(2):
                last = mm(bank[7][:, i * H:(i + 1) * H], lhsT=carry[:, i, :], rhs=ident[0:H, 0:H], start=True, stop=True)
            last.then_inc(s("chain_t"), 1)

        def win_tensor(pe, layer):
            ng = NG * B * layer
            for b in rounds(pe, B, layer == 0):
                for g in range(NG):
                    pe.wait_ge(win_loaded[g], b * (16 * 11) + 16 * 11 * (B * layer + 1))
                    pe.wait_ge(s("win_evac"), b * NG + (ng + max(0, g - 1)))
                    pe.wait_ge(s("rhs_made"), b * NG + (ng + g + 1))
                    for w in range(WG):
                        for c in range(CH):
                            last = mm(bank[g % 2][0:AGG, w * H * WN:(w + 1) * H * WN], lhsT=rows_sl[:, g, w, c * XC:c * XC + AGG],
                                      rhs=grh[:, g % 2, c * WG + w, :], start=(c == 0), stop=(c == CH - 1))
                    last.then_inc(s("win_psum"), 1)

        def win_overflow_tensor(pe, layer):
            pe.wait_ge(s("win_evac"), NGR * (layer + 1))
            count = pe.value_load(n_items, min_val=0, max_val=NW)
            with pe.If(count > 0):
                with pe.Fori(0, count) as k:
                    kk = ga_base(pe, layer) + k
                    pe.wait_ge(s("ga_rhs"), kk + 1)
                    for c in range(CH):
                        last = mm(bank[0][0:AGG, 0:H * WN], lhsT=rows_sl[:, 0, 0, c * XC:c * XC + AGG], rhs=grh[:, 0, c, :], start=(c == 0), stop=(c == CH - 1))
                    last.then_inc(s("ga_psum"), 1)

        def gat_tensor(pe, layer):
            pe.wait_ge(s("wgat_loaded"), 32 * (layer + 1))
            base = layer * B
            for i in rounds(pe, B // NG, layer == 0):
                for u in range(NG):
                    n = i * NG + (u + base)
                    pe.wait_ge(agg_loaded[u], i * 16 + 16 * (layer * (B // NG) + 1))
                    pe.wait_ge(s("gat_y"), n)
                    for half in range(2):
                        for h in range(H):
                            last = mm(bank[2 + half][0:NT, h * AGG:(h + 1) * AGG], lhsT=agg_sl[:, u, h, half * NT:(half + 1) * NT], rhs=wgat[:, h, :], start=True, stop=True)
                    last.then_inc(s("gat_psum"), 1)
                    if layer == 0:
                        pe.wait_ge(s("gat_h"), n + 1)
                        for half in range(2):
                            last = mm(bank[4][0:F, half * NT:(half + 1) * NT], lhsT=hm[:, half, :], rhs=ident[0:NT, 0:NT], start=True, stop=True)
                        last.then_inc(s("gat_hT"), 1)
                        pe.wait_ge(s("gat_hTc"), n + 1)
                        pe.wait_ge(s("gat_xt"), n)
                        for half in range(2):
                            last = mm(bank[5][0:NT, half * 2 * H:(half + 1) * 2 * H], lhsT=hT[:, half * NT:(half + 1) * NT], rhs=vw[:, 1, :], start=True, stop=True)
                        last.then_inc(s("gat_v"), 1)

        def per_node_tensor(pe):
            pe.wait_ge(s("we_made"), 1)
            for b in rounds(pe, B):
                pe.wait_ge(s("pn_copied"), b + 1)
                pe.wait_ge(s("pn_evac"), b)
                for half in range(2):
                    last = mm(bank[0][0:NT, half * QC:(half + 1) * QC], lhsT=segb[:, half * NT:(half + 1) * NT], rhs=we, start=True, stop=True)
                last.then_inc(s("pn_psum"), 1)

        def conv_tensor(pe, n, x_in):
            w = (wconv[:, n, :] if n < 3 else ident[0:F, 0:F] if n == 3 else wconv[:, n - 1, :])
            pe.wait_ge(s("cv_done"), n + 1)
            for b in rounds(pe, B, False):
                k = b + n * B
                agg = bank[0][0:F, 0:BN]
                for q in range(NQ):
                    pe.wait_ge(cv_loaded[q], b * 16 + 16 * (n * B + 1))
                    for t in range(QT):
                        last = mm(agg.rearrange("p (g n) -> p g n", n=GN), lhsT=x_in[:, q * QT + t, :], rhs=adj_sl[0:NT, q, :, t * GN:(t + 1) * GN],
                                  start=(q == 0 and t == 0), stop=False)
                    last.then_inc(cv_used[q], 1)
                pe.wait_ge(s("cv_self"), k + 1)
                for half in range(2):
                    last = mm(bank[0][0:F, half * NT:(half + 1) * NT], lhsT=xd[:, 0, half, :], rhs=ident[0:NT, 0:NT], start=False, stop=(half == 1))
                last.then_inc(s("cv_agg"), 1)
                pe.wait_ge(s("cv_aggc"), k + 1)
                for half in range(2):
                    last = mm(bank[2][0:NT, half * F:(half + 1) * F], lhsT=aggs[:, half * NT:(half + 1) * NT], rhs=w, start=True, stop=True)
                last.then_inc(s("cv_y"), 1)
                pe.wait_ge(s("cv_ev"), k + 1)
                if n < 3:
                    for i in range(2 if n == 0 else 1):
                        for half in range(2):
                            last = mm(bank[3 + i][0:F, half * NT:(half + 1) * NT], lhsT=xd[:, 1, half, :] if i else yc[:, 0, half, :], rhs=ident[0:NT, 0:NT], start=True, stop=True)
                    last.then_inc(s("cv_yT"), 1)
                    pe.wait_ge(s("cv_yTc"), k + 1)
                    for half in range(2):
                        for i in range(2 if n == 0 else 1):
                            last = mm(bank[5][0:NT, half * F:(half + 1) * F], lhsT=yT[:, i, half * NT:(half + 1) * NT], rhs=wf[:, 0 if i else n + 1, :],
                                      start=(i == 0), stop=(n > 0 or i == 1))
                    last.then_inc(s("cv_f"), 1)

        def batch_norm_tensor(pe, l):
            for i in range(2):
                pe.wait_ge(s("bn_sum"), 2 * l + i + 1)
                mm(bank[6][0:NT, 0:F], lhsT=ones[0:NT, 0:NT], rhs=stat[:, 0, :], start=True, stop=True).then_inc(s("bn_mean"), 1)

        @block.tensor
        def _(pe):
            prep_tensor(pe)
            pe.wait_ge(s("table_made"), 1)
            adj_tensor(pe)
            adj_overflow_tensor(pe)
            for layer in range(2):
                scan_tensor(pe, layer)
                win_tensor(pe, layer)
                win_overflow_tensor(pe, layer)
                gat_tensor(pe, layer)
            per_node_tensor(pe)
            for n, x_in in enumerate((xin, hout, xin, x_sb, x_sb, hout)):
                conv_tensor(pe, n, x_in)
                if n >= 4:
                    batch_norm_tensor(pe, n - 4)

        act_ = nc.scalar.activation

        def adj_scalar(act):
            act.wait_ge(s("items_back"), 16)
            act.wait_ge(s("el_psum"), 1)
            for b in rounds(act, B):
                for g in range(NG):
                    st = g % 3
                    act.wait_ge(adj_stored[st], b * (32 * (2, 2, 1)[st]) + 32 * (g >= 3))
                    for w in range(WG):
                        n = g * WG + w
                        act.wait_ge(s("adj_psum"), b * (NG * WG) + (n + 1))
                        for i in range(2):
                            last = act_(stage[:, st, i, :, w * WN:(w + 1) * WN], bank[2 * (n % 2) + i][:, 0:T * WN].rearrange("p (t n) -> p t n", n=WN), ACT.Copy)
                        last.then_inc(s("adj_evacuated"), 1)
                    group = b * NG + g
                    act_(seg_t[:, bass.ds(group * GN, GN)], bank[4 + g % 2][0:EF, 0:GN], ACT.Copy).then_inc(s("seg_evacuated"), 1)
                    act.wait_ge(s("adj_evacuated"), b * (NG * WG) + (g + 1) * WG)
                    for i, d in enumerate((adj_w_d, adj_c_d)):
                        act.dma_start(d[bass.ds(group, 1), :, :, :].rearrange("a p t n -> p (a t n)"), flat(stage[:, st, i])).then_inc(adj_stored[st], 16)

        def win_scalar(act, layer):
            ng = NG * B * layer
            for b in rounds(act, B, layer == 0):
                for g in range(NG):
                    par = g % 2
                    act.wait_ge(s("logits_made"), b * NG + (ng + g + 1))
                    act_(gex[:, par, :], gd[:, par, :], ACT.Exp).then_inc(s("exp_made"), 1)
                    act.wait_ge(win_stored[g], b * 16 + 16 * B * layer)
                    act.wait_ge(s("win_psum"), b * NG + (ng + g + 1))
                    act_(gst[:, g].rearrange("p h (w j) -> p w h j", j=WN), bank[par][0:AGG, 0:WG * H * WN].rearrange("p (w h j) -> p w h j", w=WG, h=H), ACT.Copy).then_inc(s("win_evac"), 1)
                    act.wait_ge(s("win_evac"), b * NG + (ng + g + 1))
                    act.sem_inc(win_used[g], 1)
                    act.dma_start(agg_d[:, :, bass.ds(b * BN + g * GN, GN)], gst[:, g]).then_inc(win_stored[g], 16)

        def win_overflow_scalar(act, layer):
            count = act.value_load(n_items, min_val=0, max_val=NW)
            with act.If(count > 0):
                with act.Fori(0, count) as k:
                    kk = ga_base(act, layer) + k
                    act.wait_ge(s("ga_logits"), kk + 1)
                    act_(gex[:, 0, 0:CH * H], gd[:, 0, 0:CH * H], ACT.Exp).then_inc(s("ga_exp"), 1)

        def gat_scalar(act, layer):
            base = layer * B
            if layer:
                return
            for n in rounds(act, B, False):
                act.wait_ge(s("gat_y"), n + 1)
                act_(flat(yt), flat(yv), ACT.Tanh).then_inc(s("gat_tanh"), 1)
                act.wait_ge(s("gat_hT"), n + 1)
                act_(hT, bank[4][0:F, 0:BN], ACT.Copy).then_inc(s("gat_hTc"), 1)

        std_count = [0]

        def std_scalar(act):
            std_count[0] += 1
            act.wait_ge(s("ln_var"), std_count[0])
            act_(colm[:, 2, :], colm[:, 1, :], ACT.Sqrt).then_inc(s("ln_std"), 1)

        def per_node_scalar(act):
            act.wait_ge(s("we_made"), 1)
            for b in rounds(act, B):
                act.wait_ge(s("pn_psum"), b)
                act_(segb, seg_t[:, bass.ds(b * BN, BN)], ACT.Copy).then_inc(s("pn_copied"), 1)

        def conv_scalar(act, n):
            for b in rounds(act, B, False):
                k = b + n * B
                act.wait_ge(s("cv_agg"), k + 1)
                act_(aggs, bank[0][0:F, 0:BN], ACT.Copy).then_inc(s("cv_aggc"), 1)
                if n < 3:
                    act.wait_ge(s("cv_yT"), k + 1)
                    for i in range(2 if n == 0 else 1):
                        last = act_(yT[:, i, :], bank[3 + i][0:F, 0:BN], ACT.Copy)
                    last.then_inc(s("cv_yTc"), 1)

        @block.scalar
        def _(act):
            adj_scalar(act)
            for layer in range(2):
                win_scalar(act, layer)
                win_overflow_scalar(act, layer)
                gat_scalar(act, layer)
            std_scalar(act)
            per_node_scalar(act)
            std_scalar(act)
            for n in range(6):
                conv_scalar(act, n)
                if n in (2, 3):
                    std_scalar(act)
                if n >= 4:
                    act.wait_ge(s("bn_var"), n - 3)
                    act_(stat[:, 3, :], stat[:, 2, :], ACT.Sqrt).then_inc(s("bn_std"), 1)
            std_scalar(act)


_OUT = ((N, F), "float32")


def kernel(**inputs):
    import concourse.bacc as bacc
    from concourse.bass_utils import run_bass_kernel_spmd as run

    nc = bacc.Bacc("TRN2", target_bir_lowering=False, num_devices=1)
    g = {k: np.ascontiguousarray(v) for k, v in inputs.items()}
    pad = EP - E
    src = np.concatenate([g.pop("src"), np.zeros(pad, np.int32)])
    dst = np.concatenate([g.pop("dst"), np.full(pad, N + 22, np.int32)])
    ew = g.pop("edge_weight")
    ea = g.pop("edge_attr_32")
    feats = np.zeros((EP, EF), np.float32)
    feats[:E, 0:ED] = ea
    feats[:E, ED] = 1.0
    feats[:E, ED + 1] = ew
    g["src"] = src.reshape(P, EC)
    g["dst"] = dst.reshape(EC, P)
    g["dst_heads"] = np.ascontiguousarray(dst.reshape(EC, P)[:, 0]).reshape(1, EC)
    g["edge_weight"] = np.concatenate([ew, np.zeros(pad, np.float32)]).reshape(P, EC)
    g["edge_features"] = feats
    g["xT"] = np.ascontiguousarray(g["x"].T)
    arrays, aps = {}, {}
    for k, v in g.items():
        arrays[f"in_{k}"] = v
        aps[k] = nc.dram_tensor(f"in_{k}", v.shape, mybir.dt.from_np(v.dtype), kind="ExternalInput").ap()
    aps["out"] = nc.dram_tensor("out_0", _OUT[0], F32, kind="ExternalOutput").ap()
    build(nc, aps)
    r = run(nc, [arrays], core_ids=[0])
    return r.results[0]["out_0"]
```

```python
import numpy as np
import concourse.bass as bass
from concourse import mybir
from contextlib import ExitStack

F32 = mybir.dt.float32
I32 = mybir.dt.int32
F16 = mybir.dt.float16
BF16 = mybir.dt.bfloat16
ALU = mybir.AluOpType
ACT = mybir.ActivationFunctionType
AX = mybir.AxisListType

N = 6250
E = 200000
F = 64
H = 4
ED = 32
P = 128

EC = 1568
EP = P * EC

WN = 10
WG = 5
NG = 5
GN = WN * WG
BN = GN * NG
NT = BN // 2
T = N // NT
B = N // BN
NW = N // WN
NGR = N // GN
CH = 3
CAP = CH * P
WH = H * WN
TW = 3
KEY = 512
REC = 7
XC = F + 1 + H
EF = ED + 2
AGG = F + 1
QC = 1 + 2 * F
NQ = 5
QT = T // NQ
BIG = 1.0e30
RND = 12582912.0
LN_EPS = 1e-05
BN_EPS = 1e-05


def build(nc, a):
    ctx = ExitStack()
    with ctx:
        def dram(name, shape, dt=F32):
            return nc.dram_tensor(name, shape, dt, kind="Internal").ap()

        def sem(name):
            return ctx.enter_context(nc.semaphore(name))

        rec_d = dram("rec_d", [EP, REC])
        max_d = dram("max_d", [1, NW * WH])
        table_d = dram("table_d", [N, XC])
        er_d = dram("er_d", [N, H])
        agg_d = dram("agg_d", [AGG, H, N])
        adj_w_d = dram("adj_w_d", [NGR, P, T, GN])
        adj_c_d = dram("adj_c_d", [NGR, P, T, GN])
        ptr_d = dram("ptr_d", [1, NW + 1])
        items_d = dram("items_d", [4, NW], I32)
        ptri_d = dram("ptri_d", [1, NW + 1], I32)

        SB = 53000
        arena = ctx.enter_context(nc.sbuf_tensor("arena", [P, SB], F32))
        top = [0]

        def at(off, parts, *dims):
            n = int(np.prod(dims))
            assert off + n <= SB, (off, n)
            v = arena[0:parts, off:off + n]
            if len(dims) == 1:
                return v
            names = "abcde"[:len(dims)]
            return v.rearrange(f"p ({' '.join(names)}) -> p {' '.join(names)}",
                               **{names[i]: dims[i] for i in range(1, len(dims))})

        def new(parts, *dims):
            off = top[0]
            top[0] += (int(np.prod(dims)) + 7) // 8 * 8
            return at(off, parts, *dims)

        x_sb = new(NT, T, F)
        dinv = new(NT, T)
        ident = new(P, P)
        flip = new(P, P)
        ones = new(P, P)
        iota_wn = new(P, WN)
        iota_key = new(P, T * WN // 2).bitcast(F16)
        iota_lo = new(P, P // 2).bitcast(F16)
        win_node = new(P, NW)
        win_key = new(P, NW)
        ptr_row = new(1, NW + 1).bitcast(I32)
        items = new(1, 4 * NW).bitcast(I32)
        n_items = new(1, 1).bitcast(I32)
        seg_t = new(EF, N)
        fixed = top[0]

        xt = new(NT, T, XC)
        er_sb = new(NT, T, H)
        wgat = new(AGG, H, AGG)
        vw = new(F, 2, 2 * H)
        gbias = new(NT, H * F)
        rec_sl = new(P, NG, WG, CH * REC)
        ef_sl = new(P, NG, WG, CH * EF)
        rows_top = top[0]
        rows_sl = new(P, NG, WG, CH, XC)
        er_sl = new(P, NG, GN * H)
        ckey = new(P, WG * CH)
        cdl = new(P, WG * CH)
        coh = new(P, 2, WG * CH, WN)
        pen = new(P, WG * CH, WN)
        lg = new(P, WG, CH, H, WN)
        top_e = new(P, WG * WH)
        top_s = new(TW * WH, 2)
        diag = new(TW * WH, 2, TW * WH)
        top_row = new(1, 2, WG * WH)
        gd = new(P, 2, WG * CH, WH)
        grh = new(P, 2, WG * CH, WH)
        gst = new(AGG, NG, H, GN)
        top_o = new(P, 3, WH)
        ov_agg = new(AGG, WH)
        oh_top = top[0]
        col_oh = new(P, 2, CH, T * WN // 2).bitcast(BF16)
        row_oh = new(P, 2, CH, 4, P // 2).bitcast(BF16)
        over = top[0]
        stage = new(P, 3, 2, T, GN)
        assert top[0] <= SB, top[0]
        wv = at(oh_top, F, 2, H * F)
        alr = at(oh_top + 2 * H * F, F, 4, H * F)
        vprod = at(oh_top + 6 * H * F, F, 4, H * F)
        top[0] = over
        rec_all = new(P, EC, REC)
        tmp = [at(rows_top + i * EC, P, EC) for i in range(3)] + [new(P, EC)]
        src_idx = new(P, EC).bitcast(I32)
        hi_bf = new(P, EC // 2).bitcast(BF16)
        assert top[0] <= SB, top[0]
        heads = at(over, NT, EC)
        heads_f = at(over + EC, NT, EC)
        junk = at(over + 2 * EC, NT, EC)
        thr = at(over + 3 * EC, NT, 5)
        cnt = at(over + 3 * EC + 8, NT, 5)
        rowi = at(over + 3 * EC + 16, NT, 5).bitcast(I32)
        rowd = at(over + 3 * EC + 24, NT, 5, P).bitcast(I32)
        rowf = at(over + 3 * EC + 24 + 640, NT, 5, P)
        cnt2 = at(over + 3 * EC + 1400, NT, 5)
        ptr_f = at(over + 3 * EC + 1408, NT, 5)
        ptr_end = at(over + 3 * EC + 1416, 1, 1)
        o5 = over + 3 * EC + 1424
        ptrb = at(o5, NT, NW + 1)
        nover = at(o5 + 640, NT, NW)
        cum = at(o5 + 1280, NT, NW)
        offv = at(o5 + 1920, NT, NW)
        iota_nw = at(o5 + 2560, NT, NW)
        onesw = at(o5 + 3200, NT, NW)
        kid = at(o5 + 3840, NT, 5)
        itf = at(o5 + 3848, NT, 4, 5)
        iti = at(o5 + 3872, NT, 4, 5).bitcast(I32)
        ptr_i = at(o5 + 3896, NT, 5).bitcast(I32)
        itw = at(o5 + 3904, NT, 5)
        nif = at(o5 + 3912, 1, 2)
        o6 = o5 + 3920
        xT_sb = at(o6, F, N)
        top[0] = over
        agg_sl = new(AGG, NG, H, BN)
        srec = new(NT, 2, H)
        yv = new(NT, 2, H * F)
        yt = new(NT, 2, H * F)
        hm = new(NT, 2, F)
        hT = new(F, BN)
        ov_adj = at(over, P, 2, T * WN)
        top[0] = fixed
        per_node = new(NT, T, QC)
        xin = new(NT, T, F)
        facc = new(NT, T, F)
        hout = new(NT, T, F)
        sq = new(NT, T, F)
        adj_sl = new(P, NQ, NG, QT * GN)
        wconv = new(F, 5, F)
        wf = new(F, 4, F)
        we = new(EF, QC)
        bconv = new(NT, 12, F)
        bsum = new(EF, 2, 2 * F)
        xd = new(NT, 2, 2, F)
        aggs = new(F, BN)
        yc = new(NT, 2, 2, F)
        yT = new(F, 2, BN)
        stat = new(NT, 8, F)
        colm = new(NT, 4, T)
        segb = new(EF, BN)
        assert top[0] <= SB, top[0]

        bank = [ctx.enter_context(nc.psum_tensor(f"bank{i}", [P, 512], F32)) for i in range(8)]

        def bc(ap, axis, n):
            v = ap.unsqueeze(axis)
            shape = list(v.shape)
            shape[axis] = n
            return v.to_broadcast(shape)

        S = {}

        def s(name):
            if name not in S:
                S[name] = sem(name)
            return S[name]

        for names in (
            "consts_made pool_const edges_loaded heads_loaded weights_loaded x_loaded rec_made rec_stored "
            "ptr_rows_wanted ptr_rows_here ptr_made ptr_out ptr_back items_made items_out items_back xT_loaded "
            "v_made wgat_cleared wgat_loaded el_psum table_made table_stored er_stored "
            "onehot_made rows_weighted adj_psum adj_evacuated seg_evacuated ov_loaded ov_onehot ov_weighted ov_psum ov_added "
            "ov_stored top_made top_t diag_made top_psum logits_made exp_made win_psum win_evac "
            "ga_loaded ga_rows ga_top ga_topt ga_diag ga_topp ga_logits ga_exp ga_psum ga_added "
            "ga_stored gat_psum gat_y gat_tanh gat_h gat_hT gat_hTc gat_v gat_xt "
            "gat_done conv_w we_made pn_copied pn_psum pn_evac out_stored ln_var ln_std passed_sp passed_pool "
            "cv_self cv_agg cv_aggc cv_y cv_ev cv_yT cv_yTc cv_f cv_done bn_sum bn_mean bn_var bn_std "
        ).split():
            s(names)
        rec_loaded = [sem(f"rec_loaded{i}") for i in range(NG)]
        rec_used = [sem(f"rec_used{i}") for i in range(NG)]
        gathered = [sem(f"gathered{i}") for i in range(NG)]
        top_stored = [sem(f"top_stored{i}") for i in range(2)]
        adj_loaded = [sem(f"adj_loaded{i}") for i in range(NG)]
        adj_used = [sem(f"adj_used{i}") for i in range(NG)]
        adj_stored = [sem(f"adj_stored{i}") for i in range(3)]
        win_used = [sem(f"win_used{i}") for i in range(NG)]
        win_stored = [sem(f"win_stored{i}") for i in range(NG)]
        agg_loaded = [sem(f"agg_loaded{i}") for i in range(NG)]
        agg_used = [sem(f"agg_used{i}") for i in range(NG)]
        cv_loaded = [sem(f"cv_loaded{i}") for i in range(NQ)]
        cv_used = [sem(f"cv_used{i}") for i in range(NQ)]

        block = ctx.enter_context(nc.Block())

        def edge_rows(dram_ap, off):
            return dram_ap[bass.ds(off, CAP), :].rearrange("(p c) f -> p (c f)", c=CH)

        def nodes(dram_ap):
            return dram_ap.rearrange("(t p) f -> p t f", p=NT)

        def flat(ap):
            k = len(ap.shape) - 1
            if k == 1:
                return ap
            names = "abcde"[:k]
            return ap.rearrange(f"p {' '.join(names)} -> p ({' '.join(names)})")

        def wait_reg(eng, semaphore, value):
            eng.wait_ge(semaphore, value)
            eng.sem_inc(s(f"passed_{'sp' if eng is nc.sync else 'pool'}"), 1)

        def rounds(eng, count, peel=True):
            if peel:
                yield 0
            with eng.Fori(int(peel), count) as i:
                yield i

        def prep_sync(sp):
            sp.dma_start(src_idx, a["src"]).then_inc(s("edges_loaded"), 16)
            sp.dma_start(tmp[0].bitcast(I32), a["dst"].rearrange("a b -> (a b)").rearrange("(p c) -> p c", p=P)).then_inc(s("edges_loaded"), 16)
            sp.dma_start(tmp[1], a["edge_weight"]).then_inc(s("edges_loaded"), 16)
            sp.dma_start(x_sb, nodes(a["x"])).then_inc(s("x_loaded"), 16)
            sp.wait_ge(s("rec_made"), 1)
            sp.dma_start(rec_d.rearrange("(p c) f -> p (c f)", p=P), flat(rec_all)).then_inc(s("rec_stored"), 16)
            sp.wait_ge(s("rec_stored"), 16)
            sp.dma_start(heads.bitcast(I32), a["dst_heads"].partition_broadcast(NT) if False else a["dst_heads"].to_broadcast([NT, EC])).then_inc(s("heads_loaded"), 16)
            sp.dma_start(xT_sb, a["xT"]).then_inc(s("xT_loaded"), 16)
            sp.wait_ge(s("ptr_made"), 1)
            with nc.allow_non_contiguous_dma(reason="625 window starts"):
                sp.dma_start(ptr_d[0, 0:NW].rearrange("(c p) -> p c", p=NT), ptr_f).then_inc(s("ptr_out"), 16)
                sp.dma_start(ptri_d[0, 0:NW].rearrange("(c p) -> p c", p=NT), ptr_i).then_inc(s("ptr_out"), 16)
            sp.dma_start(ptr_d[:, NW:NW + 1], ptr_end).then_inc(s("ptr_out"), 16)
            sp.wait_ge(s("ptr_out"), 48)
            sp.dma_start(ptrb, ptr_d.to_broadcast([NT, NW + 1])).then_inc(s("ptr_back"), 16)
            sp.dma_start(ptr_row[:, 0:NW], ptri_d[:, 0:NW]).then_inc(s("ptr_back"), 16)
            sp.wait_ge(s("items_made"), 1)
            with nc.allow_non_contiguous_dma(reason="the overflow items"):
                for i in range(4):
                    sp.dma_start(items_d[i, :].rearrange("(c p) -> p c", p=NT), iti[:, i, :]).then_inc(s("items_out"), 16)
            sp.wait_ge(s("items_out"), 64)
            sp.dma_start(items, items_d.rearrange("i k -> (i k)").unsqueeze(0)).then_inc(s("items_back"), 16)
            sp.wait_ge(s("items_back"), 16)

        def logit_weights_sync(sp):
            for l in range(2):
                sp.dma_start(wv[:, l, :], a[f"L0_gnn_W{l + 1}"]).then_inc(s("weights_loaded"), 16)
                for i, n in enumerate(("al", "ar")):
                    sp.dma_start(alr[:, 2 * l + i, :], a[f"L0_gnn_{n}{l + 1}"].rearrange("h f -> (h f)").unsqueeze(0).to_broadcast([F, H * F])).then_inc(s("weights_loaded"), 16)

        def gat_weights_sync(sp, layer):
            if layer:
                sp.wait_ge(s("gat_done"), 1)
            else:
                sp.wait_ge(s("wgat_cleared"), 1)
            sp.dma_start(wgat[0:F, :, 0:F], a[f"L0_gnn_W{layer + 1}"].rearrange("k (h f) -> k h f", h=H)).then_inc(s("wgat_loaded"), 16)
            sp.dma_start(gbias, a[f"L0_gnn_b{layer + 1}"].rearrange("h f -> (h f)").unsqueeze(0).to_broadcast([NT, H * F])).then_inc(s("wgat_loaded"), 16)

        def table_sync(sp, layer):
            sp.wait_ge(s("table_made"), layer + 1)
            sp.dma_start(nodes(table_d), xt).then_inc(s("table_stored"), 16)
            sp.dma_start(nodes(er_d), er_sb).then_inc(s("er_stored"), 16)

        def win_sync(sp, layer):
            sp.wait_ge(s("er_stored"), 16 * (layer + 1))
            for b in rounds(sp, B, layer == 0):
                for g in range(NG):
                    wait_reg(sp, rec_used[g], b + layer * B)
                    if layer == 0:
                        wait_reg(sp, adj_used[g], b)
                    for w in range(WG):
                        off = sp.value_load(ptr_row[0:1, bass.ds(b * (NG * WG) + g * WG + w, 1)], min_val=0, max_val=EP - CAP)
                        sp.dma_start(rec_sl[:, g, w, :], edge_rows(rec_d, off)).then_inc(rec_loaded[g], 16)
                        if layer == 0:
                            sp.dma_start(ef_sl[:, g, w, :], edge_rows(a["edge_features"], off)).then_inc(adj_loaded[g], 16)
                    sp.dma_start(er_sl[:, g, :], er_d[bass.ds(b * BN + g * GN, GN), :].rearrange("n h -> (n h)").unsqueeze(0).to_broadcast([P, GN * H])).then_inc(rec_loaded[g], 16)
            for g in range(NG):
                sp.wait_ge(win_stored[g], 16 * B * (layer + 1))
            for i in range(2):
                sp.wait_ge(top_stored[i], 16 * (NG_PAR[i] * B) * (layer + 1))

        NG_PAR = ((NG + 1) // 2, NG // 2)
        LOADS = 16 * (WG + 1)

        def adj_window(d, group, node):
            return d[bass.ds(group, 1), :, :, bass.ds(node, WN)].rearrange("a p t n -> p (a t) n")

        def item(eng, row, k, top_):
            return eng.value_load(items[0:1, bass.ds(k + row * NW, 1)], min_val=0, max_val=top_)

        def adj_overflow_sync(sp):
            for i, n in enumerate((2, 2, 1)):
                sp.wait_ge(adj_stored[i], 32 * B * n)
            count = sp.value_load(n_items, min_val=0, max_val=NW)
            with sp.If(count > 0):
                with sp.Fori(0, count) as k:
                    off = item(sp, 0, k, EP - CAP)
                    group = item(sp, 2, k, NGR - 1)
                    node = item(sp, 3, k, GN - WN)
                    sp.dma_start(rec_sl[:, 0, 0, :], edge_rows(rec_d, off)).then_inc(s("ov_loaded"), 16)
                    sp.dma_start(ef_sl[:, 0, 0, :], edge_rows(a["edge_features"], off)).then_inc(s("ov_loaded"), 16)
                    for i, d in enumerate((adj_w_d, adj_c_d)):
                        sp.dma_start(ov_adj[:, i, :].rearrange("p (t n) -> p t n", n=WN), adj_window(d, group, node)).then_inc(s("ov_loaded"), 16)
                    sp.wait_ge(s("ov_added"), k + 1)
                    for i, d in enumerate((adj_w_d, adj_c_d)):
                        sp.dma_start(adj_window(d, group, node), ov_adj[:, i, :].rearrange("p (t n) -> p t n", n=WN)).then_inc(s("ov_stored"), 16)
                    wait_reg(sp, s("ov_stored"), k * 32 + 32)

        def agg_window(node):
            return agg_d[:, :, bass.ds(node, WN)]

        def win_overflow_sync(sp, layer):
            count = sp.value_load(n_items, min_val=0, max_val=NW)
            with sp.If(count > 0):
                with sp.Fori(0, count) as k:
                    off = item(sp, 0, k, EP - CAP)
                    win = item(sp, 1, k, NW - 1)
                    node = win * WN
                    tops = max_d[:, bass.ds(win * WH, WH)]
                    sp.dma_start(rec_sl[:, 0, 0, :], edge_rows(rec_d, off)).then_inc(s("ga_loaded"), 16)
                    sp.dma_start(er_sl[:, 0, 0:WN * H], er_d[bass.ds(node, WN), :].rearrange("n h -> (n h)").unsqueeze(0).to_broadcast([P, WN * H])).then_inc(s("ga_loaded"), 16)
                    sp.dma_start(top_o[:, 0, :], tops.to_broadcast([P, WH])).then_inc(s("ga_loaded"), 16)
                    sp.dma_start(ov_agg.rearrange("p (h n) -> p h n", h=H), agg_window(node)).then_inc(s("ga_loaded"), 16)
                    sp.wait_ge(s("ga_added"), ga_base(sp, layer) + k + 1)
                    sp.dma_start(agg_window(node), ov_agg.rearrange("p (h n) -> p h n", h=H)).then_inc(s("ga_stored"), 16)
                    sp.dma_start(tops, top_o[0:1, 1, :]).then_inc(s("ga_stored"), 16)
                    wait_reg(sp, s("ga_stored"), (ga_base(sp, layer) + k) * 32 + 32)

        def ga_base(eng, layer):
            return eng.value_load(n_items, min_val=0, max_val=NW) if layer else 0

        def gat_sync(sp, layer):
            for i in rounds(sp, B // NG, layer == 0):
                for u in range(NG):
                    sp.wait_ge(agg_used[u], i + layer * (B // NG))
                    sp.dma_start(agg_sl[:, u], agg_d[:, :, bass.ds(i * (NG * BN) + u * BN, BN)]).then_inc(agg_loaded[u], 16)

        def conv_weights_sync(sp):
            sp.wait_ge(s("gat_done"), 2)
            q = s("conv_w")
            for i in range(3):
                sp.dma_start(wconv[:, i, :], a[f"L1_gnn_W{i}"]).then_inc(q, 16)
            for i in range(2):
                sp.dma_start(wconv[:, 3 + i, :], a[f"L3_gnn_W{i + 1}"]).then_inc(q, 16)
            sp.dma_start(wf, a["L1_gnn_Wf"].rearrange("(i k) f -> k i f", k=F)).then_inc(q, 16)
            for i, n in enumerate(("L1_gnn_b0", "L1_gnn_b1", "L1_gnn_b2", "L1_gnn_bf", "L3_gnn_b1", "L3_gnn_b2", "L3_gnn_bias1", "L3_gnn_bias2",
                                   "L3_gnn_g1", "L3_gnn_beta1", "L3_gnn_g2", "L3_gnn_beta2")):
                sp.dma_start(bconv[:, i, :], a[n].unsqueeze(0).to_broadcast([NT, F])).then_inc(q, 16)
            for i in range(2):
                sp.dma_start(we[0:ED, 1 + i * F:1 + (i + 1) * F], a[f"L3_gnn_We{i + 1}"]).then_inc(q, 16)
                sp.dma_start(bsum[ED:ED + 1, 0, i * F:(i + 1) * F], a[f"L3_gnn_b{i + 1}"].unsqueeze(0)).then_inc(q, 16)
                sp.dma_start(bsum[ED:ED + 1, 1, i * F:(i + 1) * F], a[f"L3_gnn_be{i + 1}"].unsqueeze(0)).then_inc(q, 16)

        CONV_W = 16 * (5 + 1 + 12 + 6)

        def conv_sync(sp, n, adj):
            for b in rounds(sp, B, n == 0):
                for q in range(NQ):
                    sp.wait_ge(cv_used[q], b + n * B)
                    sp.dma_start(adj_sl[:, q], adj[bass.ds(b * NG, NG), :, q * QT:(q + 1) * QT, :].rearrange("g p t n -> p g (t n)")).then_inc(cv_loaded[q], 16)

        @block.sync
        def _(sp):
            logit_weights_sync(sp)
            prep_sync(sp)
            gat_weights_sync(sp, 0)
            table_sync(sp, 0)
            win_sync(sp, 0)
            adj_overflow_sync(sp)
            win_overflow_sync(sp, 0)
            gat_sync(sp, 0)
            gat_weights_sync(sp, 1)
            table_sync(sp, 1)
            win_sync(sp, 1)
            win_overflow_sync(sp, 1)
            gat_sync(sp, 1)
            conv_weights_sync(sp)
            for n, adj in enumerate((adj_w_d, adj_w_d, adj_w_d, adj_c_d, adj_c_d, adj_c_d)):
                if n == 0:
                    sp.wait_ge(s("pn_evac"), 1)
                conv_sync(sp, n, adj)
            sp.wait_ge(s("cv_done"), 7)
            sp.dma_start(nodes(a["out"]), x_sb).then_inc(s("out_stored"), 16)
            sp.wait_ge(s("out_stored"), 16)

        def consts_pool(pool):
            g = nc.gpsimd
            g.iota(iota_wn, [[1, WN]], base=0, channel_multiplier=0, allow_small_or_imprecise_dtypes=True)
            g.iota(iota_key, [[1, T * WN]], base=0, channel_multiplier=0, allow_small_or_imprecise_dtypes=True)
            g.iota(iota_lo, [[1, P]], base=0, channel_multiplier=0, allow_small_or_imprecise_dtypes=True)
            g.iota(win_node, [[WN, NW]], base=0, channel_multiplier=0, allow_small_or_imprecise_dtypes=True)
            g.iota(win_key, [[KEY, NW]], base=0, channel_multiplier=0, allow_small_or_imprecise_dtypes=True)
            g.memset(ones, 1.0)
            g.memset(ident, 0.0).then_inc(s("pool_const"), 1)
            g.memset(flip, 0.0).then_inc(s("pool_const"), 1)
            pool.wait_ge(s("pool_const"), 2)
            g.affine_select(out=ident, in_=ident, compare_op=ALU.not_equal, fill=1.0, base=0, pattern=[[-1, P]], channel_multiplier=1).then_inc(s("consts_made"), 1)
            g.affine_select(out=flip, in_=flip, compare_op=ALU.not_equal, fill=1.0, base=1 - P, pattern=[[1, P]], channel_multiplier=1).then_inc(s("consts_made"), 1)
            pool.wait_ge(s("rec_stored"), 16)
            g.iota(thr, [[WN * NT, 5]], base=0, channel_multiplier=WN, allow_small_or_imprecise_dtypes=True)
            g.iota(kid, [[NT, 5]], base=0, channel_multiplier=1, allow_small_or_imprecise_dtypes=True)
            g.iota(iota_nw, [[1, NW]], base=0, channel_multiplier=0, allow_small_or_imprecise_dtypes=True)
            g.memset(onesw, 1.0).then_inc(s("consts_made"), 1)
            pool.wait_ge(s("ptr_rows_wanted"), 1)
            for c in range(5):
                g.indirect_dma_start(rowd[:, c, :], None, a["dst"], bass.IndirectOffsetOnAxis(ap=rowi[:, c:c + 1], axis=0)).then_inc(s("ptr_rows_here"), 16)

        def win_pool(pool, layer):
            g_ = nc.gpsimd
            pool.wait_ge(s("table_stored"), 16 * (layer + 1))
            for b in rounds(pool, B, layer == 0):
                for g in range(NG):
                    pool.wait_ge(rec_loaded[g], b * LOADS + LOADS * (layer * B + 1))
                    wait_reg(pool, win_used[g], b + layer * B)
                    for w in range(WG):
                        for c in range(CH):
                            g_.indirect_dma_start(rows_sl[:, g, w, c, :], None, table_d, bass.IndirectOffsetOnAxis(
                                ap=rec_sl[:, g, w, (c + 1) * REC - 1:(c + 1) * REC].bitcast(I32), axis=0)).then_inc(gathered[g], 16)

        def win_overflow_pool(pool, layer):
            count = pool.value_load(n_items, min_val=0, max_val=NW)
            with pool.If(count > 0):
                with pool.Fori(0, count) as k:
                    kk = ga_base(pool, layer) + k
                    wait_reg(pool, s("ga_loaded"), kk * 64 + 64)
                    for c in range(CH):
                        nc.gpsimd.indirect_dma_start(rows_sl[:, 0, 0, c, :], None, table_d, bass.IndirectOffsetOnAxis(
                            ap=rec_sl[:, 0, 0, (c + 1) * REC - 1:(c + 1) * REC].bitcast(I32), axis=0)).then_inc(s("ga_rows"), 16)

        @block.gpsimd
        def _(pool):
            consts_pool(pool)
            pool.wait_ge(s("items_back"), 16)
            for layer in range(2):
                win_pool(pool, layer)
                win_overflow_pool(pool, layer)

        v = nc.vector

        def prep_vector(d):
            d.wait_ge(s("edges_loaded"), 48)
            hi, dst, ew = tmp[3], tmp[2], tmp[1]
            srcf, t0 = rec_all[:, :, 0], rec_all[:, :, 1]
            v.tensor_copy(srcf, src_idx)
            v.tensor_copy(rec_all[:, :, 6].bitcast(I32), src_idx)
            v.tensor_copy(dst, tmp[0].bitcast(I32))
            v.tensor_copy(hi_bf, ew)
            d.drain()
            v.tensor_scalar(hi, srcf, 1.0 / NT, 0.5 / NT - 0.5, ALU.mult, ALU.add)
            v.tensor_scalar(tmp[0], dst, 1.0 / WN, 0.5 / WN - 0.5, ALU.mult, ALU.add)
            v.tensor_copy(rec_all[:, :, 5], dst)
            v.tensor_copy(rec_all[:, :, 2], hi_bf)
            d.drain()
            v.tensor_scalar(hi, hi, RND, None, ALU.add)
            v.tensor_scalar(tmp[0], tmp[0], RND, None, ALU.add)
            v.tensor_tensor(ew, ew, rec_all[:, :, 2], ALU.subtract)
            d.drain()
            v.tensor_scalar(hi, hi, -RND, None, ALU.add)
            v.tensor_scalar(tmp[0], tmp[0], -RND, None, ALU.add)
            v.tensor_copy(hi_bf, ew)
            d.drain()
            v.scalar_tensor_tensor(t0, hi, -float(NT), srcf, ALU.mult, ALU.add)
            v.tensor_copy(rec_all[:, :, 3], hi_bf)
            d.drain()
            v.scalar_tensor_tensor(srcf, tmp[0], float(KEY - WN), dst, ALU.mult, ALU.add)
            v.tensor_tensor(rec_all[:, :, 4], ew, rec_all[:, :, 3], ALU.subtract)
            d.drain()
            v.scalar_tensor_tensor(srcf, hi, float(WN), srcf, ALU.mult, ALU.add)
            d.drain().then_inc(s("rec_made"), 1)

        def ptr_vector(d):
            d.wait_ge(s("heads_loaded"), 16)
            d.wait_ge(s("consts_made"), 3)
            v.tensor_copy(heads_f, heads.bitcast(I32))
            d.drain()
            for c in range(5):
                v.tensor_scalar(junk, heads_f, thr[:, c:c + 1], None, ALU.is_lt, ALU.add, accum_out=cnt[:, c:c + 1])
                d.drain()
            v.tensor_scalar(cnt, cnt, -1.0, 0.0, ALU.add, ALU.max)
            d.drain()
            v.tensor_copy(rowi, cnt).then_inc(s("ptr_rows_wanted"), 1)
            d.wait_ge(s("ptr_rows_here"), 80)
            v.tensor_copy(rowf, rowd)
            d.drain()
            for c in range(5):
                v.tensor_scalar(junk[:, 0:P], rowf[:, c, :], thr[:, c:c + 1], None, ALU.is_lt, ALU.add, accum_out=cnt2[:, c:c + 1])
                d.drain()
            v.scalar_tensor_tensor(ptr_f, cnt, float(P), cnt2, ALU.mult, ALU.add)
            v.memset(ptr_end, float(E))
            d.drain()
            v.tensor_copy(ptr_i, ptr_f)
            d.drain().then_inc(s("ptr_made"), 1)
            d.wait_ge(s("ptr_back"), 32)
            v.tensor_tensor(nover, ptrb[:, 1:NW + 1], ptrb[:, 0:NW], ALU.subtract)
            d.drain()
            v.tensor_scalar(nover, nover, 1.0 / CAP, -0.5 / CAP - 0.5, ALU.mult, ALU.add)
            d.drain()
            v.tensor_scalar(nover, nover, RND, None, ALU.add)
            d.drain()
            v.tensor_scalar(nover, nover, -RND, 0.0, ALU.add, ALU.max)
            d.drain()
            v.tensor_tensor_scan(cum, onesw, nover, 0.0, ALU.mult, ALU.add)
            d.drain()
            v.tensor_copy(n_items, cum[0:1, NW - 1:NW])
            v.tensor_tensor(nover, cum, nover, ALU.subtract)
            for c in range(5):
                v.tensor_scalar(junk[:, 0:NW], cum, kid[:, c:c + 1], None, ALU.is_le, ALU.add, accum_out=itw[:, c:c + 1])
                d.drain()
            v.tensor_scalar(offv, nover, -float(CAP), float(CAP), ALU.mult, ALU.add)
            d.drain()
            v.tensor_tensor(offv, offv, ptrb[:, 0:NW], ALU.add)
            d.drain()
            for c in range(5):
                v.scalar_tensor_tensor(junk[:, 0:NW], iota_nw, itw[:, c:c + 1], offv, ALU.is_equal, ALU.mult, accum_out=itf[:, 0, c:c + 1])
                d.drain()
            v.scalar_tensor_tensor(itf[:, 0, :], kid, float(CAP), itf[:, 0, :], ALU.mult, ALU.add)
            v.tensor_copy(itf[:, 1, :], itw)
            v.tensor_scalar(itf[:, 2, :], itw, 1.0 / WG, 0.5 / WG - 0.5, ALU.mult, ALU.add)
            d.drain()
            v.tensor_scalar(itf[:, 2, :], itf[:, 2, :], RND, None, ALU.add)
            d.drain()
            v.tensor_scalar(itf[:, 2, :], itf[:, 2, :], -RND, None, ALU.add)
            d.drain()
            v.scalar_tensor_tensor(itf[:, 3, :], itf[:, 2, :], -float(WG), itw, ALU.mult, ALU.add)
            d.drain()
            v.tensor_scalar(itf[:, 3, :], itf[:, 3, :], float(WN), None, ALU.mult)
            d.drain()
            v.tensor_copy(iti, itf)
            d.drain().then_inc(s("items_made"), 1)

        def logit_weights_vector(d):
            v.memset(wgat, 0.0)
            d.drain()
            v.memset(wgat[F:AGG, :, F:AGG], 1.0)
            d.drain().then_inc(s("wgat_cleared"), 1)
            d.wait_ge(s("weights_loaded"), 16 * 6)
            for l in range(2):
                for i in range(2):
                    v.tensor_tensor(vprod[:, 2 * l + i, :], wv[:, l, :], alr[:, 2 * l + i, :], ALU.mult)
            d.drain()
            for l in range(2):
                for i in range(2):
                    v.tensor_reduce(vw[:, l, i * H:(i + 1) * H], vprod[:, 2 * l + i, :].rearrange("p (h f) -> p h f", h=H), AX.X, ALU.add)
            d.drain().then_inc(s("v_made"), 1)

        def table0_vector(d):
            d.wait_ge(s("x_loaded"), 16)
            v.tensor_copy(xt[:, :, 0:F], x_sb)
            v.memset(xt[:, :, F:F + 1], 1.0)
            d.wait_ge(s("el_psum"), 1)
            e = bank[7][0:NT, 0:T * 2 * H].rearrange("p (t k) -> p t k", k=2 * H)
            v.tensor_copy(xt[:, :, F + 1:XC], e[:, :, 0:H])
            v.tensor_copy(er_sb, e[:, :, H:2 * H])
            d.drain().then_inc(s("table_made"), 1)

        def one_hots(d, slot, rec, key, c):
            v.tensor_scalar(col_oh[:, slot, c, :], iota_key, key, None, ALU.is_equal)
            v.tensor_scalar(row_oh[:, slot, c, 3, :], iota_lo, rec[:, c * REC + 1:c * REC + 2], None, ALU.is_equal)

        def keys(d, par, recs, wk, wn, nw):
            r = recs.rearrange("p w (c r) -> p w c r", r=REC)
            n = nw * CH
            v.tensor_tensor(ckey[:, 0:n].rearrange("p (w c) -> p w c", c=CH), r[:, :, :, 0], bc(wk, 2, CH), ALU.subtract)
            v.tensor_tensor(cdl[:, 0:n].rearrange("p (w c) -> p w c", c=CH), r[:, :, :, 5], bc(wn, 2, CH), ALU.subtract)
            d.drain()
            v.tensor_tensor(coh[:, par, 0:n, :], bc(cdl[:, 0:n], 2, WN), bc(iota_wn, 1, n), ALU.is_equal)

        def logits(d, par, rows, er, nw):
            n = nw * CH
            e = er.rearrange("p (w j h) -> p w h j", j=WN, h=H)
            for c in range(CH):
                v.tensor_tensor(lg[:, 0:nw, c], bc(rows[:, :, c, F + 1:XC], 3, WN), e, ALU.add)
            d.drain()
            v.tensor_scalar(pen[:, 0:n, :], coh[:, par, 0:n, :], 1.0, BIG, ALU.subtract, ALU.mult)
            z = lg[:, 0:nw].rearrange("p w c h j -> p (w c h j)")
            v.scalar_tensor_tensor(z, z, 0.2, z, ALU.mult, ALU.max)
            d.drain()
            zz = lg[:, 0:nw].rearrange("p w c h j -> p (w c) h j")
            v.tensor_tensor(zz, zz, bc(pen[:, 0:n, :], 2, H), ALU.add)
            d.drain()
            m = top_e[:, 0:nw * WH].rearrange("p (w k) -> p w k", k=WH)
            lc = [lg[:, 0:nw, c].rearrange("p w h j -> p w (h j)") for c in range(CH)]
            v.scalar_tensor_tensor(m, lc[0], -0.1 * BIG, lc[1], ALU.max, ALU.max)
            d.drain()
            for c in range(2, CH):
                v.tensor_tensor(m, m, lc[c], ALU.max)
                d.drain()

        def diagonals(d, nw, topt):
            for i in range(-(-nw // TW)):
                k = min(TW, nw - i * TW) * WH
                v.tensor_reduce(top_s[0:k, i:i + 1], topt[0:k, i * P:(i + 1) * P], AX.X, ALU.max)
            d.drain()
            for i in range(-(-nw // TW)):
                k = min(TW, nw - i * TW) * WH
                v.tensor_scalar(diag[0:k, i, 0:k], ident[0:k, 0:k], top_s[0:k, i:i + 1], None, ALU.mult)
            d.drain()

        def win_vector(d, layer):
            ng = NG * B * layer
            for b in rounds(d, B, layer == 0):
                for g in range(NG):
                    par = g % 2
                    n1 = b * NG + (ng + g + 1)
                    d.wait_ge(rec_loaded[g], b * LOADS + LOADS * (layer * B + 1))
                    if layer == 0:
                        d.wait_ge(s("adj_psum"), b * (NG * WG) + max(0, (g - 1) * WG))
                    w0 = b * (NG * WG) + g * WG
                    keys(d, par, rec_sl[:, g], win_key[:, bass.ds(w0, WG)], win_node[:, bass.ds(w0, WG)], WG)
                    d.drain()

                    def adjacency(w):
                        if layer:
                            return
                        n = g * WG + w
                        d.wait_ge(s("adj_psum"), b * (NG * WG) + max(0, n - 1))
                        for c in range(CH):
                            one_hots(d, n % 2, rec_sl[:, g, w, :], ckey[:, w * CH + c:w * CH + c + 1], c)
                        d.drain().then_inc(s("onehot_made"), 1)

                    adjacency(0)
                    d.wait_ge(gathered[g], b * (16 * WG * CH) + 16 * WG * CH * (layer * B + 1))
                    logits(d, par, rows_sl[:, g], er_sl[:, g], WG)
                    d.drain().then_inc(s("top_made"), 1)
                    adjacency(1)
                    d.wait_ge(s("top_t"), n1)
                    diagonals(d, WG, bank[5])
                    d.drain().then_inc(s("diag_made"), 1)
                    adjacency(2)
                    adjacency(3)
                    d.wait_ge(s("top_psum"), n1)
                    first = (g + 1) // 2 if par == 0 else g // 2
                    d.wait_ge(top_stored[par], b * (16 * NG_PAR[par]) + 16 * (NG_PAR[par] * B * layer + first))
                    d.wait_ge(s("exp_made"), b * NG + (ng + max(0, g - 1)))
                    tp = bank[5][:, 2 * P:2 * P + WG * WH]
                    v.tensor_copy(top_row[:, par, :], tp[0:1])
                    v.tensor_tensor(gd[:, par].rearrange("p (w c) k -> p w c k", c=CH), lg.rearrange("p w c h j -> p w c (h j)"),
                                    bc(tp.rearrange("p (w k) -> p w k", k=WH), 2, CH), ALU.subtract)
                    d.drain().then_inc(s("logits_made"), 1)
                    adjacency(4)
                    d.sem_inc(rec_used[g], 1)

        def adj_overflow_vector(d):
            d.wait_ge(s("seg_evacuated"), NGR)
            count = d.value_load(n_items, min_val=0, max_val=NW)
            with d.If(count > 0):
                with d.Fori(0, count) as k:
                    win = item(d, 1, k, NW - 1)
                    d.wait_ge(s("ov_loaded"), k * 64 + 64)
                    keys(d, 0, rec_sl[:, 0, 0:1], win_key[:, bass.ds(win, 1)], win_node[:, bass.ds(win, 1)], 1)
                    for c in range(CH):
                        one_hots(d, 0, rec_sl[:, 0, 0, :], ckey[:, c:c + 1], c)
                    d.drain().then_inc(s("ov_onehot"), 1)
                    d.wait_ge(s("ov_psum"), k + 1)
                    for i in range(2):
                        v.tensor_tensor(ov_adj[:, i, :], ov_adj[:, i, :], bank[i][:, 0:T * WN], ALU.add)
                    sg = seg_t[:, bass.ds(win * WN, WN)]
                    v.tensor_tensor(sg, sg, bank[4][0:EF, 0:WN], ALU.add)
                    d.drain().then_inc(s("ov_added"), 1)

        def win_overflow_vector(d, layer):
            count = d.value_load(n_items, min_val=0, max_val=NW)
            with d.If(count > 0):
                with d.Fori(0, count) as k:
                    kk = ga_base(d, layer) + k
                    win = item(d, 1, k, NW - 1)
                    d.wait_ge(s("ga_loaded"), kk * 64 + 64)
                    d.wait_ge(s("ga_rows"), kk * (16 * CH) + 16 * CH)
                    keys(d, 0, rec_sl[:, 0, 0:1], win_key[:, bass.ds(win, 1)], win_node[:, bass.ds(win, 1)], 1)
                    d.drain()
                    logits(d, 0, rows_sl[:, 0, 0:1], er_sl[:, 0, 0:WN * H], 1)
                    d.drain().then_inc(s("ga_top"), 1)
                    d.wait_ge(s("ga_topt"), kk + 1)
                    diagonals(d, 1, bank[5])
                    d.drain().then_inc(s("ga_diag"), 1)
                    d.wait_ge(s("ga_topp"), kk + 1)
                    v.tensor_tensor(top_o[:, 1, :], top_o[:, 0, :], bank[5][:, 2 * P:2 * P + WH], ALU.max)
                    d.drain()
                    v.tensor_tensor(top_o[:, 2, :], top_o[:, 0, :], top_o[:, 1, :], ALU.subtract)
                    v.tensor_tensor(gd[:, 0, 0:CH, :], lg[:, 0].rearrange("p c h j -> p c (h j)"), bc(top_o[:, 1, :], 1, CH), ALU.subtract)
                    d.drain().then_inc(s("ga_logits"), 1)
                    d.wait_ge(s("ga_exp"), kk + 1)
                    v.tensor_tensor(ov_agg, ov_agg, top_o[0:AGG, 2, :], ALU.mult)
                    d.drain()
                    d.wait_ge(s("ga_psum"), kk + 1)
                    v.tensor_tensor(ov_agg, ov_agg, bank[6][0:AGG, 0:WH], ALU.add)
                    d.drain().then_inc(s("ga_added"), 1)

        def gat_vector(d, layer):
            base = layer * B
            for i in rounds(d, B // NG, layer == 0):
                for u in range(NG):
                    n = i * NG + (u + base)
                    t0 = (i * NG + u) * 2
                    d.wait_ge(s("gat_psum"), n + 1)
                    for half in range(2):
                        y = bank[2 + half][0:NT, 0:H * AGG].rearrange("p (h f) -> p h f", h=H)
                        v.tensor_scalar(srec[:, half, :], y[:, :, F], 1e-30, None, ALU.max)
                    d.drain().then_inc(agg_used[u], 1)
                    v.reciprocal(flat(srec), flat(srec))
                    d.drain()
                    for half in range(2):
                        y = bank[2 + half][0:NT, 0:H * AGG].rearrange("p (h f) -> p h f", h=H)
                        v.tensor_tensor(yv[:, half, :].rearrange("p (h f) -> p h f", h=H), y[:, :, 0:F], bc(srec[:, half, :], 2, F), ALU.mult)
                    d.drain()
                    v.tensor_tensor(yv, yv, bc(gbias, 1, 2), ALU.add)
                    d.drain().then_inc(s("gat_y"), 1)
                    src = yv
                    if layer == 0:
                        d.wait_ge(s("gat_tanh"), n + 1)
                        src = yt
                    for half in range(2):
                        v.tensor_reduce(hm[:, half, :], src[:, half, :].rearrange("p (h f) -> p f h", h=H), AX.X, ALU.add)
                    d.drain()
                    if layer == 0:
                        v.tensor_scalar(flat(hm), flat(hm), 1.0 / H, None, ALU.mult)
                        d.drain().then_inc(s("gat_h"), 1)
                        v.tensor_copy(xt[:, bass.ds(t0, 2), 0:F], hm)
                        d.wait_ge(s("gat_v"), n + 1)
                        e = bank[5][0:NT, 0:4 * H].rearrange("p (t k) -> p t k", k=2 * H)
                        v.tensor_copy(xt[:, bass.ds(t0, 2), F + 1:XC], e[:, :, 0:H])
                        v.tensor_copy(er_sb[:, bass.ds(t0, 2), :], e[:, :, H:2 * H])
                        d.drain().then_inc(s("gat_xt"), 1)
                    else:
                        v.scalar_tensor_tensor(x_sb[:, bass.ds(t0, 2), :], hm, 1.0 / H, x_sb[:, bass.ds(t0, 2), :], ALU.mult, ALU.add)
                        d.drain()

        ln_count = [0]

        def layer_norm(d):
            ln_count[0] += 1
            v.tensor_reduce(colm[:, 0, :], x_sb, AX.X, ALU.add)
            d.drain()
            v.tensor_scalar(colm[:, 0, :], colm[:, 0, :], 1.0 / F, None, ALU.mult)
            d.drain()
            v.tensor_tensor(x_sb, x_sb, bc(colm[:, 0, :], 2, F), ALU.subtract)
            d.drain()
            v.tensor_tensor(sq, x_sb, x_sb, ALU.mult)
            d.drain()
            v.tensor_reduce(colm[:, 1, :], sq, AX.X, ALU.add)
            d.drain()
            v.tensor_scalar(colm[:, 1, :], colm[:, 1, :], 1.0 / F, LN_EPS, ALU.mult, ALU.add)
            d.drain().then_inc(s("ln_var"), 1)
            d.wait_ge(s("ln_std"), ln_count[0])
            v.reciprocal(colm[:, 3, :], colm[:, 2, :])
            d.drain()
            v.tensor_tensor(x_sb, x_sb, bc(colm[:, 3, :], 2, F), ALU.mult)
            d.drain()

        def per_node_vector(d):
            d.wait_ge(s("conv_w"), CONV_W)
            v.memset(we[0:ED, 0:1], 0.0)
            v.memset(we[ED:EF, :], 0.0)
            d.drain()
            v.tensor_copy(we[ED:EF, 0:1], ident[ED:EF, EF - 1:EF])
            v.tensor_tensor(we[ED:ED + 1, 1:QC], bsum[ED:ED + 1, 0, :], bsum[ED:ED + 1, 1, :], ALU.add)
            d.drain().then_inc(s("we_made"), 1)
            for b in rounds(d, B, False):
                d.wait_ge(s("pn_psum"), b + 1)
                v.tensor_copy(per_node[:, bass.ds(b * 2, 2), :], bank[0][0:NT, 0:2 * QC].rearrange("p (t q) -> p t q", q=QC)).then_inc(s("pn_evac"), 1)
            d.wait_ge(s("pn_evac"), B)
            v.tensor_scalar(colm[:, 3, :], per_node[:, :, 0], 1.0, None, ALU.add)
            d.drain()
            v.tensor_scalar(colm[:, 0, :], colm[:, 3, :], 0.0, None, ALU.is_gt)
            v.tensor_scalar(colm[:, 1, :], colm[:, 3, :], 1e-30, None, ALU.max)
            d.drain().then_inc(s("ln_var"), 1)
            ln_count[0] += 1
            d.wait_ge(s("ln_std"), ln_count[0])
            v.reciprocal(colm[:, 3, :], colm[:, 2, :])
            d.drain()
            v.tensor_tensor(dinv, colm[:, 3, :], colm[:, 0, :], ALU.mult)
            d.drain()

        def conv_vector(d, n, x_in, x_out):
            for b in rounds(d, B, n == 0):
                k = b + n * B
                t2 = bass.ds(b * 2, 2)
                d.wait_ge(s("cv_agg"), k)
                v.tensor_copy(xd[:, 0], x_in[:, t2, :])
                if n == 0:
                    d.wait_ge(s("cv_done"), 1)
                    v.tensor_copy(xd[:, 1], x_sb[:, t2, :])
                d.drain().then_inc(s("cv_self"), 1)
                d.wait_ge(s("cv_y"), k + 1)
                y = bank[2][0:NT, 0:2 * F].rearrange("p (t f) -> p t f", f=F)
                if n < 3:
                    dv = bc(dinv[:, t2], 2, F)
                    v.tensor_tensor(yc[:, 0], y, dv, ALU.mult)
                    d.drain()
                    v.tensor_tensor(yc[:, 0], yc[:, 0], bc(bconv[:, n, :], 1, 2), ALU.add)
                    d.drain()
                    v.tensor_scalar(flat(yc[:, 0]), flat(yc[:, 0]), 0.0, None, ALU.max)
                    d.drain().then_inc(s("cv_ev"), 1)
                    if n < 2:
                        v.tensor_tensor(x_out[:, t2, :], yc[:, 0], dv, ALU.mult)
                    d.wait_ge(s("cv_f"), k + 1)
                    f = bank[5][0:NT, 0:2 * F].rearrange("p (t f) -> p t f", f=F)
                    if n == 0:
                        v.tensor_copy(facc[:, t2, :], f)
                    else:
                        v.tensor_tensor(facc[:, t2, :], facc[:, t2, :], f, ALU.add)
                    d.drain()
                elif n == 3:
                    v.tensor_copy(x_out[:, t2, :], y)
                    d.drain().then_inc(s("cv_ev"), 1)
                else:
                    l = n - 4
                    v.tensor_tensor(yc[:, 0], y, per_node[:, t2, 1 + l * F:1 + (l + 1) * F], ALU.add)
                    d.drain().then_inc(s("cv_ev"), 1)
                    v.tensor_tensor(yc[:, 0], yc[:, 0], bc(bconv[:, 4 + l, :], 1, 2), ALU.add)
                    d.drain()
                    v.tensor_scalar(flat(yc[:, 0]), flat(yc[:, 0]), 0.0, None, ALU.max)
                    d.drain()
                    v.tensor_tensor(x_out[:, t2, :], yc[:, 0], bc(bconv[:, 6 + l, :], 1, 2), ALU.add)
                    d.drain()

        def batch_norm(d, z, l):
            v.tensor_reduce(stat[:, 0, :], z.rearrange("p t f -> p f t"), AX.X, ALU.add)
            d.drain().then_inc(s("bn_sum"), 1)
            d.wait_ge(s("bn_mean"), 2 * l + 1)
            v.tensor_scalar(stat[:, 1, :], bank[6][0:NT, 0:F], 1.0 / N, None, ALU.mult)
            d.drain()
            v.tensor_tensor(z, z, bc(stat[:, 1, :], 1, T), ALU.subtract)
            d.drain()
            v.tensor_tensor(sq, z, z, ALU.mult)
            d.drain()
            v.tensor_reduce(stat[:, 0, :], sq.rearrange("p t f -> p f t"), AX.X, ALU.add)
            d.drain().then_inc(s("bn_sum"), 1)
            d.wait_ge(s("bn_mean"), 2 * l + 2)
            v.tensor_scalar(stat[:, 2, :], bank[6][0:NT, 0:F], 1.0 / N, BN_EPS, ALU.mult, ALU.add)
            d.drain().then_inc(s("bn_var"), 1)
            d.wait_ge(s("bn_std"), l + 1)
            v.reciprocal(stat[:, 4, :], stat[:, 3, :])
            d.drain()
            v.tensor_tensor(stat[:, 4, :], stat[:, 4, :], bconv[:, 8 + 2 * l, :], ALU.mult)
            d.drain()
            v.tensor_tensor(z, z, bc(stat[:, 4, :], 1, T), ALU.mult)
            d.drain()
            v.tensor_tensor(z, z, bc(bconv[:, 9 + 2 * l, :], 1, T), ALU.add)
            d.drain()

        @block.vector
        def _(d):
            prep_vector(d)
            ptr_vector(d)
            logit_weights_vector(d)
            table0_vector(d)
            d.wait_ge(s("items_back"), 16)
            win_vector(d, 0)
            adj_overflow_vector(d)
            win_overflow_vector(d, 0)
            gat_vector(d, 0)
            d.drain().then_inc(s("table_made"), 1)
            d.sem_inc(s("gat_done"), 1)
            win_vector(d, 1)
            win_overflow_vector(d, 1)
            gat_vector(d, 1)
            d.drain().then_inc(s("gat_done"), 1)
            layer_norm(d)
            per_node_vector(d)
            v.tensor_tensor(xin, x_sb, bc(dinv, 2, F), ALU.mult)
            d.drain().then_inc(s("cv_done"), 1)
            conv_vector(d, 0, xin, hout)
            d.drain().then_inc(s("cv_done"), 1)
            conv_vector(d, 1, hout, xin)
            d.drain().then_inc(s("cv_done"), 1)
            conv_vector(d, 2, xin, None)
            v.tensor_tensor(x_sb, x_sb, facc, ALU.add)
            d.drain()
            v.tensor_tensor(x_sb, x_sb, bc(bconv[:, 3, :], 1, T), ALU.add)
            d.drain()
            layer_norm(d)
            d.drain().then_inc(s("cv_done"), 1)
            conv_vector(d, 3, x_sb, hout)
            v.tensor_copy(x_sb, hout)
            d.drain()
            layer_norm(d)
            d.drain().then_inc(s("cv_done"), 1)
            conv_vector(d, 4, x_sb, hout)
            batch_norm(d, hout, 0)
            d.drain().then_inc(s("cv_done"), 1)
            conv_vector(d, 5, hout, xin)
            batch_norm(d, xin, 1)
            v.tensor_tensor(x_sb, x_sb, xin, ALU.add)
            d.drain()
            layer_norm(d)
            d.drain().then_inc(s("cv_done"), 1)

        mm = nc.tensor.matmul

        def prep_tensor(pe):
            pe.wait_ge(s("xT_loaded"), 16)
            pe.wait_ge(s("v_made"), 1)
            for t in range(T):
                last = mm(bank[7][0:NT, t * 2 * H:(t + 1) * 2 * H], lhsT=xT_sb[:, t * NT:(t + 1) * NT], rhs=vw[:, 0, :], start=True, stop=True)
            last.then_inc(s("el_psum"), 1)

        def adj_window_mms(slot, g, w, wb, cb, seg, oh, seg_done=None):
            for c in range(CH):
                last = mm(seg, lhsT=ef_sl[:, g, w, c * EF:(c + 1) * EF], rhs=oh[:, c, :], start=(c == 0), stop=(c == CH - 1))
            if seg_done is not None:
                last.then_inc(seg_done, 1)
            for c in range(CH):
                for i in range(3):
                    mm(wb, lhsT=row_oh[:, slot, c, i, :], rhs=col_oh[:, slot, c, :], start=(c == 0 and i == 0), stop=(c == CH - 1 and i == 2))
            for c in range(CH):
                last = mm(cb, lhsT=row_oh[:, slot, c, 3, :], rhs=col_oh[:, slot, c, :], start=(c == 0), stop=(c == CH - 1))
            return last

        def top_mms(nw):
            for i in range(-(-nw // TW)):
                k = min(TW, nw - i * TW) * WH
                last = mm(bank[5][0:k, i * P:(i + 1) * P], lhsT=top_e[:, i * TW * WH:i * TW * WH + k], rhs=ident, start=True, stop=True)
            return last

        def diag_mms(nw):
            for i in range(-(-nw // TW)):
                k = min(TW, nw - i * TW) * WH
                last = mm(bank[5][:, 2 * P + i * TW * WH:2 * P + i * TW * WH + k], lhsT=ones[0:k, :], rhs=diag[0:k, i, 0:k], start=True, stop=True)
            return last

        def agg_mms(out, g, w, par):
            for c in range(CH):
                last = mm(out, lhsT=rows_sl[:, g, w, c, 0:AGG], rhs=grh[:, par, w * CH + c, :], start=(c == 0), stop=(c == CH - 1))
            return last

        def win_tensor(pe, layer):
            ng = NG * B * layer

            def aggregate(n, g):
                pe.wait_ge(s("exp_made"), n + 1)
                pe.wait_ge(s("win_evac"), n)
                for w in range(WG):
                    last = agg_mms(bank[6][0:AGG, w * WH:(w + 1) * WH], g, w, g % 2)
                last.then_inc(s("win_psum"), 1)

            for b in rounds(pe, B):
                for g in range(NG):
                    n1 = b * NG + (ng + g + 1)

                    def adjacency(w):
                        if layer:
                            return
                        n = g * WG + w
                        if w == 0:
                            pe.wait_ge(adj_loaded[g], b * (16 * WG) + 16 * WG)
                            pe.wait_ge(s("seg_evacuated"), b * NG + max(0, g - 1))
                        pe.wait_ge(s("adj_evacuated"), b * (NG * WG) + max(0, n - 1))
                        pe.wait_ge(s("onehot_made"), b * (NG * WG) + (n + 1))
                        pe.wait_ge(s("rows_weighted"), b * (NG * WG) + (n + 1))
                        pair = 2 * (n % 2)
                        seg_bank = bank[4 if g % 2 == 0 else 7]
                        adj_window_mms(n % 2, g, w, bank[pair][:, 0:T * WN], bank[pair + 1][:, 0:T * WN],
                                       seg_bank[0:EF, w * WN:(w + 1) * WN], coh[:, g % 2, w * CH:(w + 1) * CH, :],
                                       adj_used[g] if w == WG - 1 else None).then_inc(s("adj_psum"), 1)

                    if not (isinstance(b, int) and g == 0):
                        aggregate(n1 - 2, (g - 1) % NG)
                    adjacency(0)
                    pe.wait_ge(s("top_made"), n1)
                    top_mms(WG).then_inc(s("top_t"), 1)
                    adjacency(1)
                    adjacency(2)
                    pe.wait_ge(s("diag_made"), n1)
                    diag_mms(WG).then_inc(s("top_psum"), 1)
                    adjacency(3)
                    adjacency(4)
            aggregate(ng + NGR - 1, NG - 1)

        def adj_overflow_tensor(pe):
            pe.wait_ge(s("adj_evacuated"), NW)
            pe.wait_ge(s("seg_evacuated"), NGR)
            count = pe.value_load(n_items, min_val=0, max_val=NW)
            with pe.If(count > 0):
                with pe.Fori(0, count) as k:
                    pe.wait_ge(s("ov_loaded"), k * 64 + 64)
                    pe.wait_ge(s("ov_weighted"), k + 1)
                    adj_window_mms(0, 0, 0, bank[0][:, 0:T * WN], bank[1][:, 0:T * WN], bank[4][0:EF, 0:WN], coh[:, 0, 0:CH, :]).then_inc(s("ov_psum"), 1)

        def win_overflow_tensor(pe, layer):
            pe.wait_ge(s("win_evac"), NGR * (layer + 1))
            count = pe.value_load(n_items, min_val=0, max_val=NW)
            with pe.If(count > 0):
                with pe.Fori(0, count) as k:
                    kk = ga_base(pe, layer) + k
                    pe.wait_ge(s("ga_top"), kk + 1)
                    top_mms(1).then_inc(s("ga_topt"), 1)
                    pe.wait_ge(s("ga_diag"), kk + 1)
                    diag_mms(1).then_inc(s("ga_topp"), 1)
                    pe.wait_ge(s("ga_exp"), kk + 1)
                    agg_mms(bank[6][0:AGG, 0:WH], 0, 0, 0).then_inc(s("ga_psum"), 1)

        def gat_tensor(pe, layer):
            pe.wait_ge(s("wgat_loaded"), 32 * (layer + 1))
            base = layer * B
            for i in rounds(pe, B // NG, layer == 0):
                for u in range(NG):
                    n = i * NG + (u + base)
                    pe.wait_ge(agg_loaded[u], i * 16 + 16 * (layer * (B // NG) + 1))
                    pe.wait_ge(s("gat_y"), n)
                    for half in range(2):
                        for h in range(H):
                            last = mm(bank[2 + half][0:NT, h * AGG:(h + 1) * AGG], lhsT=agg_sl[:, u, h, half * NT:(half + 1) * NT], rhs=wgat[:, h, :], start=True, stop=True)
                    last.then_inc(s("gat_psum"), 1)
                    if layer == 0:
                        pe.wait_ge(s("gat_h"), n + 1)
                        for half in range(2):
                            last = mm(bank[4][0:F, half * NT:(half + 1) * NT], lhsT=hm[:, half, :], rhs=ident[0:NT, 0:NT], start=True, stop=True)
                        last.then_inc(s("gat_hT"), 1)
                        pe.wait_ge(s("gat_hTc"), n + 1)
                        pe.wait_ge(s("gat_xt"), n)
                        for half in range(2):
                            last = mm(bank[5][0:NT, half * 2 * H:(half + 1) * 2 * H], lhsT=hT[:, half * NT:(half + 1) * NT], rhs=vw[:, 1, :], start=True, stop=True)
                        last.then_inc(s("gat_v"), 1)

        def per_node_tensor(pe):
            pe.wait_ge(s("we_made"), 1)
            for b in rounds(pe, B):
                pe.wait_ge(s("pn_copied"), b + 1)
                pe.wait_ge(s("pn_evac"), b)
                for half in range(2):
                    last = mm(bank[0][0:NT, half * QC:(half + 1) * QC], lhsT=segb[:, half * NT:(half + 1) * NT], rhs=we, start=True, stop=True)
                last.then_inc(s("pn_psum"), 1)

        def conv_tensor(pe, n, x_in):
            w = (wconv[:, n, :] if n < 3 else ident[0:F, 0:F] if n == 3 else wconv[:, n - 1, :])
            pe.wait_ge(s("cv_done"), n + 1)
            for b in rounds(pe, B, False):
                k = b + n * B
                agg = bank[0][0:F, 0:BN]
                for q in range(NQ):
                    pe.wait_ge(cv_loaded[q], b * 16 + 16 * (n * B + 1))
                    for t in range(QT):
                        last = mm(agg.rearrange("p (g n) -> p g n", n=GN), lhsT=x_in[:, q * QT + t, :], rhs=adj_sl[0:NT, q, :, t * GN:(t + 1) * GN],
                                  start=(q == 0 and t == 0), stop=False)
                    last.then_inc(cv_used[q], 1)
                pe.wait_ge(s("cv_self"), k + 1)
                for half in range(2):
                    last = mm(bank[0][0:F, half * NT:(half + 1) * NT], lhsT=xd[:, 0, half, :], rhs=ident[0:NT, 0:NT], start=False, stop=(half == 1))
                last.then_inc(s("cv_agg"), 1)
                pe.wait_ge(s("cv_aggc"), k + 1)
                for half in range(2):
                    last = mm(bank[2][0:NT, half * F:(half + 1) * F], lhsT=aggs[:, half * NT:(half + 1) * NT], rhs=w, start=True, stop=True)
                last.then_inc(s("cv_y"), 1)
                pe.wait_ge(s("cv_ev"), k + 1)
                if n < 3:
                    for i in range(2 if n == 0 else 1):
                        for half in range(2):
                            last = mm(bank[3 + i][0:F, half * NT:(half + 1) * NT], lhsT=xd[:, 1, half, :] if i else yc[:, 0, half, :], rhs=ident[0:NT, 0:NT], start=True, stop=True)
                    last.then_inc(s("cv_yT"), 1)
                    pe.wait_ge(s("cv_yTc"), k + 1)
                    for half in range(2):
                        for i in range(2 if n == 0 else 1):
                            last = mm(bank[5][0:NT, half * F:(half + 1) * F], lhsT=yT[:, i, half * NT:(half + 1) * NT], rhs=wf[:, 0 if i else n + 1, :],
                                      start=(i == 0), stop=(n > 0 or i == 1))
                    last.then_inc(s("cv_f"), 1)

        def batch_norm_tensor(pe, l):
            for i in range(2):
                pe.wait_ge(s("bn_sum"), 2 * l + i + 1)
                mm(bank[6][0:NT, 0:F], lhsT=ones[0:NT, 0:NT], rhs=stat[:, 0, :], start=True, stop=True).then_inc(s("bn_mean"), 1)

        @block.tensor
        def _(pe):
            prep_tensor(pe)
            pe.wait_ge(s("table_made"), 1)
            for layer in range(2):
                win_tensor(pe, layer)
                if layer == 0:
                    adj_overflow_tensor(pe)
                win_overflow_tensor(pe, layer)
                gat_tensor(pe, layer)
            per_node_tensor(pe)
            for n, x_in in enumerate((xin, hout, xin, x_sb, x_sb, hout)):
                conv_tensor(pe, n, x_in)
                if n >= 4:
                    batch_norm_tensor(pe, n - 4)

        act_ = nc.scalar.activation

        def weigh_rows(slot, rec):
            for c in range(CH):
                for i in range(3):
                    last = act_(row_oh[:, slot, c, i, :], row_oh[:, slot, c, 3, :], ACT.Copy, scale=rec[:, c * REC + 2 + i:c * REC + 3 + i])
            return last

        def win_scalar(act, layer):
            ng = NG * B * layer

            def evacuate(group, g, w):
                if layer:
                    return
                n = g * WG + w
                act.wait_ge(s("adj_psum"), group * WG + (w + 1))
                for i in range(2):
                    last = act_(stage[:, g % 3, i, :, w * WN:(w + 1) * WN], bank[2 * (n % 2) + i][:, 0:T * WN].rearrange("p (t n) -> p t n", n=WN), ACT.Copy)
                last.then_inc(s("adj_evacuated"), 1)

            def finish(b, g):
                group = b * NG + g
                n1 = group + (ng + 1)
                if layer == 0:
                    evacuate(group, g, WG - 1)
                    act_(seg_t[:, bass.ds(group * GN, GN)], bank[4 if g % 2 == 0 else 7][0:EF, 0:GN], ACT.Copy).then_inc(s("seg_evacuated"), 1)
                    act.wait_ge(s("adj_evacuated"), group * WG + WG)
                    for i, d in enumerate((adj_w_d, adj_c_d)):
                        act.dma_start(d[bass.ds(group, 1), :, :, :].rearrange("a p t n -> p (a t n)"), flat(stage[:, g % 3, i])).then_inc(adj_stored[g % 3], 16)
                act.wait_ge(win_stored[g], b * 16 + 16 * B * layer)
                act.wait_ge(s("win_psum"), n1)
                act_(gst[:, g].rearrange("p h (w j) -> p w h j", j=WN), bank[6][0:AGG, 0:WG * WH].rearrange("p (w h j) -> p w h j", w=WG, h=H), ACT.Copy).then_inc(s("win_evac"), 1)
                act.wait_ge(s("win_evac"), n1)
                act.sem_inc(win_used[g], 1)
                act.dma_start(agg_d[:, :, bass.ds(group * GN, GN)], gst[:, g]).then_inc(win_stored[g], 16)

            for b in rounds(act, B):
                for g in range(NG):
                    n1 = b * NG + (ng + g + 1)

                    def weigh(w):
                        if layer:
                            return
                        n = g * WG + w
                        act.wait_ge(s("onehot_made"), b * (NG * WG) + (n + 1))
                        weigh_rows(n % 2, rec_sl[:, g, w, :]).then_inc(s("rows_weighted"), 1)

                    weigh(0)
                    if not (isinstance(b, int) and g == 0):
                        finish(b if g else b - 1, (g - 1) % NG)
                    if layer == 0:
                        act.wait_ge(adj_stored[g % 3], b * (32 * (2, 2, 1)[g % 3]) + 32 * (g >= 3))
                    weigh(1)
                    evacuate(b * NG + g, g, 0)
                    weigh(2)
                    evacuate(b * NG + g, g, 1)
                    weigh(3)
                    evacuate(b * NG + g, g, 2)
                    act.wait_ge(s("logits_made"), n1)
                    act.wait_ge(s("win_psum"), b * NG + (ng + max(0, g - 1)))
                    act_(flat(grh[:, g % 2]), flat(gd[:, g % 2]), ACT.Exp).then_inc(s("exp_made"), 1)
                    act.dma_start(max_d[:, bass.ds((b * NG + g) * (WG * WH), WG * WH)], top_row[:, g % 2, :]).then_inc(top_stored[g % 2], 16)
                    weigh(4)
                    evacuate(b * NG + g, g, 3)
            finish(B - 1, NG - 1)

        def adj_overflow_scalar(act):
            count = act.value_load(n_items, min_val=0, max_val=NW)
            with act.If(count > 0):
                with act.Fori(0, count) as k:
                    act.wait_ge(s("ov_onehot"), k + 1)
                    weigh_rows(0, rec_sl[:, 0, 0, :]).then_inc(s("ov_weighted"), 1)

        def win_overflow_scalar(act, layer):
            count = act.value_load(n_items, min_val=0, max_val=NW)
            with act.If(count > 0):
                with act.Fori(0, count) as k:
                    kk = ga_base(act, layer) + k
                    act.wait_ge(s("ga_logits"), kk + 1)
                    act_(top_o[:, 2, :], top_o[:, 2, :], ACT.Exp)
                    act_(grh[:, 0, 0:CH, :], gd[:, 0, 0:CH, :], ACT.Exp).then_inc(s("ga_exp"), 1)

        def gat_scalar(act, layer):
            base = layer * B
            if layer:
                return
            for n in rounds(act, B, False):
                act.wait_ge(s("gat_y"), n + 1)
                act_(flat(yt), flat(yv), ACT.Tanh).then_inc(s("gat_tanh"), 1)
                act.wait_ge(s("gat_hT"), n + 1)
                act_(hT, bank[4][0:F, 0:BN], ACT.Copy).then_inc(s("gat_hTc"), 1)

        std_count = [0]

        def std_scalar(act):
            std_count[0] += 1
            act.wait_ge(s("ln_var"), std_count[0])
            act_(colm[:, 2, :], colm[:, 1, :], ACT.Sqrt).then_inc(s("ln_std"), 1)

        def per_node_scalar(act):
            act.wait_ge(s("we_made"), 1)
            for b in rounds(act, B):
                act.wait_ge(s("pn_psum"), b)
                act_(segb, seg_t[:, bass.ds(b * BN, BN)], ACT.Copy).then_inc(s("pn_copied"), 1)

        def conv_scalar(act, n):
            for b in rounds(act, B, False):
                k = b + n * B
                act.wait_ge(s("cv_agg"), k + 1)
                act_(aggs, bank[0][0:F, 0:BN], ACT.Copy).then_inc(s("cv_aggc"), 1)
                if n < 3:
                    act.wait_ge(s("cv_yT"), k + 1)
                    for i in range(2 if n == 0 else 1):
                        last = act_(yT[:, i, :], bank[3 + i][0:F, 0:BN], ACT.Copy)
                    last.then_inc(s("cv_yTc"), 1)

        @block.scalar
        def _(act):
            act.wait_ge(s("items_back"), 16)
            act.wait_ge(s("el_psum"), 1)
            for layer in range(2):
                win_scalar(act, layer)
                if layer == 0:
                    adj_overflow_scalar(act)
                win_overflow_scalar(act, layer)
                gat_scalar(act, layer)
            std_scalar(act)
            per_node_scalar(act)
            std_scalar(act)
            for n in range(6):
                conv_scalar(act, n)
                if n in (2, 3):
                    std_scalar(act)
                if n >= 4:
                    act.wait_ge(s("bn_var"), n - 3)
                    act_(stat[:, 3, :], stat[:, 2, :], ACT.Sqrt).then_inc(s("bn_std"), 1)
            std_scalar(act)


_OUT = ((N, F), "float32")


def kernel(**inputs):
    import concourse.bacc as bacc
    from concourse.bass_utils import run_bass_kernel_spmd as run

    nc = bacc.Bacc("TRN2", target_bir_lowering=False, num_devices=1)
    g = {k: np.ascontiguousarray(v) for k, v in inputs.items()}
    pad = EP - E
    src = np.concatenate([g.pop("src"), np.zeros(pad, np.int32)])
    dst = np.concatenate([g.pop("dst"), np.full(pad, N + 22, np.int32)])
    ew = g.pop("edge_weight")
    ea = g.pop("edge_attr_32")
    feats = np.zeros((EP, EF), np.float32)
    feats[:E, 0:ED] = ea
    feats[:E, ED] = 1.0
    feats[:E, ED + 1] = ew
    g["src"] = src.reshape(P, EC)
    g["dst"] = dst.reshape(EC, P)
    g["dst_heads"] = np.ascontiguousarray(dst.reshape(EC, P)[:, 0]).reshape(1, EC)
    g["edge_weight"] = np.concatenate([ew, np.zeros(pad, np.float32)]).reshape(P, EC)
    g["edge_features"] = feats
    g["xT"] = np.ascontiguousarray(g["x"].T)
    arrays, aps = {}, {}
    for k, v in g.items():
        arrays[f"in_{k}"] = v
        aps[k] = nc.dram_tensor(f"in_{k}", v.shape, mybir.dt.from_np(v.dtype), kind="ExternalInput").ap()
    aps["out"] = nc.dram_tensor("out_0", _OUT[0], F32, kind="ExternalOutput").ap()
    build(nc, aps)
    r = run(nc, [arrays], core_ids=[0])
    return r.results[0]["out_0"]
```

```python
import numpy as np
import concourse.bass as bass
from concourse import mybir
from contextlib import ExitStack

F32 = mybir.dt.float32
I32 = mybir.dt.int32
F16 = mybir.dt.float16
BF16 = mybir.dt.bfloat16
ALU = mybir.AluOpType
ACT = mybir.ActivationFunctionType
AX = mybir.AxisListType

N = 6250
E = 200000
F = 64
H = 4
ED = 32
P = 128

EC = 1568
EP = P * EC

WN = 10
WG = 5
NG = 5
GN = WN * WG
BN = GN * NG
NT = BN // 2
T = N // NT
B = N // BN
NW = N // WN
NGR = N // GN
CH = 3
CAP = CH * P
WH = H * WN
TW = 3
KEY = 512
REC = 7
XC = F + 1 + H
EF = ED + 2
AGG = F + 1
QC = 1 + 2 * F
GS = 3
OHS = 5
NQ = 5
QT = T // NQ
KILO = 1024
BIG = 1.0e30
RND = 12582912.0
LN_EPS = 1e-05
BN_EPS = 1e-05


def build(nc, a):
    ctx = ExitStack()
    with ctx:
        def dram(name, shape, dt=F32):
            return nc.dram_tensor(name, shape, dt, kind="Internal").ap()

        def sem(name):
            return ctx.enter_context(nc.semaphore(name))

        rec_d = dram("rec_d", [EP, REC])
        max_d = dram("max_d", [1, NW * WH])
        table_d = dram("table_d", [N, XC])
        er_d = dram("er_d", [N, H])
        agg_d = dram("agg_d", [AGG, H, N])
        adj_w_d = dram("adj_w_d", [NGR, P, T, GN])
        adj_c_d = dram("adj_c_d", [NGR, P, T, GN], F16)
        adj_k_d = dram("adj_k_d", [NGR, P, T, GN], F16)
        ptr_d = dram("ptr_d", [1, NW + 1])
        items_d = dram("items_d", [4, NW], I32)
        ptri_d = dram("ptri_d", [1, NW + 1], I32)

        SB = 53000
        arena = ctx.enter_context(nc.sbuf_tensor("arena", [P, SB], F32))
        top = [0]

        def at(off, parts, *dims):
            n = int(np.prod(dims))
            assert off + n <= SB, (off, n)
            v = arena[0:parts, off:off + n]
            if len(dims) == 1:
                return v
            names = "abcde"[:len(dims)]
            return v.rearrange(f"p ({' '.join(names)}) -> p {' '.join(names)}",
                               **{names[i]: dims[i] for i in range(1, len(dims))})

        def new(parts, *dims):
            off = top[0]
            top[0] += (int(np.prod(dims)) + 7) // 8 * 8
            return at(off, parts, *dims)

        x_sb = new(NT, T, F)
        dinv = new(NT, T)
        ident = new(P, P)
        flip = new(P, P)
        ones = new(P, P)
        iota_wn = new(P, WN)
        iota_key = new(P, T * WN // 2).bitcast(F16)
        iota_lo = new(P, P // 2).bitcast(F16)
        win_node = new(P, NW)
        win_key = new(P, NW)
        ptr_row = new(1, NW + 1).bitcast(I32)
        items = new(1, 4 * NW).bitcast(I32)
        n_items = new(1, 1).bitcast(I32)
        seg_off = top[0]
        seg_t = new(EF, N)
        fixed = top[0]

        xt = new(NT, T, XC)
        er_sb = new(NT, T, H)
        wgat = new(AGG, H, AGG)
        vw = new(F, 2, 2 * H)
        gbias = new(NT, H * F)
        rec_sl = new(P, NG, WG, CH * REC)
        ef_sl = new(P, 3, WG, CH * EF)
        rows_top = top[0]
        rows_sl = new(P, NG, WG, CH, XC)
        er_sl = new(P, NG, GN * H)
        ckey = new(P, WG * CH)
        cdl = new(P, WG * CH)
        coh = new(P, GS, WG * CH, WN)
        pen = new(P, WG * CH, WN)
        lg = new(P, WG, CH, H, WN)
        top_e = new(P, WG * WH)
        top_s = new(TW * WH, 2)
        diag = new(TW * WH, 2, TW * WH)
        top_row = new(1, 2, WG * WH)
        gd = new(P, GS, WG * CH, WH)
        grh = new(P, GS, WG * CH, WH)
        gst = new(AGG, NG, H, GN)
        top_o = new(P, 3, WH)
        ov_agg = new(AGG, WH)
        oh_top = top[0]
        col_oh = new(P, OHS, CH, T * WN // 2).bitcast(BF16)
        row_oh = new(P, OHS, CH, 4, P // 2).bitcast(BF16)
        over = top[0]
        stage_w = new(P, 3, T, GN)
        stage_c = new(P, 3, T * GN // 2).bitcast(F16).rearrange("p s (t n) -> p s t n", n=GN)
        assert top[0] <= SB, top[0]
        wv = at(oh_top, F, 2, H * F)
        alr = at(oh_top + 2 * H * F, F, 4, H * F)
        vprod = at(oh_top + 6 * H * F, F, 4, H * F)
        over_stage = over
        over = oh_top + 10 * H * F
        top[0] = over
        rec_all = new(P, EC, REC)
        tmp = [at(rows_top + i * EC, P, EC) for i in range(3)] + [new(P, EC)]
        src_idx = new(P, EC).bitcast(I32)
        hi_bf = new(P, EC // 2).bitcast(BF16)
        assert top[0] <= SB, top[0]
        heads = at(over, NT, EC)
        heads_f = at(over + EC, NT, EC)
        junk = at(over + 2 * EC, NT, EC)
        thr = at(over + 3 * EC, NT, 5)
        cnt = at(over + 3 * EC + 8, NT, 5)
        rowi = at(over + 3 * EC + 16, NT, 5).bitcast(I32)
        rowd = at(over + 3 * EC + 24, NT, 5, P).bitcast(I32)
        rowf = at(over + 3 * EC + 24 + 640, NT, 5, P)
        cnt2 = at(over + 3 * EC + 1400, NT, 5)
        ptr_f = at(over + 3 * EC + 1408, NT, 5)
        ptr_end = at(over + 3 * EC + 1416, 1, 1)
        o5 = over + 3 * EC + 1424
        ptrb = at(o5, NT, NW + 1)
        nover = at(o5 + 640, NT, NW)
        cum = at(o5 + 1280, NT, NW)
        offv = at(o5 + 1920, NT, NW)
        iota_nw = at(o5 + 2560, NT, NW)
        onesw = at(o5 + 3200, NT, NW)
        kid = at(o5 + 3840, NT, 5)
        itf = at(o5 + 3848, NT, 4, 5)
        iti = at(o5 + 3872, NT, 4, 5).bitcast(I32)
        ptr_i = at(o5 + 3896, NT, 5).bitcast(I32)
        itw = at(o5 + 3904, NT, 5)
        nif = at(o5 + 3912, 1, 2)
        o6 = o5 + 3920
        xT_sb = at(o6, F, N)
        over = over_stage
        top[0] = over
        agg_sl = new(AGG, NG, H, BN)
        srec = new(NT, 2, H)
        yv = new(NT, NG, 2, H * F)
        yt = new(NT, NG, 2, H * F)
        hm = new(NT, NG, 2, F)
        hT = new(F, BN)
        ov_w = at(over, P, T * WN)
        ov_c = at(over + 500, P, T * WN // 2).bitcast(F16)
        ov_k = at(over + 750, P, T * WN // 2).bitcast(F16)
        ov_sum = at(over + 1000, P, T * WN)
        ov_kf = at(over + 1500, P, T * WN)
        zeros = at(over + 2000, P, T * GN // 2).bitcast(F16)
        top[0] = fixed
        per_node = new(NT, T, QC)
        xin = new(NT, T, F)
        facc = new(NT, T, F)
        hout = new(NT, T, F)
        sq = new(NT, T, F)
        adj_sl = new(P, NQ, NG, QT * GN)
        adj16_sl = adj_sl.rearrange("p q g n -> p q (g n)")[:, :, 0:NG * QT * GN // 2].bitcast(F16).rearrange("p q (g n) -> p q g n", g=NG)
        x_hm = facc.bitcast(BF16)
        x_l = new(NT, T, F // 2).bitcast(BF16)
        wcc = new(2 * F, 3, F)
        wconv = new(F, 3, F)
        wf = new(F, 4, F)
        we = new(EF, QC)
        bconv = new(NT, 12, F)
        bsum = new(EF, 2, 2 * F)
        xd = new(NT, 2, 2, 2, F)
        aggs = new(2 * F, BN)
        yc = new(NT, 2, F)
        yT = new(F, 2, BN)
        stat = new(NT, 8, F)
        colm = new(NT, 4, T)
        segb = new(EF, BN)
        extra = at(seg_off, 2 * F, N)
        assert top[0] <= SB, top[0]

        bank = [ctx.enter_context(nc.psum_tensor(f"bank{i}", [P, 512], F32)) for i in range(8)]

        def bc(ap, axis, n):
            v = ap.unsqueeze(axis)
            shape = list(v.shape)
            shape[axis] = n
            return v.to_broadcast(shape)

        S = {}

        def s(name):
            if name not in S:
                S[name] = sem(name)
            return S[name]

        for names in (
            "consts_made pool_const edges_loaded heads_loaded weights_loaded x_loaded rec_made rec_stored "
            "ptr_rows_wanted ptr_rows_here ptr_made ptr_out ptr_back items_made items_out items_back xT_loaded "
            "v_made wgat_cleared wgat_loaded el_psum table_made table_stored er_stored "
            "onehot_made rows_weighted adj_psum adj_evacuated seg_evacuated ov_loaded ov_onehot ov_weighted ov_psum ov_added "
            "ov_stored top_made top_t diag_made top_psum logits_made exp_made win_psum win_evac "
            "ga_loaded ga_rows ga_top ga_topt ga_diag ga_topp ga_logits ga_exp ga_psum ga_added "
            "ga_stored gat_psum gat_y gat_tanh gat_h gat_hT gat_hTc gat_v gat_xt "
            "gat_done conv_w we_made pn_copied pn_psum pn_evac out_stored ln_var ln_std passed_sp passed_pool "
            "ov_cleared ov_zeroed ex_loaded ex_psum ex_done cv_self cv_agg cv_aggc cv_y cv_ev cv_yT cv_yTc cv_f cv_done bn_sum bn_mean bn_var bn_std "
        ).split():
            s(names)
        rec_loaded = [sem(f"rec_loaded{i}") for i in range(NG)]
        rec_used = [sem(f"rec_used{i}") for i in range(NG)]
        gathered = [sem(f"gathered{i}") for i in range(NG)]
        top_stored = [sem(f"top_stored{i}") for i in range(2)]
        adj_loaded = [sem(f"adj_loaded{i}") for i in range(NG)]
        adj_used = [sem(f"adj_used{i}") for i in range(NG)]
        adj_stored = [sem(f"adj_stored{i}") for i in range(3)]
        win_used = [sem(f"win_used{i}") for i in range(NG)]
        win_stored = [sem(f"win_stored{i}") for i in range(NG)]
        agg_loaded = [sem(f"agg_loaded{i}") for i in range(NG)]
        agg_used = [sem(f"agg_used{i}") for i in range(NG)]
        cv_loaded = [sem(f"cv_loaded{i}") for i in range(NQ)]
        cv_used = [sem(f"cv_used{i}") for i in range(NQ)]

        block = ctx.enter_context(nc.Block())

        def edge_rows(dram_ap, off):
            return dram_ap[bass.ds(off, CAP), :].rearrange("(p c) f -> p (c f)", c=CH)

        def nodes(dram_ap):
            return dram_ap.rearrange("(t p) f -> p t f", p=NT)

        def flat(ap):
            k = len(ap.shape) - 1
            if k == 1:
                return ap
            names = "abcde"[:k]
            return ap.rearrange(f"p {' '.join(names)} -> p ({' '.join(names)})")

        def wait_reg(eng, semaphore, value):
            eng.wait_ge(semaphore, value)
            eng.sem_inc(s(f"passed_{'sp' if eng is nc.sync else 'pool'}"), 1)

        def rounds(eng, count, peel=True):
            if peel:
                yield 0
            with eng.Fori(int(peel), count) as i:
                yield i

        def pairs(eng):
            for i in rounds(eng, B // 2):
                yield i * 2, 0
                yield i * 2 + 1, 1
            yield B - 1, 0

        def first(b):
            return isinstance(b, int) and b == 0

        def prep_sync(sp):
            sp.dma_start(src_idx, a["src"]).then_inc(s("edges_loaded"), 16)
            sp.dma_start(tmp[0].bitcast(I32), a["dst"].rearrange("a b -> (a b)").rearrange("(p c) -> p c", p=P)).then_inc(s("edges_loaded"), 16)
            sp.dma_start(tmp[1], a["edge_weight"]).then_inc(s("edges_loaded"), 16)
            sp.dma_start(x_sb, nodes(a["x"])).then_inc(s("x_loaded"), 16)
            sp.wait_ge(s("rec_made"), 1)
            sp.dma_start(rec_d.rearrange("(p c) f -> p (c f)", p=P), flat(rec_all)).then_inc(s("rec_stored"), 16)
            sp.wait_ge(s("rec_stored"), 16)
            sp.dma_start(heads.bitcast(I32), a["dst_heads"].to_broadcast([NT, EC])).then_inc(s("heads_loaded"), 16)
            sp.dma_start(xT_sb, a["xT"]).then_inc(s("xT_loaded"), 16)
            sp.wait_ge(s("ptr_made"), 1)
            with nc.allow_non_contiguous_dma(reason="625 window starts"):
                sp.dma_start(ptr_d[0, 0:NW].rearrange("(c p) -> p c", p=NT), ptr_f).then_inc(s("ptr_out"), 16)
                sp.dma_start(ptri_d[0, 0:NW].rearrange("(c p) -> p c", p=NT), ptr_i).then_inc(s("ptr_out"), 16)
            sp.dma_start(ptr_d[:, NW:NW + 1], ptr_end).then_inc(s("ptr_out"), 16)
            sp.wait_ge(s("ptr_out"), 48)
            sp.dma_start(ptrb, ptr_d.to_broadcast([NT, NW + 1])).then_inc(s("ptr_back"), 16)
            sp.dma_start(ptr_row[:, 0:NW], ptri_d[:, 0:NW]).then_inc(s("ptr_back"), 16)
            sp.wait_ge(s("items_made"), 1)
            with nc.allow_non_contiguous_dma(reason="the overflow items"):
                for i in range(4):
                    sp.dma_start(items_d[i, :].rearrange("(c p) -> p c", p=NT), iti[:, i, :]).then_inc(s("items_out"), 16)
            sp.wait_ge(s("items_out"), 64)
            sp.dma_start(items, items_d.rearrange("i k -> (i k)").unsqueeze(0)).then_inc(s("items_back"), 16)
            sp.wait_ge(s("items_back"), 16)

        def logit_weights_sync(sp):
            for l in range(2):
                sp.dma_start(wv[:, l, :], a[f"L0_gnn_W{l + 1}"]).then_inc(s("weights_loaded"), 16)
                for i, n in enumerate(("al", "ar")):
                    sp.dma_start(alr[:, 2 * l + i, :], a[f"L0_gnn_{n}{l + 1}"].rearrange("h f -> (h f)").unsqueeze(0).to_broadcast([F, H * F])).then_inc(s("weights_loaded"), 16)

        def gat_weights_sync(sp, layer):
            if layer:
                sp.wait_ge(s("gat_done"), 1)
            else:
                sp.wait_ge(s("wgat_cleared"), 1)
            sp.dma_start(wgat[0:F, :, 0:F], a[f"L0_gnn_W{layer + 1}"].rearrange("k (h f) -> k h f", h=H)).then_inc(s("wgat_loaded"), 16)
            sp.dma_start(gbias, a[f"L0_gnn_b{layer + 1}"].rearrange("h f -> (h f)").unsqueeze(0).to_broadcast([NT, H * F])).then_inc(s("wgat_loaded"), 16)

        def table_sync(sp, layer):
            sp.wait_ge(s("table_made"), layer + 1)
            sp.dma_start(nodes(table_d), xt).then_inc(s("table_stored"), 16)
            sp.dma_start(nodes(er_d), er_sb).then_inc(s("er_stored"), 16)

        def win_sync(sp, layer):
            sp.wait_ge(s("er_stored"), 16 * (layer + 1))
            for b in rounds(sp, B):
                for g in range(NG):
                    wait_reg(sp, rec_used[g], b + layer * B)
                    if g in ADJ[layer]:
                        wait_reg(sp, adj_used[g], b)
                    for w in range(WG):
                        off = sp.value_load(ptr_row[0:1, bass.ds(b * (NG * WG) + g * WG + w, 1)], min_val=0, max_val=EP - CAP)
                        sp.dma_start(rec_sl[:, g, w, :], edge_rows(rec_d, off)).then_inc(rec_loaded[g], 16)
                        if g in ADJ[layer]:
                            sp.dma_start(ef_sl[:, built_before(layer, g), w, :], edge_rows(a["edge_features"], off)).then_inc(adj_loaded[g], 16)
                    sp.dma_start(er_sl[:, g, :], er_d[bass.ds(b * BN + g * GN, GN), :].rearrange("n h -> (n h)").unsqueeze(0).to_broadcast([P, GN * H])).then_inc(rec_loaded[g], 16)
            for g in range(NG):
                sp.wait_ge(win_stored[g], 16 * B * (layer + 1))
            for i in range(2):
                sp.wait_ge(top_stored[i], 16 * (NG_PAR[i] * B) * (layer + 1))
            for i in range(3):
                sp.wait_ge(adj_stored[i], stage_stores(layer + 1, 0, i))

        NG_PAR = ((NG + 1) // 2, NG // 2)
        ADJ = (tuple(range(0, NG, 2)), tuple(range(1, NG, 2)))
        ADJ_BASE = (0, B * len(ADJ[0]))

        def groups_before(layer, b, i):
            return b * len(ADJ[layer]) + (ADJ_BASE[layer] + i)

        def windows_before(layer, b, n):
            return b * (len(ADJ[layer]) * WG) + (ADJ_BASE[layer] * WG + n)

        def built_before(layer, g):
            return sum(1 for x in ADJ[layer] if x < g)

        def built_through(layer, g):
            return built_before(layer, g + 1) if g >= 0 else built_before(layer, g + 1 + NG) - len(ADJ[layer])

        def former_group(g):
            return next(x for x in range(g - 1, g - NG - 1, -1) if (x % NG) % GS == g % GS)

        def wait_some(eng, semaphore, value):
            if not (isinstance(value, int) and value <= 0):
                eng.wait_ge(semaphore, value)

        def ahead(layer, g):
            return g - 1 not in ADJ[layer] and g in ADJ[layer] and g > 0

        def stage_stores(layer, b, slot):
            return b * 32 + 32 * sum(B for l in range(layer) if slot < len(ADJ[l]))
        LOADS = 16 * (WG + 1)

        def adj_window(d, group, node):
            return d[bass.ds(group, 1), :, :, bass.ds(node, WN)].rearrange("a p t n -> p (a t) n")

        def item(eng, row, k, top_):
            return eng.value_load(items[0:1, bass.ds(k + row * NW, 1)], min_val=0, max_val=top_)

        def adj_overflow_sync(sp):
            count = sp.value_load(n_items, min_val=0, max_val=NW)
            with sp.If(count > 0):
                sp.wait_ge(s("ov_cleared"), 1)
                with sp.Fori(0, NGR) as group:
                    sp.dma_start(adj_k_d[bass.ds(group, 1), :, :, :].rearrange("a p t n -> p (a t n)"), zeros).then_inc(s("ov_zeroed"), 16)
                sp.wait_ge(s("ov_zeroed"), 16 * NGR)
                with sp.Fori(0, count) as k:
                    off = item(sp, 0, k, EP - CAP)
                    group = item(sp, 2, k, NGR - 1)
                    node = item(sp, 3, k, GN - WN)
                    sp.dma_start(rec_sl[:, 0, 0, :], edge_rows(rec_d, off)).then_inc(s("ov_loaded"), 16)
                    sp.dma_start(ef_sl[:, 0, 0, :], edge_rows(a["edge_features"], off)).then_inc(s("ov_loaded"), 16)
                    for d, o in ((adj_w_d, ov_w), (adj_c_d, ov_c), (adj_k_d, ov_k)):
                        sp.dma_start(o.rearrange("p (t n) -> p t n", n=WN), adj_window(d, group, node)).then_inc(s("ov_loaded"), 16)
                    sp.wait_ge(s("ov_added"), k + 1)
                    for d, o in ((adj_w_d, ov_w), (adj_c_d, ov_c), (adj_k_d, ov_k)):
                        sp.dma_start(adj_window(d, group, node), o.rearrange("p (t n) -> p t n", n=WN)).then_inc(s("ov_stored"), 16)
                    wait_reg(sp, s("ov_stored"), k * 48 + 48)

        def agg_window(node):
            return agg_d[:, :, bass.ds(node, WN)]

        def win_overflow_sync(sp, layer):
            count = sp.value_load(n_items, min_val=0, max_val=NW)
            with sp.If(count > 0):
                with sp.Fori(0, count) as k:
                    off = item(sp, 0, k, EP - CAP)
                    win = item(sp, 1, k, NW - 1)
                    node = win * WN
                    tops = max_d[:, bass.ds(win * WH, WH)]
                    sp.dma_start(rec_sl[:, 0, 0, :], edge_rows(rec_d, off)).then_inc(s("ga_loaded"), 16)
                    sp.dma_start(er_sl[:, 0, 0:WN * H], er_d[bass.ds(node, WN), :].rearrange("n h -> (n h)").unsqueeze(0).to_broadcast([P, WN * H])).then_inc(s("ga_loaded"), 16)
                    sp.dma_start(top_o[:, 0, :], tops.to_broadcast([P, WH])).then_inc(s("ga_loaded"), 16)
                    sp.dma_start(ov_agg.rearrange("p (h n) -> p h n", h=H), agg_window(node)).then_inc(s("ga_loaded"), 16)
                    sp.wait_ge(s("ga_added"), ga_base(sp, layer) + k + 1)
                    sp.dma_start(agg_window(node), ov_agg.rearrange("p (h n) -> p h n", h=H)).then_inc(s("ga_stored"), 16)
                    sp.dma_start(tops, top_o[0:1, 1, :]).then_inc(s("ga_stored"), 16)
                    wait_reg(sp, s("ga_stored"), (ga_base(sp, layer) + k) * 32 + 32)

        def ga_base(eng, layer):
            return eng.value_load(n_items, min_val=0, max_val=NW) if layer else 0

        def gat_banks(u):
            return ((bank[0], bank[1]), (bank[2], bank[3]), (bank[6], bank[7]))[u % 3]

        def gat_sync(sp, layer):
            for i in rounds(sp, B // NG, layer == 0):
                for u in range(NG):
                    sp.wait_ge(agg_used[u], i + layer * (B // NG))
                    sp.dma_start(agg_sl[:, u], agg_d[:, :, bass.ds(i * (NG * BN) + u * BN, BN)]).then_inc(agg_loaded[u], 16)

        def conv_weights_sync(sp):
            sp.wait_ge(s("gat_done"), 2)
            q = s("conv_w")
            for i in range(3):
                sp.dma_start(wconv[:, i, :], a[f"L1_gnn_W{i}"]).then_inc(q, 16)
            for i in range(2):
                for part in range(2):
                    sp.dma_start(wcc[part * F:(part + 1) * F, 1 + i, :], a[f"L3_gnn_W{i + 1}"]).then_inc(q, 16)
            sp.dma_start(wf, a["L1_gnn_Wf"].rearrange("(i k) f -> k i f", k=F)).then_inc(q, 16)
            for i, n in enumerate(("L1_gnn_b0", "L1_gnn_b1", "L1_gnn_b2", "L1_gnn_bf", "L3_gnn_b1", "L3_gnn_b2", "L3_gnn_bias1", "L3_gnn_bias2",
                                   "L3_gnn_g1", "L3_gnn_beta1", "L3_gnn_g2", "L3_gnn_beta2")):
                sp.dma_start(bconv[:, i, :], a[n].unsqueeze(0).to_broadcast([NT, F])).then_inc(q, 16)
            for i in range(2):
                sp.dma_start(we[0:ED, 1 + i * F:1 + (i + 1) * F], a[f"L3_gnn_We{i + 1}"]).then_inc(q, 16)
                sp.dma_start(bsum[ED:ED + 1, 0, i * F:(i + 1) * F], a[f"L3_gnn_b{i + 1}"].unsqueeze(0)).then_inc(q, 16)
                sp.dma_start(bsum[ED:ED + 1, 1, i * F:(i + 1) * F], a[f"L3_gnn_be{i + 1}"].unsqueeze(0)).then_inc(q, 16)

        CONV_W = 16 * (3 + 4 + 1 + 12 + 6)

        def extra_sync(sp, n):
            count = sp.value_load(n_items, min_val=0, max_val=NW)
            with sp.If(count > 0):
                sp.wait_ge(s("cv_done"), n + 1)
                with sp.Fori(0, B) as b:
                    for q in range(NQ):
                        sp.dma_start(adj16_sl[:, q], adj_k_d[bass.ds(b * NG, NG), :, q * QT:(q + 1) * QT, :].rearrange("g p t n -> p g (t n)")).then_inc(s("ex_loaded"), 16)
                    wait_reg(sp, s("ex_psum"), b + ((n - 3) * B + 1))

        def conv_sync(sp, n, adj, slots):
            for b in rounds(sp, B, n == 0):
                for q in range(NQ):
                    sp.wait_ge(cv_used[q], b + n * B)
                    sp.dma_start(slots[:, q], adj[bass.ds(b * NG, NG), :, q * QT:(q + 1) * QT, :].rearrange("g p t n -> p g (t n)")).then_inc(cv_loaded[q], 16)

        @block.sync
        def _(sp):
            logit_weights_sync(sp)
            prep_sync(sp)
            gat_weights_sync(sp, 0)
            table_sync(sp, 0)
            win_sync(sp, 0)
            win_overflow_sync(sp, 0)
            gat_sync(sp, 0)
            gat_weights_sync(sp, 1)
            table_sync(sp, 1)
            win_sync(sp, 1)
            adj_overflow_sync(sp)
            win_overflow_sync(sp, 1)
            gat_sync(sp, 1)
            conv_weights_sync(sp)
            for n, adj in enumerate((adj_w_d, adj_w_d, adj_w_d, adj_c_d, adj_c_d, adj_c_d)):
                if n == 0:
                    sp.wait_ge(s("pn_evac"), 1)
                if n >= 3:
                    extra_sync(sp, n)
                conv_sync(sp, n, adj, adj_sl if n < 3 else adj16_sl)
            sp.wait_ge(s("cv_done"), 7)
            sp.dma_start(nodes(a["out"]), x_sb).then_inc(s("out_stored"), 16)
            sp.wait_ge(s("out_stored"), 16)

        def consts_pool(pool):
            g = nc.gpsimd
            g.iota(iota_wn, [[1, WN]], base=0, channel_multiplier=0, allow_small_or_imprecise_dtypes=True)
            g.iota(iota_key, [[1, T * WN]], base=0, channel_multiplier=0, allow_small_or_imprecise_dtypes=True)
            g.iota(iota_lo, [[1, P]], base=0, channel_multiplier=0, allow_small_or_imprecise_dtypes=True)
            g.iota(win_node, [[WN, NW]], base=0, channel_multiplier=0, allow_small_or_imprecise_dtypes=True)
            g.iota(win_key, [[KEY, NW]], base=0, channel_multiplier=0, allow_small_or_imprecise_dtypes=True)
            g.memset(ones, 1.0)
            g.memset(ident, 0.0).then_inc(s("pool_const"), 1)
            g.memset(flip, 0.0).then_inc(s("pool_const"), 1)
            pool.wait_ge(s("pool_const"), 2)
            g.affine_select(out=ident, in_=ident, compare_op=ALU.not_equal, fill=1.0, base=0, pattern=[[-1, P]], channel_multiplier=1).then_inc(s("consts_made"), 1)
            g.affine_select(out=flip, in_=flip, compare_op=ALU.not_equal, fill=1.0, base=1 - P, pattern=[[1, P]], channel_multiplier=1).then_inc(s("consts_made"), 1)
            pool.wait_ge(s("rec_stored"), 16)
            g.iota(thr, [[WN * NT, 5]], base=0, channel_multiplier=WN, allow_small_or_imprecise_dtypes=True)
            g.iota(kid, [[NT, 5]], base=0, channel_multiplier=1, allow_small_or_imprecise_dtypes=True)
            g.iota(iota_nw, [[1, NW]], base=0, channel_multiplier=0, allow_small_or_imprecise_dtypes=True)
            g.memset(onesw, 1.0).then_inc(s("consts_made"), 1)
            pool.wait_ge(s("ptr_rows_wanted"), 1)
            for c in range(5):
                g.indirect_dma_start(rowd[:, c, :], None, a["dst"], bass.IndirectOffsetOnAxis(ap=rowi[:, c:c + 1], axis=0)).then_inc(s("ptr_rows_here"), 16)

        def win_pool(pool, layer):
            g_ = nc.gpsimd
            pool.wait_ge(s("table_stored"), 16 * (layer + 1))
            for b in rounds(pool, B, layer == 0):
                for g in range(NG):
                    pool.wait_ge(rec_loaded[g], b * LOADS + LOADS * (layer * B + 1))
                    wait_reg(pool, win_used[g], b + layer * B)
                    for w in range(WG):
                        for c in range(CH):
                            g_.indirect_dma_start(rows_sl[:, g, w, c, :], None, table_d, bass.IndirectOffsetOnAxis(
                                ap=rec_sl[:, g, w, (c + 1) * REC - 1:(c + 1) * REC].bitcast(I32), axis=0)).then_inc(gathered[g], 16)

        def win_overflow_pool(pool, layer):
            count = pool.value_load(n_items, min_val=0, max_val=NW)
            with pool.If(count > 0):
                with pool.Fori(0, count) as k:
                    kk = ga_base(pool, layer) + k
                    wait_reg(pool, s("ga_loaded"), kk * 64 + 64)
                    for c in range(CH):
                        nc.gpsimd.indirect_dma_start(rows_sl[:, 0, 0, c, :], None, table_d, bass.IndirectOffsetOnAxis(
                            ap=rec_sl[:, 0, 0, (c + 1) * REC - 1:(c + 1) * REC].bitcast(I32), axis=0)).then_inc(s("ga_rows"), 16)

        @block.gpsimd
        def _(pool):
            consts_pool(pool)
            pool.wait_ge(s("items_back"), 16)
            for layer in range(2):
                win_pool(pool, layer)
                win_overflow_pool(pool, layer)

        v = nc.vector

        def prep_vector(d):
            d.wait_ge(s("edges_loaded"), 48)
            hi, dst, ew = tmp[3], tmp[2], tmp[1]
            srcf, t0 = rec_all[:, :, 0], rec_all[:, :, 1]
            v.tensor_copy(srcf, src_idx)
            v.tensor_copy(rec_all[:, :, 6].bitcast(I32), src_idx)
            v.tensor_copy(dst, tmp[0].bitcast(I32))
            v.tensor_copy(hi_bf, ew)
            d.drain()
            v.tensor_scalar(hi, srcf, 1.0 / NT, 0.5 / NT - 0.5, ALU.mult, ALU.add)
            v.tensor_scalar(tmp[0], dst, 1.0 / WN, 0.5 / WN - 0.5, ALU.mult, ALU.add)
            v.tensor_copy(rec_all[:, :, 5], dst)
            v.tensor_copy(rec_all[:, :, 2], hi_bf)
            d.drain()
            v.tensor_scalar(hi, hi, RND, None, ALU.add)
            v.tensor_scalar(tmp[0], tmp[0], RND, None, ALU.add)
            v.tensor_tensor(ew, ew, rec_all[:, :, 2], ALU.subtract)
            d.drain()
            v.tensor_scalar(hi, hi, -RND, None, ALU.add)
            v.tensor_scalar(tmp[0], tmp[0], -RND, None, ALU.add)
            v.tensor_copy(hi_bf, ew)
            d.drain()
            v.scalar_tensor_tensor(t0, hi, -float(NT), srcf, ALU.mult, ALU.add)
            v.tensor_copy(rec_all[:, :, 3], hi_bf)
            d.drain()
            v.scalar_tensor_tensor(srcf, tmp[0], float(KEY - WN), dst, ALU.mult, ALU.add)
            v.tensor_tensor(rec_all[:, :, 4], ew, rec_all[:, :, 3], ALU.subtract)
            d.drain()
            v.scalar_tensor_tensor(srcf, hi, float(WN), srcf, ALU.mult, ALU.add)
            d.drain().then_inc(s("rec_made"), 1)

        def ptr_vector(d):
            d.wait_ge(s("heads_loaded"), 16)
            d.wait_ge(s("consts_made"), 3)
            v.tensor_copy(heads_f, heads.bitcast(I32))
            d.drain()
            for c in range(5):
                v.tensor_scalar(junk, heads_f, thr[:, c:c + 1], None, ALU.is_lt, ALU.add, accum_out=cnt[:, c:c + 1])
                d.drain()
            v.tensor_scalar(cnt, cnt, -1.0, 0.0, ALU.add, ALU.max)
            d.drain()
            v.tensor_copy(rowi, cnt).then_inc(s("ptr_rows_wanted"), 1)
            d.wait_ge(s("ptr_rows_here"), 80)
            v.tensor_copy(rowf, rowd)
            d.drain()
            for c in range(5):
                v.tensor_scalar(junk[:, 0:P], rowf[:, c, :], thr[:, c:c + 1], None, ALU.is_lt, ALU.add, accum_out=cnt2[:, c:c + 1])
                d.drain()
            v.scalar_tensor_tensor(ptr_f, cnt, float(P), cnt2, ALU.mult, ALU.add)
            v.memset(ptr_end, float(E))
            d.drain()
            v.tensor_copy(ptr_i, ptr_f)
            d.drain().then_inc(s("ptr_made"), 1)
            d.wait_ge(s("ptr_back"), 32)
            v.tensor_tensor(nover, ptrb[:, 1:NW + 1], ptrb[:, 0:NW], ALU.subtract)
            d.drain()
            v.tensor_scalar(nover, nover, 1.0 / CAP, -0.5 / CAP - 0.5, ALU.mult, ALU.add)
            d.drain()
            v.tensor_scalar(nover, nover, RND, None, ALU.add)
            d.drain()
            v.tensor_scalar(nover, nover, -RND, 0.0, ALU.add, ALU.max)
            d.drain()
            v.tensor_tensor_scan(cum, onesw, nover, 0.0, ALU.mult, ALU.add)
            d.drain()
            v.tensor_copy(n_items, cum[0:1, NW - 1:NW])
            v.tensor_tensor(nover, cum, nover, ALU.subtract)
            for c in range(5):
                v.tensor_scalar(junk[:, 0:NW], cum, kid[:, c:c + 1], None, ALU.is_le, ALU.add, accum_out=itw[:, c:c + 1])
                d.drain()
            v.tensor_scalar(offv, nover, -float(CAP), float(CAP), ALU.mult, ALU.add)
            d.drain()
            v.tensor_tensor(offv, offv, ptrb[:, 0:NW], ALU.add)
            d.drain()
            for c in range(5):
                v.scalar_tensor_tensor(junk[:, 0:NW], iota_nw, itw[:, c:c + 1], offv, ALU.is_equal, ALU.mult, accum_out=itf[:, 0, c:c + 1])
                d.drain()
            v.scalar_tensor_tensor(itf[:, 0, :], kid, float(CAP), itf[:, 0, :], ALU.mult, ALU.add)
            v.tensor_copy(itf[:, 1, :], itw)
            v.tensor_scalar(itf[:, 2, :], itw, 1.0 / WG, 0.5 / WG - 0.5, ALU.mult, ALU.add)
            d.drain()
            v.tensor_scalar(itf[:, 2, :], itf[:, 2, :], RND, None, ALU.add)
            d.drain()
            v.tensor_scalar(itf[:, 2, :], itf[:, 2, :], -RND, None, ALU.add)
            d.drain()
            v.scalar_tensor_tensor(itf[:, 3, :], itf[:, 2, :], -float(WG), itw, ALU.mult, ALU.add)
            d.drain()
            v.tensor_scalar(itf[:, 3, :], itf[:, 3, :], float(WN), None, ALU.mult)
            d.drain()
            v.tensor_copy(iti, itf)
            d.drain().then_inc(s("items_made"), 1)

        def logit_weights_vector(d):
            v.memset(wgat, 0.0)
            d.drain()
            v.memset(wgat[F:AGG, :, F:AGG], 1.0)
            d.drain().then_inc(s("wgat_cleared"), 1)
            d.wait_ge(s("weights_loaded"), 16 * 6)
            for l in range(2):
                for i in range(2):
                    v.tensor_tensor(vprod[:, 2 * l + i, :], wv[:, l, :], alr[:, 2 * l + i, :], ALU.mult)
            d.drain()
            for l in range(2):
                for i in range(2):
                    v.tensor_reduce(vw[:, l, i * H:(i + 1) * H], vprod[:, 2 * l + i, :].rearrange("p (h f) -> p h f", h=H), AX.X, ALU.add)
            d.drain().then_inc(s("v_made"), 1)

        def table0_vector(d):
            d.wait_ge(s("x_loaded"), 16)
            v.tensor_copy(xt[:, :, 0:F], x_sb)
            v.memset(xt[:, :, F:F + 1], 1.0)
            d.wait_ge(s("el_psum"), 1)
            e = bank[7][0:NT, 0:T * 2 * H].rearrange("p (t k) -> p t k", k=2 * H)
            v.tensor_copy(xt[:, :, F + 1:XC], e[:, :, 0:H])
            v.tensor_copy(er_sb, e[:, :, H:2 * H])
            d.drain().then_inc(s("table_made"), 1)

        def one_hots(d, slot, rec, key, c):
            v.tensor_scalar(col_oh[:, slot, c, :], iota_key, key, None, ALU.is_equal)
            v.tensor_scalar(row_oh[:, slot, c, 3, :], iota_lo, rec[:, c * REC + 1:c * REC + 2], None, ALU.is_equal)
            v.tensor_scalar(row_oh[:, slot, c, 0, :], iota_lo, rec[:, c * REC + 1:c * REC + 2], rec[:, c * REC + 2:c * REC + 3], ALU.is_equal, ALU.mult)

        def keys(d, par, recs, wk, wn, nw):
            r = recs.rearrange("p w (c r) -> p w c r", r=REC)
            n = nw * CH
            v.tensor_tensor(ckey[:, 0:n].rearrange("p (w c) -> p w c", c=CH), r[:, :, :, 0], bc(wk, 2, CH), ALU.subtract)
            v.tensor_tensor(cdl[:, 0:n].rearrange("p (w c) -> p w c", c=CH), r[:, :, :, 5], bc(wn, 2, CH), ALU.subtract)
            d.drain()
            v.tensor_tensor(coh[:, par, 0:n, :], bc(cdl[:, 0:n], 2, WN), bc(iota_wn, 1, n), ALU.is_equal)

        def logits(d, par, rows, er, nw):
            n = nw * CH
            e = er.rearrange("p (w j h) -> p w h j", j=WN, h=H)
            for c in range(CH):
                v.tensor_tensor(lg[:, 0:nw, c], bc(rows[:, :, c, F + 1:XC], 3, WN), e, ALU.add)
            d.drain()
            v.tensor_scalar(pen[:, 0:n, :], coh[:, par, 0:n, :], 1.0, BIG, ALU.subtract, ALU.mult)
            z = lg[:, 0:nw].rearrange("p w c h j -> p (w c h j)")
            v.scalar_tensor_tensor(z, z, 0.2, z, ALU.mult, ALU.max)
            d.drain()
            zz = lg[:, 0:nw].rearrange("p w c h j -> p (w c) h j")
            v.tensor_tensor(zz, zz, bc(pen[:, 0:n, :], 2, H), ALU.add)
            d.drain()
            m = top_e[:, 0:nw * WH].rearrange("p (w k) -> p w k", k=WH)
            lc = [lg[:, 0:nw, c].rearrange("p w h j -> p w (h j)") for c in range(CH)]
            v.scalar_tensor_tensor(m, lc[0], -0.1 * BIG, lc[1], ALU.max, ALU.max)
            d.drain()
            for c in range(2, CH):
                v.tensor_tensor(m, m, lc[c], ALU.max)
                d.drain()

        def diagonals(d, nw, topt):
            for i in range(-(-nw // TW)):
                k = min(TW, nw - i * TW) * WH
                v.tensor_reduce(top_s[0:k, i:i + 1], topt[0:k, i * P:(i + 1) * P], AX.X, ALU.max)
            d.drain()
            for i in range(-(-nw // TW)):
                k = min(TW, nw - i * TW) * WH
                v.tensor_scalar(diag[0:k, i, 0:k], ident[0:k, 0:k], top_s[0:k, i:i + 1], None, ALU.mult)
            d.drain()

        def win_vector(d, layer):
            ng = NG * B * layer
            for b in rounds(d, B):
                for g in range(NG):
                    par = g % 2
                    n1 = b * NG + (ng + g + 1)

                    def adjacency(w, g=g):
                        if g not in ADJ[layer]:
                            return
                        n = built_before(layer, g) * WG + w
                        wait_some(d, s("adj_psum"), windows_before(layer, b, n - (OHS - 1)))
                        for c in range(CH):
                            one_hots(d, n % OHS, rec_sl[:, g, w, :], ckey[:, w * CH + c:w * CH + c + 1], c)
                        d.drain().then_inc(s("onehot_made"), 1)

                    def start(g):
                        d.wait_ge(rec_loaded[g], b * LOADS + LOADS * (layer * B + 1))
                        wait_some(d, s("adj_psum"), windows_before(layer, b, built_through(layer, former_group(g)) * WG))
                        w0 = b * (NG * WG) + g * WG
                        keys(d, g % GS, rec_sl[:, g], win_key[:, bass.ds(w0, WG)], win_node[:, bass.ds(w0, WG)], WG)
                        d.drain()
                        adjacency(0, g)
                        adjacency(1, g)

                    if not ahead(layer, g):
                        start(g)
                    d.wait_ge(gathered[g], b * (16 * WG * CH) + 16 * WG * CH * (layer * B + 1))
                    logits(d, g % GS, rows_sl[:, g], er_sl[:, g], WG)
                    d.drain().then_inc(s("top_made"), 1)
                    if ahead(layer, g + 1):
                        start(g + 1)
                    adjacency(2)
                    d.wait_ge(s("top_t"), n1)
                    diagonals(d, WG, bank[5])
                    d.drain().then_inc(s("diag_made"), 1)
                    adjacency(3)
                    d.wait_ge(s("top_psum"), n1)
                    former = (g + 1) // 2 if par == 0 else g // 2
                    d.wait_ge(top_stored[par], b * (16 * NG_PAR[par]) + 16 * (NG_PAR[par] * B * layer + former))
                    wait_some(d, s("exp_made"), b * NG + (ng + former_group(g) + 1))
                    tp = bank[5][:, 2 * P:2 * P + WG * WH]
                    v.tensor_copy(top_row[:, par, :], tp[0:1])
                    v.tensor_tensor(gd[:, g % GS].rearrange("p (w c) k -> p w c k", c=CH), lg.rearrange("p w c h j -> p w c (h j)"),
                                    bc(tp.rearrange("p (w k) -> p w k", k=WH), 2, CH), ALU.subtract)
                    d.drain().then_inc(s("logits_made"), 1)
                    adjacency(4)
                    d.sem_inc(rec_used[g], 1)

        def adj_overflow_vector(d):
            d.wait_ge(s("seg_evacuated"), NGR)
            count = d.value_load(n_items, min_val=0, max_val=NW)
            with d.If(count > 0):
                for i in range(3):
                    d.wait_ge(adj_stored[i], stage_stores(2, 0, i))
                v.memset(zeros, 0.0)
                d.drain().then_inc(s("ov_cleared"), 1)
                with d.Fori(0, count) as k:
                    win = item(d, 1, k, NW - 1)
                    d.wait_ge(s("ov_loaded"), k * 80 + 80)
                    keys(d, 0, rec_sl[:, 0, 0:1], win_key[:, bass.ds(win, 1)], win_node[:, bass.ds(win, 1)], 1)
                    for c in range(CH):
                        one_hots(d, 0, rec_sl[:, 0, 0, :], ckey[:, c:c + 1], c)
                    d.drain().then_inc(s("ov_onehot"), 1)
                    d.wait_ge(s("ov_psum"), k + 1)
                    v.tensor_tensor(ov_w, ov_w, bank[0][:, 0:T * WN], ALU.add)
                    v.tensor_tensor(ov_sum, ov_c, bank[1][:, 0:T * WN], ALU.add)
                    d.drain()
                    v.tensor_scalar(ov_kf, ov_sum, 1.0 / KILO, 0.5 / KILO - 0.5, ALU.mult, ALU.add)
                    d.drain()
                    v.tensor_scalar(ov_kf, ov_kf, RND, None, ALU.add)
                    d.drain()
                    v.tensor_scalar(ov_kf, ov_kf, -RND, None, ALU.add)
                    d.drain()
                    v.scalar_tensor_tensor(ov_c, ov_kf, -float(KILO), ov_sum, ALU.mult, ALU.add)
                    v.tensor_tensor(ov_k, ov_k, ov_kf, ALU.add)
                    sg = seg_t[:, bass.ds(win * WN, WN)]
                    v.tensor_tensor(sg, sg, bank[4][0:EF, 0:WN], ALU.add)
                    d.drain().then_inc(s("ov_added"), 1)

        def win_overflow_vector(d, layer):
            count = d.value_load(n_items, min_val=0, max_val=NW)
            with d.If(count > 0):
                with d.Fori(0, count) as k:
                    kk = ga_base(d, layer) + k
                    win = item(d, 1, k, NW - 1)
                    d.wait_ge(s("ga_loaded"), kk * 64 + 64)
                    d.wait_ge(s("ga_rows"), kk * (16 * CH) + 16 * CH)
                    keys(d, 0, rec_sl[:, 0, 0:1], win_key[:, bass.ds(win, 1)], win_node[:, bass.ds(win, 1)], 1)
                    d.drain()
                    logits(d, 0, rows_sl[:, 0, 0:1], er_sl[:, 0, 0:WN * H], 1)
                    d.drain().then_inc(s("ga_top"), 1)
                    d.wait_ge(s("ga_topt"), kk + 1)
                    diagonals(d, 1, bank[5])
                    d.drain().then_inc(s("ga_diag"), 1)
                    d.wait_ge(s("ga_topp"), kk + 1)
                    v.tensor_tensor(top_o[:, 1, :], top_o[:, 0, :], bank[5][:, 2 * P:2 * P + WH], ALU.max)
                    d.drain()
                    v.tensor_tensor(top_o[:, 2, :], top_o[:, 0, :], top_o[:, 1, :], ALU.subtract)
                    v.tensor_tensor(gd[:, 0, 0:CH, :], lg[:, 0].rearrange("p c h j -> p c (h j)"), bc(top_o[:, 1, :], 1, CH), ALU.subtract)
                    d.drain().then_inc(s("ga_logits"), 1)
                    d.wait_ge(s("ga_exp"), kk + 1)
                    v.tensor_tensor(ov_agg, ov_agg, top_o[0:AGG, 2, :], ALU.mult)
                    d.drain()
                    d.wait_ge(s("ga_psum"), kk + 1)
                    v.tensor_tensor(ov_agg, ov_agg, bank[6][0:AGG, 0:WH], ALU.add)
                    d.drain().then_inc(s("ga_added"), 1)

        def gat_vector(d, layer):
            base = layer * B

            def normalise(n, u):
                ypair = gat_banks(u)
                d.wait_ge(s("gat_psum"), n + 1)
                for half in range(2):
                    y = ypair[half][0:NT, 0:H * AGG].rearrange("p (h f) -> p h f", h=H)
                    v.tensor_scalar(srec[:, half, :], y[:, :, F], 1e-30, None, ALU.max)
                d.drain().then_inc(agg_used[u], 1)
                v.reciprocal(flat(srec), flat(srec))
                d.drain()
                for half in range(2):
                    y = ypair[half][0:NT, 0:H * AGG].rearrange("p (h f) -> p h f", h=H)
                    v.tensor_tensor(yv[:, u, half, :].rearrange("p (h f) -> p h f", h=H), y[:, :, 0:F], bc(srec[:, half, :], 2, F), ALU.mult)
                d.drain()
                v.tensor_tensor(yv[:, u], yv[:, u], bc(gbias, 1, 2), ALU.add)
                d.drain().then_inc(s("gat_y"), 1)

            def heads_sum(u, src):
                for half in range(2):
                    v.tensor_reduce(hm[:, u, half, :], src[:, u, half, :].rearrange("p (h f) -> p f h", h=H), AX.X, ALU.add)
                d.drain()

            def mean(n, u, t0):
                d.wait_ge(s("gat_tanh"), n + 1)
                heads_sum(u, yt)
                v.tensor_scalar(flat(hm[:, u]), flat(hm[:, u]), 1.0 / H, None, ALU.mult)
                d.drain().then_inc(s("gat_h"), 1)
                v.tensor_copy(xt[:, bass.ds(t0, 2), 0:F], hm[:, u])

            def logits_parts(n, t0):
                d.wait_ge(s("gat_v"), n + 1)
                e = bank[5][0:NT, 0:4 * H].rearrange("p (t k) -> p t k", k=2 * H)
                v.tensor_copy(xt[:, bass.ds(t0, 2), F + 1:XC], e[:, :, 0:H])
                v.tensor_copy(er_sb[:, bass.ds(t0, 2), :], e[:, :, H:2 * H])
                d.drain().then_inc(s("gat_xt"), 1)

            for i in rounds(d, B // NG):
                for u in range(NG):
                    n = i * NG + u
                    normalise(n + base, u)
                    if layer == 1:
                        heads_sum(u, yv)
                        own = x_sb[:, bass.ds(n * 2, 2), :]
                        v.scalar_tensor_tensor(own, hm[:, u], 1.0 / H, own, ALU.mult, ALU.add)
                        d.drain()
                        continue
                    if not (first(i) and u < 1):
                        mean(n - 1, (u - 1) % NG, n * 2 - 2)
                    if not (first(i) and u < 2):
                        logits_parts(n - 2, n * 2 - 4)
            if layer == 0:
                mean(B - 1, NG - 1, 2 * B - 2)
                logits_parts(B - 2, 2 * B - 4)
                logits_parts(B - 1, 2 * B - 2)

        ln_count = [0]

        def layer_norm(d):
            ln_count[0] += 1
            v.tensor_reduce(colm[:, 0, :], x_sb, AX.X, ALU.add)
            d.drain()
            v.tensor_scalar(colm[:, 0, :], colm[:, 0, :], 1.0 / F, None, ALU.mult)
            d.drain()
            v.tensor_tensor(x_sb, x_sb, bc(colm[:, 0, :], 2, F), ALU.subtract)
            d.drain()
            v.tensor_tensor(sq, x_sb, x_sb, ALU.mult)
            d.drain()
            v.tensor_reduce(colm[:, 1, :], sq, AX.X, ALU.add)
            d.drain()
            v.tensor_scalar(colm[:, 1, :], colm[:, 1, :], 1.0 / F, LN_EPS, ALU.mult, ALU.add)
            d.drain().then_inc(s("ln_var"), 1)
            d.wait_ge(s("ln_std"), ln_count[0])
            v.reciprocal(colm[:, 3, :], colm[:, 2, :])
            d.drain()
            v.tensor_tensor(x_sb, x_sb, bc(colm[:, 3, :], 2, F), ALU.mult)
            d.drain()

        def per_node_vector(d):
            d.wait_ge(s("conv_w"), CONV_W)
            v.memset(we[0:ED, 0:1], 0.0)
            v.memset(we[ED:EF, :], 0.0)
            d.drain()
            v.tensor_copy(we[ED:EF, 0:1], ident[ED:EF, EF - 1:EF])
            v.tensor_tensor(we[ED:ED + 1, 1:QC], bsum[ED:ED + 1, 0, :], bsum[ED:ED + 1, 1, :], ALU.add)
            d.drain().then_inc(s("we_made"), 1)
            for b in rounds(d, B, False):
                d.wait_ge(s("pn_psum"), b + 1)
                v.tensor_copy(per_node[:, bass.ds(b * 2, 2), :], bank[0][0:NT, 0:2 * QC].rearrange("p (t q) -> p t q", q=QC)).then_inc(s("pn_evac"), 1)
            d.wait_ge(s("pn_evac"), B)
            v.tensor_scalar(colm[:, 3, :], per_node[:, :, 0], 1.0, None, ALU.add)
            d.drain()
            v.tensor_scalar(colm[:, 0, :], colm[:, 3, :], 0.0, None, ALU.is_gt)
            v.tensor_scalar(colm[:, 1, :], colm[:, 3, :], 1e-30, None, ALU.max)
            d.drain().then_inc(s("ln_var"), 1)
            ln_count[0] += 1
            d.wait_ge(s("ln_std"), ln_count[0])
            v.reciprocal(colm[:, 3, :], colm[:, 2, :])
            d.drain()
            v.tensor_tensor(dinv, colm[:, 3, :], colm[:, 0, :], ALU.mult)
            d.drain()

        def parts_vector(d, x_in):
            v.tensor_copy(x_hm[:, :, 0:F], x_in)
            d.drain()
            v.tensor_tensor(sq, x_in, x_hm[:, :, 0:F], ALU.subtract)
            d.drain()
            v.tensor_copy(x_hm[:, :, F:2 * F], sq)
            d.drain()
            v.tensor_tensor(x_l, sq, x_hm[:, :, F:2 * F], ALU.subtract)
            d.drain()

        def extra_vector(d, n):
            count = d.value_load(n_items, min_val=0, max_val=NW)
            with d.If(count > 0):
                with d.Fori(0, B) as b:
                    k = b + (n - 3) * B
                    d.wait_ge(s("ex_psum"), k + 1)
                    v.tensor_scalar(extra[:, bass.ds(b * BN, BN)], bank[6][:, 0:BN], float(KILO), None, ALU.mult).then_inc(s("ex_done"), 1)
                d.drain()

        def conv_vector(d, n, x_in, x_out):

            def post(b, par, k):
                t2 = bass.ds(b * 2, 2)
                if n >= 3:
                    d.wait_ge(cv_used[NQ - 1], k + 1)
                    d.wait_ge(s("cv_y"), k)
                    v.tensor_tensor(aggs, bank[par][:, 0:BN], extra[:, bass.ds(b * BN, BN)], ALU.add)
                    d.drain().then_inc(s("cv_aggc"), 1)
                d.wait_ge(s("cv_y"), k + 1)
                y = bank[2][0:NT, 0:2 * F].rearrange("p (t f) -> p t f", f=F)
                if n < 3:
                    dv = bc(dinv[:, t2], 2, F)
                    v.tensor_tensor(yc, y, dv, ALU.mult)
                    d.drain()
                    v.tensor_tensor(yc, yc, bc(bconv[:, n, :], 1, 2), ALU.add)
                    d.drain()
                    v.tensor_scalar(flat(yc), flat(yc), 0.0, None, ALU.max)
                    d.drain().then_inc(s("cv_ev"), 1)
                    if n < 2:
                        v.tensor_tensor(x_out[:, t2, :], yc, dv, ALU.mult)
                    d.wait_ge(s("cv_f"), k + 1)
                    f = bank[5][0:NT, 0:2 * F].rearrange("p (t f) -> p t f", f=F)
                    if n == 0:
                        v.tensor_copy(facc[:, t2, :], f)
                    else:
                        v.tensor_tensor(facc[:, t2, :], facc[:, t2, :], f, ALU.add)
                    d.drain()
                elif n == 3:
                    v.tensor_copy(x_out[:, t2, :], y)
                    d.drain().then_inc(s("cv_ev"), 1)
                else:
                    l = n - 4
                    v.tensor_tensor(yc, y, per_node[:, t2, 1 + l * F:1 + (l + 1) * F], ALU.add)
                    d.drain().then_inc(s("cv_ev"), 1)
                    v.tensor_tensor(yc, yc, bc(bconv[:, 4 + l, :], 1, 2), ALU.add)
                    d.drain()
                    v.tensor_scalar(flat(yc), flat(yc), 0.0, None, ALU.max)
                    d.drain()
                    v.tensor_tensor(x_out[:, t2, :], yc, bc(bconv[:, 6 + l, :], 1, 2), ALU.add)
                    d.drain()

            for b, par in pairs(d):
                k = b + n * B
                t2 = bass.ds(b * 2, 2)
                v.tensor_copy(xd[:, par, 0], x_in[:, t2, :])
                if n == 0:
                    v.tensor_copy(xd[:, par, 1], x_sb[:, t2, :])
                d.drain().then_inc(s("cv_self"), 1)
                if not first(b):
                    post(b - 1, 1 - par, k - 1)
            post(B - 1, 0, n * B + B - 1)

        def batch_norm(d, z, l):
            v.tensor_reduce(stat[:, 0, :], z.rearrange("p t f -> p f t"), AX.X, ALU.add)
            d.drain().then_inc(s("bn_sum"), 1)
            d.wait_ge(s("bn_mean"), 2 * l + 1)
            v.tensor_scalar(stat[:, 1, :], bank[6][0:NT, 0:F], 1.0 / N, None, ALU.mult)
            d.drain()
            v.tensor_tensor(z, z, bc(stat[:, 1, :], 1, T), ALU.subtract)
            d.drain()
            v.tensor_tensor(sq, z, z, ALU.mult)
            d.drain()
            v.tensor_reduce(stat[:, 0, :], sq.rearrange("p t f -> p f t"), AX.X, ALU.add)
            d.drain().then_inc(s("bn_sum"), 1)
            d.wait_ge(s("bn_mean"), 2 * l + 2)
            v.tensor_scalar(stat[:, 2, :], bank[6][0:NT, 0:F], 1.0 / N, BN_EPS, ALU.mult, ALU.add)
            d.drain().then_inc(s("bn_var"), 1)
            d.wait_ge(s("bn_std"), l + 1)
            v.reciprocal(stat[:, 4, :], stat[:, 3, :])
            d.drain()
            v.tensor_tensor(stat[:, 4, :], stat[:, 4, :], bconv[:, 8 + 2 * l, :], ALU.mult)
            d.drain()
            v.tensor_tensor(z, z, bc(stat[:, 4, :], 1, T), ALU.mult)
            d.drain()
            v.tensor_tensor(z, z, bc(bconv[:, 9 + 2 * l, :], 1, T), ALU.add)
            d.drain()

        @block.vector
        def _(d):
            prep_vector(d)
            ptr_vector(d)
            logit_weights_vector(d)
            table0_vector(d)
            d.wait_ge(s("items_back"), 16)
            win_vector(d, 0)
            win_overflow_vector(d, 0)
            gat_vector(d, 0)
            d.drain().then_inc(s("table_made"), 1)
            d.sem_inc(s("gat_done"), 1)
            win_vector(d, 1)
            adj_overflow_vector(d)
            win_overflow_vector(d, 1)
            gat_vector(d, 1)
            d.drain().then_inc(s("gat_done"), 1)
            layer_norm(d)
            per_node_vector(d)
            v.tensor_tensor(xin, x_sb, bc(dinv, 2, F), ALU.mult)
            d.drain().then_inc(s("cv_done"), 1)
            conv_vector(d, 0, xin, hout)
            d.drain().then_inc(s("cv_done"), 1)
            conv_vector(d, 1, hout, xin)
            d.drain().then_inc(s("cv_done"), 1)
            conv_vector(d, 2, xin, None)
            v.tensor_tensor(x_sb, x_sb, facc, ALU.add)
            d.drain()
            v.tensor_tensor(x_sb, x_sb, bc(bconv[:, 3, :], 1, T), ALU.add)
            d.drain()
            layer_norm(d)
            v.memset(extra, 0.0)
            v.tensor_copy(wcc[0:F, 0, :], ident[0:F, 0:F])
            v.tensor_copy(wcc[F:2 * F, 0, :], ident[F:2 * F, F:2 * F])
            parts_vector(d, x_sb)
            d.drain().then_inc(s("cv_done"), 1)
            extra_vector(d, 3)
            conv_vector(d, 3, x_sb, hout)
            v.tensor_copy(x_sb, hout)
            d.drain()
            layer_norm(d)
            parts_vector(d, x_sb)
            d.drain().then_inc(s("cv_done"), 1)
            extra_vector(d, 4)
            conv_vector(d, 4, x_sb, hout)
            batch_norm(d, hout, 0)
            parts_vector(d, hout)
            d.drain().then_inc(s("cv_done"), 1)
            extra_vector(d, 5)
            conv_vector(d, 5, hout, xin)
            batch_norm(d, xin, 1)
            v.tensor_tensor(x_sb, x_sb, xin, ALU.add)
            d.drain()
            layer_norm(d)
            d.drain().then_inc(s("cv_done"), 1)

        mm = nc.tensor.matmul

        def prep_tensor(pe):
            pe.wait_ge(s("xT_loaded"), 16)
            pe.wait_ge(s("v_made"), 1)
            for t in range(T):
                last = mm(bank[7][0:NT, t * 2 * H:(t + 1) * 2 * H], lhsT=xT_sb[:, t * NT:(t + 1) * NT], rhs=vw[:, 0, :], start=True, stop=True)
            last.then_inc(s("el_psum"), 1)

        def adj_window_mms(slot, ef_slot, w, wb, cb, seg, oh, seg_done=None):
            for c in range(CH):
                last = mm(seg, lhsT=ef_sl[:, ef_slot, w, c * EF:(c + 1) * EF], rhs=oh[:, c, :], start=(c == 0), stop=(c == CH - 1))
            if seg_done is not None:
                last.then_inc(seg_done, 1)
            for c in range(CH):
                for i in range(3):
                    mm(wb, lhsT=row_oh[:, slot, c, i, :], rhs=col_oh[:, slot, c, :], start=(c == 0 and i == 0), stop=(c == CH - 1 and i == 2))
            for c in range(CH):
                last = mm(cb, lhsT=row_oh[:, slot, c, 3, :], rhs=col_oh[:, slot, c, :], start=(c == 0), stop=(c == CH - 1))
            return last

        def top_mms(nw):
            for i in range(-(-nw // TW)):
                k = min(TW, nw - i * TW) * WH
                last = mm(bank[5][0:k, i * P:(i + 1) * P], lhsT=top_e[:, i * TW * WH:i * TW * WH + k], rhs=ident, start=True, stop=True)
            return last

        def diag_mms(nw):
            for i in range(-(-nw // TW)):
                k = min(TW, nw - i * TW) * WH
                last = mm(bank[5][:, 2 * P + i * TW * WH:2 * P + i * TW * WH + k], lhsT=ones[0:k, :], rhs=diag[0:k, i, 0:k], start=True, stop=True)
            return last

        def agg_mms(out, g, w, par):
            for c in range(CH):
                last = mm(out, lhsT=rows_sl[:, g, w, c, 0:AGG], rhs=grh[:, par, w * CH + c, :], start=(c == 0), stop=(c == CH - 1))
            return last

        def win_tensor(pe, layer):
            ng = NG * B * layer

            def aggregate(n, g):
                pe.wait_ge(s("exp_made"), n + 1)
                pe.wait_ge(s("win_evac"), n)
                for w in range(WG):
                    last = agg_mms(bank[6][0:AGG, w * WH:(w + 1) * WH], g, w, g % GS)
                last.then_inc(s("win_psum"), 1)

            for b in rounds(pe, B):
                for g in range(NG):
                    n1 = b * NG + (ng + g + 1)

                    def adjacency(w):
                        if g not in ADJ[layer]:
                            return
                        i = built_before(layer, g)
                        n = i * WG + w
                        if w == 0:
                            pe.wait_ge(adj_loaded[g], b * (16 * WG) + 16 * WG)
                            pe.wait_ge(s("seg_evacuated"), groups_before(layer, b, max(0, i - 1)))
                        pe.wait_ge(s("adj_evacuated"), windows_before(layer, b, max(0, n - 1)))
                        pe.wait_ge(s("onehot_made"), windows_before(layer, b, n + 1))
                        pe.wait_ge(s("rows_weighted"), windows_before(layer, b, n + 1))
                        pair = 2 * (n % 2)
                        seg_bank = bank[4 if i % 2 == 0 else 7]
                        adj_window_mms(n % OHS, i, w, bank[pair][:, 0:T * WN], bank[pair + 1][:, 0:T * WN],
                                       seg_bank[0:EF, w * WN:(w + 1) * WN], coh[:, g % GS, w * CH:(w + 1) * CH, :],
                                       adj_used[g] if w == WG - 1 else None).then_inc(s("adj_psum"), 1)

                    if not (isinstance(b, int) and g == 0):
                        aggregate(n1 - 2, (g - 1) % NG)
                    adjacency(0)
                    pe.wait_ge(s("top_made"), n1)
                    top_mms(WG).then_inc(s("top_t"), 1)
                    adjacency(1)
                    adjacency(2)
                    pe.wait_ge(s("diag_made"), n1)
                    diag_mms(WG).then_inc(s("top_psum"), 1)
                    adjacency(3)
                    adjacency(4)
            aggregate(ng + NGR - 1, NG - 1)

        def adj_overflow_tensor(pe):
            pe.wait_ge(s("adj_evacuated"), NW)
            pe.wait_ge(s("seg_evacuated"), NGR)
            count = pe.value_load(n_items, min_val=0, max_val=NW)
            with pe.If(count > 0):
                with pe.Fori(0, count) as k:
                    pe.wait_ge(s("ov_loaded"), k * 80 + 80)
                    pe.wait_ge(s("ov_weighted"), k + 1)
                    adj_window_mms(0, 0, 0, bank[0][:, 0:T * WN], bank[1][:, 0:T * WN], bank[4][0:EF, 0:WN], coh[:, 0, 0:CH, :]).then_inc(s("ov_psum"), 1)

        def win_overflow_tensor(pe, layer):
            pe.wait_ge(s("win_evac"), NGR * (layer + 1))
            count = pe.value_load(n_items, min_val=0, max_val=NW)
            with pe.If(count > 0):
                with pe.Fori(0, count) as k:
                    kk = ga_base(pe, layer) + k
                    pe.wait_ge(s("ga_top"), kk + 1)
                    top_mms(1).then_inc(s("ga_topt"), 1)
                    pe.wait_ge(s("ga_diag"), kk + 1)
                    diag_mms(1).then_inc(s("ga_topp"), 1)
                    pe.wait_ge(s("ga_exp"), kk + 1)
                    agg_mms(bank[6][0:AGG, 0:WH], 0, 0, 0).then_inc(s("ga_psum"), 1)

        def gat_tensor(pe, layer):
            pe.wait_ge(s("wgat_loaded"), 32 * (layer + 1))
            base = layer * B

            def transposes(n, u):
                pe.wait_ge(s("gat_h"), n + 1)
                wait_some(pe, s("gat_hTc"), n)
                for half in range(2):
                    last = mm(bank[4][0:F, half * NT:(half + 1) * NT], lhsT=hm[:, u, half, :], rhs=ident[0:NT, 0:NT], start=True, stop=True)
                last.then_inc(s("gat_hT"), 1)

            def logits_parts(n):
                pe.wait_ge(s("gat_hTc"), n + 1)
                wait_some(pe, s("gat_xt"), n)
                for half in range(2):
                    last = mm(bank[5][0:NT, half * 2 * H:(half + 1) * 2 * H], lhsT=hT[:, half * NT:(half + 1) * NT], rhs=vw[:, 1, :], start=True, stop=True)
                last.then_inc(s("gat_v"), 1)

            for i in rounds(pe, B // NG):
                for u in range(NG):
                    n = i * NG + u
                    pe.wait_ge(agg_loaded[u], i * 16 + 16 * (layer * (B // NG) + 1))
                    wait_some(pe, s("gat_y"), n + (base - 1))
                    for half in range(2):
                        for h in range(H):
                            last = mm(gat_banks(u)[half][0:NT, h * AGG:(h + 1) * AGG], lhsT=agg_sl[:, u, h, half * NT:(half + 1) * NT], rhs=wgat[:, h, :], start=True, stop=True)
                    last.then_inc(s("gat_psum"), 1)
                    if layer == 1:
                        continue
                    if not (first(i) and u < 2):
                        logits_parts(n - 2)
                    if not (first(i) and u < 1):
                        transposes(n - 1, (u - 1) % NG)
            if layer == 0:
                logits_parts(B - 2)
                transposes(B - 1, NG - 1)
                logits_parts(B - 1)

        def per_node_tensor(pe):
            pe.wait_ge(s("we_made"), 1)
            for b in rounds(pe, B):
                pe.wait_ge(s("pn_copied"), b + 1)
                pe.wait_ge(s("pn_evac"), b)
                for half in range(2):
                    last = mm(bank[0][0:NT, half * QC:(half + 1) * QC], lhsT=segb[:, half * NT:(half + 1) * NT], rhs=we, start=True, stop=True)
                last.then_inc(s("pn_psum"), 1)

        def count_mms(out, q, t, self_mms=None):
            rhs = adj16_sl[0:NT, q, :, t * GN:(t + 1) * GN]
            start, stop = q == 0 and t == 0, q == NQ - 1 and t == QT - 1
            hm = lambda: mm(out.rearrange("p (g n) -> p g n", n=GN), lhsT=x_hm[:, q * QT + t, :], rhs=rhs, start=start, stop=stop)
            if start:
                hm()
            last = mm(out[0:F].rearrange("p (g n) -> p g n", n=GN), lhsT=x_l[:, q * QT + t, :], rhs=rhs, start=False, stop=False)
            if stop and self_mms:
                self_mms()
            return last if start else hm()

        def extra_tensor(pe, n):
            count = pe.value_load(n_items, min_val=0, max_val=NW)
            with pe.If(count > 0):
                pe.wait_ge(s("cv_done"), n + 1)
                with pe.Fori(0, B) as b:
                    k = b + (n - 3) * B
                    pe.wait_ge(s("ex_loaded"), k * (16 * NQ) + 16 * NQ)
                    pe.wait_ge(s("ex_done"), k)
                    for q in range(NQ):
                        for t in range(QT):
                            last = count_mms(bank[6][:, 0:BN], q, t)
                    last.then_inc(s("ex_psum"), 1)
                pe.wait_ge(s("ex_done"), (n - 2) * B)

        def conv_tensor(pe, n, x_in):
            pe.wait_ge(s("cv_done"), n + 1)
            two = n == 0
            rows = F if n < 3 else 2 * F

            def product(k):
                pe.wait_ge(s("cv_aggc"), k + 1)
                pe.wait_ge(s("cv_ev"), k)
                for half in range(2):
                    last = mm(bank[2][0:NT, half * F:(half + 1) * F], lhsT=aggs[0:rows, half * NT:(half + 1) * NT],
                              rhs=wconv[:, n, :] if n < 3 else wcc[:, n - 3, :], start=True, stop=True)
                last.then_inc(s("cv_y"), 1)

            def transposes(par, k):
                pe.wait_ge(s("cv_ev"), k + 1)
                for i in range(2 if two else 1):
                    for half in range(2):
                        last = mm(bank[3 + i][0:F, half * NT:(half + 1) * NT], lhsT=xd[:, par, 1, half, :] if i else yc[:, half, :], rhs=ident[0:NT, 0:NT], start=True, stop=True)
                last.then_inc(s("cv_yT"), 1)

            def final(k):
                pe.wait_ge(s("cv_yTc"), k + 1)
                for half in range(2):
                    for i in range(2 if two else 1):
                        last = mm(bank[5][0:NT, half * F:(half + 1) * F], lhsT=yT[:, i, half * NT:(half + 1) * NT], rhs=wf[:, 0 if i else n + 1, :],
                                  start=(i == 0), stop=(not two or i == 1))
                last.then_inc(s("cv_f"), 1)

            for b, par in pairs(pe):
                k = b + n * B

                def own_rows():
                    pe.wait_ge(s("cv_self"), k + 1)
                    for half in range(2):
                        last = mm(bank[par][0:F, half * NT:(half + 1) * NT], lhsT=xd[:, par, 0, half, :], rhs=ident[0:NT, 0:NT], start=False, stop=(n < 3 and half == 1))
                    return last

                for q in range(NQ):
                    pe.wait_ge(cv_loaded[q], b * 16 + 16 * (n * B + 1))
                    for t in range(QT):
                        start = q == 0 and t == 0
                        if n < 3:
                            last = mm(bank[par][0:F, 0:BN].rearrange("p (g n) -> p g n", n=GN), lhsT=x_in[:, q * QT + t, :],
                                      rhs=adj_sl[0:NT, q, :, t * GN:(t + 1) * GN], start=start, stop=False)
                        else:
                            last = count_mms(bank[par][:, 0:BN], q, t, own_rows)
                    last.then_inc(cv_used[q], 1)
                    if not first(b):
                        if q == 1:
                            product(k - 1)
                        if n < 3 and q == 2:
                            transposes(1 - par, k - 1)
                        if n < 3 and q == 3:
                            final(k - 1)
                if n < 3:
                    own_rows().then_inc(s("cv_agg"), 1)
            k = n * B + B - 1
            product(k)
            if n < 3:
                transposes(0, k)
                final(k)

        def batch_norm_tensor(pe, l):
            for i in range(2):
                pe.wait_ge(s("bn_sum"), 2 * l + i + 1)
                mm(bank[6][0:NT, 0:F], lhsT=ones[0:NT, 0:NT], rhs=stat[:, 0, :], start=True, stop=True).then_inc(s("bn_mean"), 1)

        @block.tensor
        def _(pe):
            prep_tensor(pe)
            pe.wait_ge(s("table_made"), 1)
            for layer in range(2):
                win_tensor(pe, layer)
                if layer == 1:
                    adj_overflow_tensor(pe)
                win_overflow_tensor(pe, layer)
                gat_tensor(pe, layer)
            per_node_tensor(pe)
            for n, x_in in enumerate((xin, hout, xin, x_sb, x_sb, hout)):
                if n >= 3:
                    extra_tensor(pe, n)
                conv_tensor(pe, n, x_in)
                if n >= 4:
                    batch_norm_tensor(pe, n - 4)

        act_ = nc.scalar.activation

        def weigh_rows(slot, rec):
            for c in range(CH):
                for i in (1, 2):
                    last = act_(row_oh[:, slot, c, i, :], row_oh[:, slot, c, 3, :], ACT.Copy, scale=rec[:, c * REC + 2 + i:c * REC + 3 + i])
            return last

        def win_scalar(act, layer):
            ng = NG * B * layer

            def evacuate(b, g, w):
                if g not in ADJ[layer]:
                    return
                slot = built_before(layer, g)
                n = slot * WG + w
                act.wait_ge(s("adj_psum"), windows_before(layer, b, n + 1))
                for i, st in enumerate((stage_w, stage_c)):
                    last = act_(st[:, slot, :, w * WN:(w + 1) * WN], bank[2 * (n % 2) + i][:, 0:T * WN].rearrange("p (t n) -> p t n", n=WN), ACT.Copy)
                last.then_inc(s("adj_evacuated"), 1)

            def finish(b, g):
                group = b * NG + g
                n1 = group + (ng + 1)
                if g in ADJ[layer]:
                    slot = built_before(layer, g)
                    evacuate(b, g, WG - 1)
                    act_(seg_t[:, bass.ds(group * GN, GN)], bank[4 if slot % 2 == 0 else 7][0:EF, 0:GN], ACT.Copy).then_inc(s("seg_evacuated"), 1)
                    act.wait_ge(s("adj_evacuated"), windows_before(layer, b, (slot + 1) * WG))
                    for d, st in ((adj_w_d, stage_w), (adj_c_d, stage_c)):
                        act.dma_start(d[bass.ds(group, 1), :, :, :].rearrange("a p t n -> p (a t n)"), flat(st[:, slot])).then_inc(adj_stored[slot], 16)
                act.wait_ge(win_stored[g], b * 16 + 16 * B * layer)
                act.wait_ge(s("win_psum"), n1)
                act_(gst[:, g].rearrange("p h (w j) -> p w h j", j=WN), bank[6][0:AGG, 0:WG * WH].rearrange("p (w h j) -> p w h j", w=WG, h=H), ACT.Copy).then_inc(s("win_evac"), 1)
                act.wait_ge(s("win_evac"), n1)
                act.sem_inc(win_used[g], 1)
                act.dma_start(agg_d[:, :, bass.ds(group * GN, GN)], gst[:, g]).then_inc(win_stored[g], 16)

            for b in rounds(act, B):
                for g in range(NG):
                    n1 = b * NG + (ng + g + 1)

                    def weigh(w, g=g):
                        if g not in ADJ[layer]:
                            return
                        n = built_before(layer, g) * WG + w
                        act.wait_ge(s("onehot_made"), windows_before(layer, b, n + 1))
                        weigh_rows(n % OHS, rec_sl[:, g, w, :]).then_inc(s("rows_weighted"), 1)

                    if not ahead(layer, g):
                        weigh(0)
                    if not (isinstance(b, int) and g == 0):
                        finish(b if g else b - 1, (g - 1) % NG)
                    if g in ADJ[layer]:
                        slot = built_before(layer, g)
                        act.wait_ge(adj_stored[slot], stage_stores(layer, b, slot))
                    weigh(1)
                    weigh(2)
                    evacuate(b, g, 0)
                    weigh(3)
                    evacuate(b, g, 1)
                    weigh(4)
                    evacuate(b, g, 2)
                    if ahead(layer, g + 1):
                        weigh(0, g + 1)
                    act.wait_ge(s("logits_made"), n1)
                    wait_some(act, s("win_psum"), b * NG + (ng + former_group(g) + 1))
                    act_(flat(grh[:, g % GS]), flat(gd[:, g % GS]), ACT.Exp).then_inc(s("exp_made"), 1)
                    act.dma_start(max_d[:, bass.ds((b * NG + g) * (WG * WH), WG * WH)], top_row[:, g % 2, :]).then_inc(top_stored[g % 2], 16)
                    evacuate(b, g, 3)
            finish(B - 1, NG - 1)

        def adj_overflow_scalar(act):
            count = act.value_load(n_items, min_val=0, max_val=NW)
            with act.If(count > 0):
                with act.Fori(0, count) as k:
                    act.wait_ge(s("ov_onehot"), k + 1)
                    weigh_rows(0, rec_sl[:, 0, 0, :]).then_inc(s("ov_weighted"), 1)

        def win_overflow_scalar(act, layer):
            count = act.value_load(n_items, min_val=0, max_val=NW)
            with act.If(count > 0):
                with act.Fori(0, count) as k:
                    kk = ga_base(act, layer) + k
                    act.wait_ge(s("ga_logits"), kk + 1)
                    act_(top_o[:, 2, :], top_o[:, 2, :], ACT.Exp)
                    act_(grh[:, 0, 0:CH, :], gd[:, 0, 0:CH, :], ACT.Exp).then_inc(s("ga_exp"), 1)

        def gat_scalar(act):

            def transposed(n):
                act.wait_ge(s("gat_hT"), n + 1)
                act_(hT, bank[4][0:F, 0:BN], ACT.Copy).then_inc(s("gat_hTc"), 1)

            for i in rounds(act, B // NG):
                for u in range(NG):
                    n = i * NG + u
                    act.wait_ge(s("gat_y"), n + 1)
                    act_(flat(yt[:, u]), flat(yv[:, u]), ACT.Tanh).then_inc(s("gat_tanh"), 1)
                    if not (first(i) and u < 1):
                        transposed(n - 1)
            transposed(B - 1)

        std_count = [0]

        def std_scalar(act):
            std_count[0] += 1
            act.wait_ge(s("ln_var"), std_count[0])
            act_(colm[:, 2, :], colm[:, 1, :], ACT.Sqrt).then_inc(s("ln_std"), 1)

        def per_node_scalar(act):
            act.wait_ge(s("we_made"), 1)
            for b in rounds(act, B):
                act.wait_ge(s("pn_psum"), b)
                act_(segb, seg_t[:, bass.ds(b * BN, BN)], ACT.Copy).then_inc(s("pn_copied"), 1)

        def conv_scalar(act, n):
            for b, par in pairs(act):
                k = b + n * B
                act.wait_ge(s("cv_agg"), k + 1)
                act.wait_ge(s("cv_y"), k)
                act_(aggs[0:F], bank[par][0:F, 0:BN], ACT.Copy).then_inc(s("cv_aggc"), 1)
                act.wait_ge(s("cv_yT"), k + 1)
                act.wait_ge(s("cv_f"), k)
                for i in range(2 if n == 0 else 1):
                    last = act_(yT[:, i, :], bank[3 + i][0:F, 0:BN], ACT.Copy)
                last.then_inc(s("cv_yTc"), 1)

        @block.scalar
        def _(act):
            act.wait_ge(s("items_back"), 16)
            act.wait_ge(s("el_psum"), 1)
            for layer in range(2):
                act.wait_ge(s("table_made"), layer + 1)
                win_scalar(act, layer)
                if layer == 1:
                    adj_overflow_scalar(act)
                win_overflow_scalar(act, layer)
                if layer == 0:
                    gat_scalar(act)
            std_scalar(act)
            per_node_scalar(act)
            std_scalar(act)
            for n in range(6):
                if n < 3:
                    conv_scalar(act, n)
                if n in (2, 3):
                    std_scalar(act)
                if n >= 4:
                    act.wait_ge(s("bn_var"), n - 3)
                    act_(stat[:, 3, :], stat[:, 2, :], ACT.Sqrt).then_inc(s("bn_std"), 1)
            std_scalar(act)


_OUT = ((N, F), "float32")


def kernel(**inputs):
    import concourse.bacc as bacc
    from concourse.bass_utils import run_bass_kernel_spmd as run

    nc = bacc.Bacc("TRN2", target_bir_lowering=False, num_devices=1)
    g = {k: np.ascontiguousarray(v) for k, v in inputs.items()}
    pad = EP - E
    src = np.concatenate([g.pop("src"), np.zeros(pad, np.int32)])
    dst = np.concatenate([g.pop("dst"), np.full(pad, N + 22, np.int32)])
    ew = g.pop("edge_weight")
    ea = g.pop("edge_attr_32")
    feats = np.zeros((EP, EF), np.float32)
    feats[:E, 0:ED] = ea
    feats[:E, ED] = 1.0
    feats[:E, ED + 1] = ew
    g["src"] = src.reshape(P, EC)
    g["dst"] = dst.reshape(EC, P)
    g["dst_heads"] = np.ascontiguousarray(dst.reshape(EC, P)[:, 0]).reshape(1, EC)
    g["edge_weight"] = np.concatenate([ew, np.zeros(pad, np.float32)]).reshape(P, EC)
    g["edge_features"] = feats
    g["xT"] = np.ascontiguousarray(g["x"].T)
    arrays, aps = {}, {}
    for k, v in g.items():
        arrays[f"in_{k}"] = v
        aps[k] = nc.dram_tensor(f"in_{k}", v.shape, mybir.dt.from_np(v.dtype), kind="ExternalInput").ap()
    aps["out"] = nc.dram_tensor("out_0", _OUT[0], F32, kind="ExternalOutput").ap()
    build(nc, aps)
    r = run(nc, [arrays], core_ids=[0])
    return r.results[0]["out_0"]
```
